# Optimizing a Trainium2 kernel written in Bass

```python
import numpy as np
import jax
import jax.numpy as jnp

def _softmax(x, axis=-1):
    return jax.nn.softmax(x, axis=axis)

def _gelu(x):
    return jax.nn.gelu(x, approximate=True)

def _silu(x):
    return jax.nn.silu(x)

def _sigmoid(x):
    return jax.nn.sigmoid(x)

def _layernorm(x, axis=-1, eps=1e-05):
    m = jnp.mean(x, axis=axis, keepdims=True)
    v = jnp.var(x, axis=axis, keepdims=True)
    return (x - m) / jnp.sqrt(v + eps)

def _scatter_add(tgt, idx, src, axis=0):
    return tgt.at[idx].add(src)

def _segment_sum(src, seg, n):
    return jax.ops.segment_sum(src, seg, n)
kernel_name = 'mk_gnn_preln_d4_gnn_r16_eaebb5'

def setup_inputs(seed: int=0):
    np.random.seed(seed)
    _w = jnp.asarray

    def _rec_inputs():
        import jax
        import jax.numpy as jnp
        _gk = jax.random.key(seed)
        x = -0.000202 + 1 * jax.random.normal(jax.random.fold_in(_gk, 1), (3125, 128), jnp.float32)
        _s = jax.random.randint(jax.random.fold_in(_gk, 2), (25000,), 0, 3125, jnp.int32)
        _d = jax.random.randint(jax.random.fold_in(_gk, 3), (25000,), 0, 3125, jnp.int32)
        _loop = jnp.arange(3125, dtype=jnp.int32)
        src = jnp.concatenate([_s, _d, _loop])
        dst = jnp.concatenate([_d, _s, _loop])
        _o = jnp.argsort(dst, stable=True)
        src = src[_o]
        dst = dst[_o]
        return (x, src, dst)
    x, src, dst = _rec_inputs()

    def _L0_gnn_setup():
        import jax, jax.numpy as jnp
        import numpy as np
        N_NODES = 3125
        N_EDGES = 40000
        D = 128
        BN_EPS = 1e-05
        key = jax.random.key(seed)
        k1, k2, k3 = jax.random.split(key, 3)
        x = jax.random.normal(k1, (N_NODES, D), dtype=jnp.float32)
        W = jax.random.normal(k2, (D, D), dtype=jnp.float32) * (1.0 / np.sqrt(D))
        b = jnp.zeros((D,), dtype=jnp.float32)
        gamma = jnp.ones((D,), dtype=jnp.float32)
        beta = jnp.zeros((D,), dtype=jnp.float32)
        edge_index = jax.random.randint(k3, (2, N_EDGES), 0, N_NODES, dtype=jnp.int64)
        return {'x': x, 'W': W, 'b': b, 'gamma': gamma, 'beta': beta, 'edge_index': edge_index}
    _L0_gnn_all = _L0_gnn_setup()
    _L0_gnn_in = {k: v for k, v in _L0_gnn_all.items() if k in ('W', 'b', 'gamma', 'beta')}
    del _L0_gnn_all

    def _L1_gnn_setup():
        import jax, jax.numpy as jnp
        import numpy as np
        N = 3125
        IN_DIM = 128
        OUT_DIM = 128
        HEADS = 2
        EPS = 1e-05
        NEG_SLOPE = 0.2

        def _add_self_loops(edge_index, num_nodes):
            loop = jnp.arange(num_nodes, dtype=edge_index.dtype)
            src = jnp.concatenate([edge_index[0], loop])
            dst = jnp.concatenate([edge_index[1], loop])
            return (src, dst)

        def _layernorm(h, gamma, beta):
            mu = jnp.mean(h, axis=-1, keepdims=True)
            var = jnp.mean(jnp.square(h - mu), axis=-1, keepdims=True)
            return (h - mu) * jax.lax.rsqrt(var + EPS) * gamma + beta

        def _silu(h):
            return h * jax.nn.sigmoid(h)

        def _gcn_conv(x, src, dst, W, b, num_nodes):
            h = x @ W
            deg = jnp.zeros((num_nodes,), h.dtype).at[dst].add(1.0)
            dinv = jnp.where(deg > 0, jax.lax.rsqrt(jnp.maximum(deg, 1.0)), 0.0)
            norm = dinv[src] * dinv[dst]
            msg = h[src] * norm[:, None]
            out = jnp.zeros((num_nodes, h.shape[1]), h.dtype).at[dst].add(msg)
            return out + b

        def _gat_conv(x, src, dst, W, att_src, att_dst, b, num_nodes, heads):
            C = W.shape[1] // heads
            h = (x @ W).reshape(num_nodes, heads, C)
            a_src = jnp.sum(h * att_src, axis=-1)
            a_dst = jnp.sum(h * att_dst, axis=-1)
            e = a_src[src] + a_dst[dst]
            e = jnp.where(e > 0, e, NEG_SLOPE * e)
            m = jax.ops.segment_max(e, dst, num_segments=num_nodes)
            ex = jnp.exp(e - m[dst])
            den = jax.ops.segment_sum(ex, dst, num_segments=num_nodes)
            alpha = ex / den[dst]
            msg = h[src] * alpha[:, :, None]
            out = jnp.zeros((num_nodes, heads, C), h.dtype).at[dst].add(msg)
            return jnp.mean(out, axis=1) + b
        key = jax.random.key(seed)
        ks = jax.random.split(key, 9)
        x = jax.random.normal(ks[0], (N, IN_DIM), dtype=jnp.float32)
        edge_index = jax.random.randint(ks[1], (2, 50000), 0, N, dtype=jnp.int64)
        s = 1.0 / np.sqrt(IN_DIM)
        gcn_w = jax.random.uniform(ks[2], (IN_DIM, OUT_DIM), jnp.float32, -s, s)
        gcn_b = jnp.zeros((OUT_DIM,), jnp.float32)
        so = 1.0 / np.sqrt(OUT_DIM)
        gat_w = jax.random.uniform(ks[3], (OUT_DIM, HEADS * OUT_DIM), jnp.float32, -so, so)
        att_src = jax.random.uniform(ks[4], (HEADS, OUT_DIM), jnp.float32, -so, so)
        att_dst = jax.random.uniform(ks[5], (HEADS, OUT_DIM), jnp.float32, -so, so)
        gat_b = jnp.zeros((OUT_DIM,), jnp.float32)
        ln_gamma = jnp.ones((OUT_DIM,), jnp.float32)
        ln_beta = jnp.zeros((OUT_DIM,), jnp.float32)
        return dict(x=x, edge_index=edge_index, gcn_w=gcn_w, gcn_b=gcn_b, gat_w=gat_w, att_src=att_src, att_dst=att_dst, gat_b=gat_b, ln_gamma=ln_gamma, ln_beta=ln_beta)
    _L1_gnn_all = _L1_gnn_setup()
    _L1_gnn_in = {k: v for k, v in _L1_gnn_all.items() if k in ('gcn_w', 'gcn_b', 'gat_w', 'att_src', 'att_dst', 'gat_b', 'ln_gamma', 'ln_beta')}
    del _L1_gnn_all

    def _L2_gnn_setup():
        import jax, jax.numpy as jnp
        import numpy as np
        N = 6250
        E = 100000
        ANN = 128
        HID = 128
        S = ANN + HID
        L = 5
        MLP_H = 256
        OUT = 128

        def _forward(x, edge_index, W, w_ih, w_hh, b_ih, b_hh, l0_w, l0_b, l1_w, l1_b):
            n = x.shape[0]
            s = W.shape[-1]
            src, dst = (edge_index[0], edge_index[1])
            h = jnp.pad(x, ((0, 0), (0, s - x.shape[-1])))

            def step(h, Wl):
                m = h @ Wl
                agg = jax.ops.segment_sum(m[src], dst, num_segments=n)
                gi = agg @ w_ih.T + b_ih
                gh = h @ w_hh.T + b_hh
                ir, iz, in_ = jnp.split(gi, 3, axis=-1)
                hr, hz, hn = jnp.split(gh, 3, axis=-1)
                r = jax.nn.sigmoid(ir + hr)
                z = jax.nn.sigmoid(iz + hz)
                ng = jnp.tanh(in_ + r * hn)
                h_new = (1.0 - z) * ng + z * h
                return (h_new, None)
            h, _ = jax.lax.scan(step, h, W)
            cat = jnp.concatenate([h, x], axis=-1)
            y = jax.nn.relu(cat @ l0_w.T + l0_b)
            y = jax.nn.relu(y @ l1_w.T + l1_b)
            return y
        key = jax.random.key(seed)
        ks = jax.random.split(key, 12)
        sc = 0.05
        return {'x': jax.random.normal(ks[0], (N, ANN), dtype=jnp.float32), 'edge_index': jax.random.randint(ks[1], (2, E), 0, N, dtype=jnp.int64), 'W': jax.random.normal(ks[2], (L, S, S), dtype=jnp.float32) * sc, 'w_ih': jax.random.normal(ks[3], (3 * S, S), dtype=jnp.float32) * sc, 'w_hh': jax.random.normal(ks[4], (3 * S, S), dtype=jnp.float32) * sc, 'b_ih': jax.random.normal(ks[5], (3 * S,), dtype=jnp.float32) * sc, 'b_hh': jax.random.normal(ks[6], (3 * S,), dtype=jnp.float32) * sc, 'l0_w': jax.random.normal(ks[7], (MLP_H, S + ANN), dtype=jnp.float32) * sc, 'l0_b': jax.random.normal(ks[8], (MLP_H,), dtype=jnp.float32) * sc, 'l1_w': jax.random.normal(ks[9], (OUT, MLP_H), dtype=jnp.float32) * sc, 'l1_b': jax.random.normal(ks[10], (OUT,), dtype=jnp.float32) * sc}
    _L2_gnn_all = _L2_gnn_setup()
    _L2_gnn_in = {k: v for k, v in _L2_gnn_all.items() if k in ('W', 'w_ih', 'w_hh', 'b_ih', 'b_hh', 'l0_w', 'l0_b', 'l1_w', 'l1_b')}
    del _L2_gnn_all

    def _L3_gnn_setup():
        import jax, jax.numpy as jnp
        import numpy as np
        N = 3125
        E = 100000
        IN_CH = 128
        OUT_CH = 128
        NEG_SLOPE = 0.2

        def _gat_conv(x, W, att_src, att_dst, bias, src, dst, heads, out_ch, concat):
            n = x.shape[0]
            h = (x @ W).reshape(n, heads, out_ch)
            a_src = jnp.einsum('nhc,hc->nh', h, att_src)
            a_dst = jnp.einsum('nhc,hc->nh', h, att_dst)
            logits = jax.nn.leaky_relu(a_src[src] + a_dst[dst], NEG_SLOPE)
            m = jax.ops.segment_max(logits, dst, num_segments=n)
            e = jnp.exp(logits - m[dst])
            denom = jax.ops.segment_sum(e, dst, num_segments=n)
            alpha = e / denom[dst]
            msgs = h[src] * alpha[:, :, None]
            out = jax.ops.segment_sum(msgs, dst, num_segments=n)
            out = out.reshape(n, heads * out_ch) if concat else out.mean(axis=1)
            return out + bias
        key = jax.random.key(seed)
        ks = jax.random.split(key, 12)
        x = jax.random.normal(ks[0], (N, IN_CH), dtype=jnp.float32)
        edge_index = jax.random.randint(ks[1], (2, E), 0, N, dtype=jnp.int32)
        s = 0.1
        W_map = jax.random.normal(ks[2], (IN_CH, OUT_CH), dtype=jnp.float32) * s
        b_map = jnp.zeros((OUT_CH,), dtype=jnp.float32)
        W1 = jax.random.normal(ks[3], (OUT_CH, 64), dtype=jnp.float32) * s
        att_src1 = jax.random.normal(ks[4], (8, 8), dtype=jnp.float32) * s
        att_dst1 = jax.random.normal(ks[5], (8, 8), dtype=jnp.float32) * s
        b1 = jnp.zeros((64,), dtype=jnp.float32)
        W2 = jax.random.normal(ks[6], (64, OUT_CH), dtype=jnp.float32) * s
        att_src2 = jax.random.normal(ks[7], (1, OUT_CH), dtype=jnp.float32) * s
        att_dst2 = jax.random.normal(ks[8], (1, OUT_CH), dtype=jnp.float32) * s
        b2 = jnp.zeros((OUT_CH,), dtype=jnp.float32)
        return {'x': x, 'edge_index': edge_index, 'W_map': W_map, 'b_map': b_map, 'W1': W1, 'att_src1': att_src1, 'att_dst1': att_dst1, 'b1': b1, 'W2': W2, 'att_src2': att_src2, 'att_dst2': att_dst2, 'b2': b2}
    _L3_gnn_all = _L3_gnn_setup()
    _L3_gnn_in = {k: v for k, v in _L3_gnn_all.items() if k in ('W_map', 'b_map', 'W1', 'att_src1', 'att_dst1', 'b1', 'W2', 'att_src2', 'att_dst2', 'b2')}
    del _L3_gnn_all
    return {'x': x, 'src': src, 'dst': dst, 'L0_gnn_W': _L0_gnn_in['W'], 'L0_gnn_b': _L0_gnn_in['b'], 'L0_gnn_gamma': _L0_gnn_in['gamma'], 'L0_gnn_beta': _L0_gnn_in['beta'], 'L1_gnn_gcn_w': _L1_gnn_in['gcn_w'], 'L1_gnn_gcn_b': _L1_gnn_in['gcn_b'], 'L1_gnn_gat_w': _L1_gnn_in['gat_w'], 'L1_gnn_att_src': _L1_gnn_in['att_src'], 'L1_gnn_att_dst': _L1_gnn_in['att_dst'], 'L1_gnn_gat_b': _L1_gnn_in['gat_b'], 'L1_gnn_ln_gamma': _L1_gnn_in['ln_gamma'], 'L1_gnn_ln_beta': _L1_gnn_in['ln_beta'], 'L2_gnn_W': _L2_gnn_in['W'], 'L2_gnn_w_ih': _L2_gnn_in['w_ih'], 'L2_gnn_w_hh': _L2_gnn_in['w_hh'], 'L2_gnn_b_ih': _L2_gnn_in['b_ih'], 'L2_gnn_b_hh': _L2_gnn_in['b_hh'], 'L2_gnn_l0_w': _L2_gnn_in['l0_w'], 'L2_gnn_l0_b': _L2_gnn_in['l0_b'], 'L2_gnn_l1_w': _L2_gnn_in['l1_w'], 'L2_gnn_l1_b': _L2_gnn_in['l1_b'], 'L3_gnn_W_map': _L3_gnn_in['W_map'], 'L3_gnn_b_map': _L3_gnn_in['b_map'], 'L3_gnn_W1': _L3_gnn_in['W1'], 'L3_gnn_att_src1': _L3_gnn_in['att_src1'], 'L3_gnn_att_dst1': _L3_gnn_in['att_dst1'], 'L3_gnn_b1': _L3_gnn_in['b1'], 'L3_gnn_W2': _L3_gnn_in['W2'], 'L3_gnn_att_src2': _L3_gnn_in['att_src2'], 'L3_gnn_att_dst2': _L3_gnn_in['att_dst2'], 'L3_gnn_b2': _L3_gnn_in['b2']}

def reference(x, src, dst, L0_gnn_W, L0_gnn_b, L0_gnn_gamma, L0_gnn_beta, L1_gnn_gcn_w, L1_gnn_gcn_b, L1_gnn_gat_w, L1_gnn_att_src, L1_gnn_att_dst, L1_gnn_gat_b, L1_gnn_ln_gamma, L1_gnn_ln_beta, L2_gnn_W, L2_gnn_w_ih, L2_gnn_w_hh, L2_gnn_b_ih, L2_gnn_b_hh, L2_gnn_l0_w, L2_gnn_l0_b, L2_gnn_l1_w, L2_gnn_l1_b, L3_gnn_W_map, L3_gnn_b_map, L3_gnn_W1, L3_gnn_att_src1, L3_gnn_att_dst1, L3_gnn_b1, L3_gnn_W2, L3_gnn_att_src2, L3_gnn_att_dst2, L3_gnn_b2):
    import jax
    import jax.numpy as jnp

    def _L0_gnn_ref(x, W, b, gamma, beta, edge_index):
        import jax, jax.numpy as jnp
        import numpy as np
        N_NODES = 3125
        N_EDGES = 40000
        D = 128
        BN_EPS = 1e-05
        N = x.shape[0]
        xw = x @ W
        loops = jnp.arange(N, dtype=edge_index.dtype)
        src = jnp.concatenate([edge_index[0], loops])
        dst = jnp.concatenate([edge_index[1], loops])
        ones = jnp.ones(src.shape[0], dtype=x.dtype)
        deg = jax.ops.segment_sum(ones, dst, num_segments=N)
        dinv = jnp.where(deg > 0, jax.lax.rsqrt(deg), 0.0)
        norm = dinv[src] * dinv[dst]
        msg = xw[src] * norm[:, None]
        h = jax.ops.segment_sum(msg, dst, num_segments=N) + b
        mean = jnp.mean(h, axis=0)
        var = jnp.mean(jnp.square(h - mean), axis=0)
        h = (h - mean) * jax.lax.rsqrt(var + BN_EPS) * gamma + beta
        h = jax.nn.relu(h)
        h = x + h
        return h

    def _L1_gnn_ref(x, edge_index, gcn_w, gcn_b, gat_w, att_src, att_dst, gat_b, ln_gamma, ln_beta):
        import jax, jax.numpy as jnp
        import numpy as np
        N = 3125
        IN_DIM = 128
        OUT_DIM = 128
        HEADS = 2
        EPS = 1e-05
        NEG_SLOPE = 0.2

        def _add_self_loops(edge_index, num_nodes):
            loop = jnp.arange(num_nodes, dtype=edge_index.dtype)
            src = jnp.concatenate([edge_index[0], loop])
            dst = jnp.concatenate([edge_index[1], loop])
            return (src, dst)

        def _layernorm(h, gamma, beta):
            mu = jnp.mean(h, axis=-1, keepdims=True)
            var = jnp.mean(jnp.square(h - mu), axis=-1, keepdims=True)
            return (h - mu) * jax.lax.rsqrt(var + EPS) * gamma + beta

        def _silu(h):
            return h * jax.nn.sigmoid(h)

        def _gcn_conv(x, src, dst, W, b, num_nodes):
            h = x @ W
            deg = jnp.zeros((num_nodes,), h.dtype).at[dst].add(1.0)
            dinv = jnp.where(deg > 0, jax.lax.rsqrt(jnp.maximum(deg, 1.0)), 0.0)
            norm = dinv[src] * dinv[dst]
            msg = h[src] * norm[:, None]
            out = jnp.zeros((num_nodes, h.shape[1]), h.dtype).at[dst].add(msg)
            return out + b

        def _gat_conv(x, src, dst, W, att_src, att_dst, b, num_nodes, heads):
            C = W.shape[1] // heads
            h = (x @ W).reshape(num_nodes, heads, C)
            a_src = jnp.sum(h * att_src, axis=-1)
            a_dst = jnp.sum(h * att_dst, axis=-1)
            e = a_src[src] + a_dst[dst]
            e = jnp.where(e > 0, e, NEG_SLOPE * e)
            m = jax.ops.segment_max(e, dst, num_segments=num_nodes)
            ex = jnp.exp(e - m[dst])
            den = jax.ops.segment_sum(ex, dst, num_segments=num_nodes)
            alpha = ex / den[dst]
            msg = h[src] * alpha[:, :, None]
            out = jnp.zeros((num_nodes, heads, C), h.dtype).at[dst].add(msg)
            return jnp.mean(out, axis=1) + b
        num_nodes = x.shape[0]
        src, dst = _add_self_loops(edge_index, num_nodes)
        h = _gcn_conv(x, src, dst, gcn_w, gcn_b, num_nodes)
        h = _silu(_layernorm(h, ln_gamma, ln_beta))
        h = _gat_conv(h, src, dst, gat_w, att_src, att_dst, gat_b, num_nodes, HEADS)
        h = _silu(_layernorm(h, ln_gamma, ln_beta))
        return h

    def _L2_gnn_ref(x, edge_index, W, w_ih, w_hh, b_ih, b_hh, l0_w, l0_b, l1_w, l1_b):
        import jax, jax.numpy as jnp
        import numpy as np
        N = 6250
        E = 100000
        ANN = 128
        HID = 128
        S = ANN + HID
        L = 5
        MLP_H = 256
        OUT = 128

        def _forward(x, edge_index, W, w_ih, w_hh, b_ih, b_hh, l0_w, l0_b, l1_w, l1_b):
            n = x.shape[0]
            s = W.shape[-1]
            src, dst = (edge_index[0], edge_index[1])
            h = jnp.pad(x, ((0, 0), (0, s - x.shape[-1])))

            def step(h, Wl):
                m = h @ Wl
                agg = jax.ops.segment_sum(m[src], dst, num_segments=n)
                gi = agg @ w_ih.T + b_ih
                gh = h @ w_hh.T + b_hh
                ir, iz, in_ = jnp.split(gi, 3, axis=-1)
                hr, hz, hn = jnp.split(gh, 3, axis=-1)
                r = jax.nn.sigmoid(ir + hr)
                z = jax.nn.sigmoid(iz + hz)
                ng = jnp.tanh(in_ + r * hn)
                h_new = (1.0 - z) * ng + z * h
                return (h_new, None)
            h, _ = jax.lax.scan(step, h, W)
            cat = jnp.concatenate([h, x], axis=-1)
            y = jax.nn.relu(cat @ l0_w.T + l0_b)
            y = jax.nn.relu(y @ l1_w.T + l1_b)
            return y
        return _forward(x, edge_index, W, w_ih, w_hh, b_ih, b_hh, l0_w, l0_b, l1_w, l1_b)

    def _L3_gnn_ref(x, edge_index, W_map, b_map, W1, att_src1, att_dst1, b1, W2, att_src2, att_dst2, b2):
        import jax, jax.numpy as jnp
        import numpy as np
        N = 3125
        E = 100000
        IN_CH = 128
        OUT_CH = 128
        NEG_SLOPE = 0.2

        def _gat_conv(x, W, att_src, att_dst, bias, src, dst, heads, out_ch, concat):
            n = x.shape[0]
            h = (x @ W).reshape(n, heads, out_ch)
            a_src = jnp.einsum('nhc,hc->nh', h, att_src)
            a_dst = jnp.einsum('nhc,hc->nh', h, att_dst)
            logits = jax.nn.leaky_relu(a_src[src] + a_dst[dst], NEG_SLOPE)
            m = jax.ops.segment_max(logits, dst, num_segments=n)
            e = jnp.exp(logits - m[dst])
            denom = jax.ops.segment_sum(e, dst, num_segments=n)
            alpha = e / denom[dst]
            msgs = h[src] * alpha[:, :, None]
            out = jax.ops.segment_sum(msgs, dst, num_segments=n)
            out = out.reshape(n, heads * out_ch) if concat else out.mean(axis=1)
            return out + bias
        loops = jnp.arange(N, dtype=edge_index.dtype)
        src = jnp.concatenate([edge_index[0], loops])
        dst = jnp.concatenate([edge_index[1], loops])
        h = x @ W_map + b_map
        h = _gat_conv(h, W1, att_src1, att_dst1, b1, src, dst, heads=8, out_ch=8, concat=True)
        h = jax.nn.elu(h)
        out = _gat_conv(h, W2, att_src2, att_dst2, b2, src, dst, heads=1, out_ch=OUT_CH, concat=False)
        return out
    edge_index = jnp.stack([src, dst])
    h = jnp.maximum(_layernorm(x, axis=-1), 0.0)
    x = x + _L0_gnn_ref(h, L0_gnn_W, L0_gnn_b, L0_gnn_gamma, L0_gnn_beta, edge_index)
    h = jnp.maximum(_layernorm(x, axis=-1), 0.0)
    x = x + _L1_gnn_ref(h, edge_index, L1_gnn_gcn_w, L1_gnn_gcn_b, L1_gnn_gat_w, L1_gnn_att_src, L1_gnn_att_dst, L1_gnn_gat_b, L1_gnn_ln_gamma, L1_gnn_ln_beta)
    h = jnp.maximum(_layernorm(x, axis=-1), 0.0)
    x = x + _L2_gnn_ref(h, edge_index, L2_gnn_W, L2_gnn_w_ih, L2_gnn_w_hh, L2_gnn_b_ih, L2_gnn_b_hh, L2_gnn_l0_w, L2_gnn_l0_b, L2_gnn_l1_w, L2_gnn_l1_b)
    h = jnp.maximum(_layernorm(x, axis=-1), 0.0)
    x = x + _L3_gnn_ref(h, edge_index, L3_gnn_W_map, L3_gnn_b_map, L3_gnn_W1, L3_gnn_att_src1, L3_gnn_att_dst1, L3_gnn_b1, L3_gnn_W2, L3_gnn_att_src2, L3_gnn_att_dst2, L3_gnn_b2)
    return x

_drawn_inputs = setup_inputs


def setup_inputs(seed=0):
    import zlib

    import numpy as np

    out = dict(_drawn_inputs(seed))
    spreads = {'L0_gnn_b': (0.0, 2.0),
     'L0_gnn_gamma': (1.0, 0.2),
     'L0_gnn_beta': (0.0, 0.1),
     'L1_gnn_gcn_b': (0.0, 0.1),
     'L1_gnn_gat_b': (0.0, 0.1),
     'L1_gnn_ln_gamma': (1.0, 0.2),
     'L1_gnn_ln_beta': (0.0, 0.1),
     'L3_gnn_b_map': (0.0, 0.1),
     'L3_gnn_b1': (0.0, 0.1),
     'L3_gnn_b2': (0.0, 0.1)}
    factors = {'L1_gnn_att_src': 8.0,
     'L1_gnn_att_dst': 46.626,
     'L2_gnn_l0_b': 5.999,
     'L2_gnn_l1_b': 2.89,
     'L3_gnn_att_src1': 5.199,
     'L3_gnn_att_dst1': 8.0,
     'L3_gnn_att_src2': 8.0,
     'L3_gnn_att_dst2': 22.045}
    for name, (base, spread) in spreads.items():
        noise = np.random.default_rng([zlib.crc32(name.encode()), seed]).standard_normal(out[name].shape)
        drawn = base * np.exp(spread * noise) if base else spread * noise
        out[name] = jnp.asarray(drawn.astype(out[name].dtype))
    for name, factor in factors.items():
        out[name] = (out[name] * factor).astype(out[name].dtype)
    return out
```

```python
from contextlib import ExitStack

import numpy as np

import concourse.bass as bass
from concourse import mybir

F32 = mybir.dt.float32
BF16 = mybir.dt.bfloat16
I32 = mybir.dt.int32
ALU = mybir.AluOpType
ACT = mybir.ActivationFunctionType
AX = mybir.AxisListType

P = 128
N = 3125
E = 53125
D = 128
NT = -(-N // P)
NP = NT * P
LAST = N - (NT - 1) * P
ET = -(-E // P)
EPR = 512
ER = ET * P // EPR
ETR = EPR // P
STEPS = ET + NT - 1
KJ = 4
KP = STEPS // KJ
BODY = 20
GRP = 5
NG = BODY // GRP
ITERS = STEPS // BODY
RING = 4
BIG = 1e30
NEG = 0.2
EPS = 1e-5
S2 = 256
LAYERS = 5
CH = 400
NCH = NP // CH
TQ = 100
assert ER * EPR == ET * P and KP * KJ == STEPS and ITERS * BODY == STEPS and NCH * CH == NP


class Chain:

    def __init__(self, nc, name):
        self.nc, self.name = nc, name
        self.done = nc.alloc_semaphore(name + "_done")
        self.landed = nc.alloc_semaphore(name + "_landed")
        self.fetched = nc.alloc_semaphore(name + "_fetched")
        self.counts = (0, 0, 0)
        self.queues = {k: [] for k in "ptvas"}
        self.floor = None

    def together(self):
        return _Together(self)

    def _queue(self, engine, build, kind):
        self.queues[engine].append((self.floor or self.counts, build, kind))
        self.counts = tuple(n + (0 if k != kind else 16 if k else 1) for k, n in enumerate(self.counts))

    def op(self, engine, build):
        self._queue(engine, build, 0)

    def dma(self, engine, out, in_):
        self._queue(engine, lambda e: e.dma_start(out, in_), 1)

    def gather(self, out, table, index):
        self._queue("p", lambda e: e.indirect_dma_start(
            out=out, out_offset=None, in_=table,
            in_offset=bass.IndirectOffsetOnAxis(ap=index, axis=0)), 2)

    def run(self):
        sems = (self.done, self.landed, self.fetched)
        queues, self.queues = self.queues, {k: [] for k in "ptvas"}

        def wait(e, need, seen):
            for sem, n, was in zip(sems, need, seen):
                if n > was:
                    e.wait_ge(sem, n)
            return tuple(map(max, need, seen))

        def emit(e, queue):
            seen = (0, 0, 0)
            for need, build, kind in queue:
                seen = wait(e, need, seen)
                build(e).then_inc(sems[kind], 16 if kind else 1)

        with self.nc.Block() as block:
            @block.gpsimd
            def _(e):
                emit(e, queues["p"])

            @block.tensor
            def _(e):
                emit(e, queues["t"])

            @block.vector
            def _(e):
                emit(e, queues["v"])

            @block.scalar
            def _(e):
                emit(e, queues["a"])

            @block.sync
            def _(e):
                emit(e, queues["s"])
                wait(e, self.counts, (0, 0, 0))


class _Together:
    def __init__(self, chain):
        self.chain = chain

    def __enter__(self):
        self.chain.floor = self.chain.counts

    def __exit__(self, *_):
        self.chain.floor = None


def node_rows(dram):
    return dram.rearrange("(t p) w -> p t w", p=P)


def over_nodes(ap, nt=NT):
    return ap.unsqueeze(1).to_broadcast([ap.shape[0], nt, ap.shape[1]])


def over_features(ap, w):
    return ap.unsqueeze(2).to_broadcast([ap.shape[0], ap.shape[1], w])


class Kernel:
    def __init__(self, nc, ins, out):
        self.nc, self.ins, self.out = nc, ins, out
        self.stack = ExitStack()
        self.count = 0

    def name(self, what):
        self.count += 1
        return f"{what}_{self.count}"

    def sb(self, what, shape, dt=F32, stack=None):
        return (stack or self.stack).enter_context(self.nc.sbuf_tensor(self.name(what), shape, dt))

    def dram(self, what, shape, dt=F32):
        return self.nc.dram_tensor(self.name(what), shape, dt, kind="Internal").ap()

    def psum(self, stack, shape=(P, 8, 512)):
        return stack.enter_context(self.nc.psum_tensor(self.name("psum"), list(shape), F32))

    def constants(self):
        sb = self.sb
        self.ident = sb("ident", [P, P])
        self.iota = sb("iota", [P, P])
        self.iota_nt = sb("iota_nt", [P, NT])
        self.pidx = sb("pidx", [P, 1])
        self.ones = sb("ones", [P, P])
        self.live = sb("live", [P, P])
        self.src_idx = sb("src_idx", [P, STEPS], I32)
        self.place = sb("place", [P, STEPS])
        self.window = sb("window", [1, STEPS + 4], I32)
        self.src_win = sb("src_win", [P, STEPS])
        self.valid = sb("valid", [P, STEPS])
        self.last = sb("last", [P, STEPS])
        self.cut_start = sb("cut_start", [KP, KJ, P])
        self.cut_last = sb("cut_last", [KP, KJ, P])
        self.rows_start = sb("rows_start", [8, STEPS])
        self.rows_last = sb("rows_last", [8, STEPS])
        self.win_hot = sb("win_hot", [KP, KJ, NT])
        self.dinv = sb("dinv", [P, NT])
        self.x = sb("x", [P, NT, D])
        self.row_scratch = self.dram("row_scratch", [2, STEPS * P], BF16)
        self.edge_scratch = self.dram("edge_scratch", [ET, 4 * P])
        c = self.c = Chain(self.nc, "c")
        with c.together():
            c.op("p", lambda e: e.memset(self.ident[:], 0.0))
            c.op("p", lambda e: e.iota(self.iota[:], [[1, P]], base=0, channel_multiplier=0,
                                       allow_small_or_imprecise_dtypes=True))
            c.op("p", lambda e: e.iota(self.iota_nt[:], [[1, NT]], base=0, channel_multiplier=0,
                                       allow_small_or_imprecise_dtypes=True))
            c.op("p", lambda e: e.iota(self.pidx[:], [[1, 1]], base=0, channel_multiplier=1,
                                       allow_small_or_imprecise_dtypes=True))
            c.op("v", lambda e: e.memset(self.ones[:], 1.0))
            c.op("v", lambda e: e.memset(self.live[:], 0.0))
            c.op("v", lambda e: e.memset(self.window[:], 0))
            c.op("v", lambda e: e.memset(self.x[:, NT - 1, :], 0.0))
        with c.together():
            c.op("p", lambda e: e.affine_select(out=self.ident[:], in_=self.ident[:], compare_op=ALU.not_equal,
                                                fill=1.0, base=0, pattern=[[-1, P]], channel_multiplier=1))
            c.op("v", lambda e: e.memset(self.live[0:LAST, :], 1.0))
            x = self.ins["x"]
            c.dma("s", self.x[:, 0:NT - 1, :], node_rows(x[0:(NT - 1) * P, :]))
            c.dma("s", self.x[0:LAST, NT - 1, :], x[(NT - 1) * P:N, :])

    def graph(self):
        c = self.c
        st = ExitStack()
        sb = lambda *a: self.sb(*a, stack=st)
        src, dst = self.ins["src"], self.ins["dst"]
        whole, rest = E // EPR, E % EPR
        si, di, pi, ni = (sb(w, [ER, EPR], I32) for w in ("src_i", "dst_i", "prev_i", "next_i"))
        pack = sb("pack", [ER, ETR, 4, P])
        first = sb("first", [ER, ETR], I32)
        first_f = sb("first_f", [ER, ETR])
        tile_no = sb("tile_no", [ER, ETR])
        some = sb("some", [ER, ETR])
        step_row = sb("step_row", [P, STEPS])
        reached = sb("reached", [ER, ETR, STEPS])
        tile_c = sb("tile_c", [KP, KJ])
        tile_i = sb("tile_i", [KP, KJ], I32)
        step_c = sb("step_c", [KP, KJ])
        win_c = sb("win_c", [KP, KJ])
        win128 = sb("win128", [KP, KJ])
        win_r = sb("win_r", [1, STEPS])
        rows = sb("rows", [KP, KJ, 4 * P])
        place_r = sb("place_r", [KP, KJ, P])
        valid_r = sb("valid_r", [KP, KJ, P])
        start_r = sb("start_r", [KP, KJ, P])
        last_r = sb("last_r", [KP, KJ, P])
        src_ri = sb("src_ri", [KP, KJ, P], I32)
        low_i = sb("low_i", [KP, KJ, P], I32)
        high_i = sb("high_i", [KP, KJ, P], I32)
        low_f = sb("low_f", [KP, KJ, P])
        high_f = sb("high_f", [KP, KJ, P])
        bf = sb("bf", [KP, 2, KJ, P], BF16)
        any_f = sb("any_f", [KP, 2, KJ])
        any8 = sb("any8", [KP, 2, KJ, 8])
        ps = self.psum(st)

        with c.together():
            for t, fill in ((si, 0), (di, NP), (pi, -1), (ni, -1)):
                c.op("v", lambda e, t=t, fill=fill: e.memset(t[:], fill))
            c.op("p", lambda e: e.iota(tile_no[:], [[1, ETR]], base=0, channel_multiplier=ETR,
                                       allow_small_or_imprecise_dtypes=True))
            c.op("p", lambda e: e.iota(step_row[:], [[1, STEPS]], base=0, channel_multiplier=0,
                                       allow_small_or_imprecise_dtypes=True))
            c.op("p", lambda e: e.iota(step_c[:], [[KP, KJ]], base=0, channel_multiplier=1,
                                       allow_small_or_imprecise_dtypes=True))
        one = lambda ap: ap.rearrange("(a b) -> a b", a=1)
        many = lambda ap: ap.rearrange("(a b) -> a b", b=EPR)
        with c.together():
            for t, a in ((si, src), (di, dst)):
                c.dma("s", t[0:whole, :], many(a[0:whole * EPR]))
                c.dma("a", t[whole:whole + 1, 0:rest], one(a[whole * EPR:E]))
            c.dma("s", pi[0:1, 1:EPR], one(dst[0:EPR - 1]))
            c.dma("s", pi[1:whole, :], many(dst[EPR - 1:whole * EPR - 1]))
            c.dma("a", pi[whole:whole + 1, 0:rest + 1], one(dst[whole * EPR - 1:E]))
            c.dma("s", ni[0:whole, :], many(dst[1:whole * EPR + 1]))
            c.dma("a", ni[whole:whole + 1, 0:rest - 1], one(dst[whole * EPR + 1:E]))
        row = lambda t: t[:].rearrange("p (g q) -> p g q", g=ETR)
        with c.together():
            c.op("v", lambda e: e.tensor_copy(pack[:, :, 0, :], row(si)))
            c.op("v", lambda e: e.tensor_copy(pack[:, :, 1, :], row(di)))
            c.op("v", lambda e: e.tensor_tensor(pack[:, :, 2, :], row(di), row(pi), ALU.not_equal))
            c.op("v", lambda e: e.tensor_tensor(pack[:, :, 3, :], row(di), row(ni), ALU.not_equal))
            c.op("v", lambda e: e.tensor_scalar(first[:], di[:, 0:EPR:P], 7, None, ALU.arith_shift_right))
            c.op("v", lambda e: e.tensor_scalar(some[:], tile_no[:], 1.0, None, ALU.min))
        c.dma("s", self.edge_scratch.rearrange("(p g) w -> p (g w)", g=ETR),
              pack[:].rearrange("p g c q -> p (g c q)"))
        c.op("v", lambda e: e.tensor_copy(first_f[:], first[:]))
        c.op("v", lambda e: e.tensor_tensor(first_f[:], first_f[:], tile_no[:], ALU.add))
        c.op("v", lambda e: e.tensor_tensor(first_f[:], first_f[:], some[:], ALU.mult))
        with c.together():
            for g in range(ETR):
                c.op("v", lambda e, g=g: e.tensor_scalar(reached[:, g, :], step_row[0:ER, :],
                                                         first_f[:, g:g + 1], None, ALU.is_ge))

        def count(e):
            for g in range(ETR):
                e.matmul(ps[0:1, 0, 0:STEPS], self.ones[0:ER, 0:1], reached[:, g, :],
                         start=g == 0, stop=g == ETR - 1)
            for j in range(KJ):
                for g in range(ETR):
                    last = e.matmul(ps[0:KP, 1, j:j + 1], reached[:, g, KP * j:KP * (j + 1)],
                                    self.ones[0:ER, 0:1], start=g == 0, stop=g == ETR - 1)
            return last
        c.op("t", count)
        with c.together():
            c.op("v", lambda e: e.tensor_scalar(tile_c[:], ps[0:KP, 1, 0:KJ], -1.0, None, ALU.add))
            c.op("v", lambda e: e.scalar_tensor_tensor(win_r[:], ps[0:1, 0, 0:STEPS], -1.0, step_row[0:1, :],
                                                       ALU.mult, ALU.add))
        with c.together():
            c.op("v", lambda e: e.tensor_copy(tile_i[:], tile_c[:]))
            c.op("v", lambda e: e.tensor_tensor(win_c[:], step_c[:], tile_c[:], ALU.subtract))
            c.op("v", lambda e: e.tensor_scalar(self.window[:, 1:STEPS + 1], win_r[:], 1.0, None, ALU.add))
        c.op("v", lambda e: e.tensor_scalar(win128[:], win_c[:], float(P), None, ALU.mult))
        with c.together():
            for j in range(KJ):
                c.gather(rows[:, j, :], self.edge_scratch, tile_i[:, j:j + 1])
                c.op("v", lambda e, j=j: e.tensor_scalar(self.win_hot[:, j, :], self.iota_nt[0:KP, :],
                                                         win_c[:, j:j + 1], None, ALU.is_equal))
        part = lambda n: rows[:, :, n * P:(n + 1) * P]
        with c.together():
            for j in range(KJ):
                c.op("v", lambda e, j=j: e.tensor_scalar(place_r[:, j, :], rows[:, j, P:2 * P],
                                                         win128[:, j:j + 1], None, ALU.subtract))
            c.op("a", lambda e: e.copy(src_ri[:], part(0)))
        with c.together():
            c.op("v", lambda e: e.tensor_scalar(valid_r[:], place_r[:], 0.0, None, ALU.is_ge))
            c.op("v", lambda e: e.tensor_scalar(low_i[:], src_ri[:], P - 1, None, ALU.bitwise_and))
            c.op("v", lambda e: e.tensor_scalar(high_i[:], src_ri[:], 7, None, ALU.arith_shift_right))
            c.op("a", lambda e: e.copy(bf[:, 1, :, :], place_r[:]))
        with c.together():
            c.op("v", lambda e: e.scalar_tensor_tensor(valid_r[:], place_r[:], P - 1.0, valid_r[:],
                                                       ALU.is_le, ALU.mult))
            c.op("a", lambda e: e.copy(low_f[:], low_i[:]))
            c.op("a", lambda e: e.copy(bf[:, 0, :, :], low_i[:]))
            c.op("a", lambda e: e.copy(high_f[:], high_i[:]))
        with c.together():
            c.op("v", lambda e: e.tensor_tensor(start_r[:], part(2), valid_r[:], ALU.mult))
            c.op("v", lambda e: e.tensor_tensor(last_r[:], part(3), valid_r[:], ALU.mult))
            for n in range(2):
                c.dma("s", self.row_scratch[n, :].rearrange("(j p q) -> p j q", j=KJ, p=KP), bf[:, n, :, :])
        with c.together():
            c.op("v", lambda e: e.tensor_scalar(self.cut_start[:], start_r[:], -BIG, None, ALU.mult))
            c.op("v", lambda e: e.tensor_scalar(self.cut_last[:], last_r[:], -BIG, None, ALU.mult))
        with c.together():
            c.op("v", lambda e: e.tensor_reduce(any_f[:, 0, :], self.cut_start[:], AX.X, ALU.min))
            c.op("v", lambda e: e.tensor_reduce(any_f[:, 1, :], self.cut_last[:], AX.X, ALU.min))
        c.op("v", lambda e: e.tensor_copy(any8[:], any_f[:].unsqueeze(3).to_broadcast([KP, 2, KJ, 8])))

        turned = (part(0), place_r, high_f, valid_r, last_r)

        def turn(e):
            for n, t in enumerate(turned):
                for j in range(KJ):
                    e.transpose(ps[:, n, KP * j:KP * (j + 1)], t[:, j, :], self.ident[0:KP, 0:KP])
            for n in range(2):
                for j in range(KJ):
                    last = e.transpose(ps[0:8, 5 + n, KP * j:KP * (j + 1)], any8[:, n, j, :],
                                       self.ident[0:KP, 0:KP])
            return last
        c.op("t", turn)
        with c.together():
            for n, t in enumerate((self.src_idx, self.place, self.src_win, self.valid, self.last)):
                c.op("va"[n % 2], lambda e, n=n, t=t: (e.copy if n % 2 else e.tensor_copy)(t[:], ps[:, n, 0:STEPS]))
            c.op("v", lambda e: e.tensor_copy(self.rows_start[:], ps[0:8, 5, 0:STEPS]))
            c.op("v", lambda e: e.tensor_copy(self.rows_last[:], ps[0:8, 6, 0:STEPS]))
        c.run()
        st.close()

    def degrees(self):
        nc, c = self.nc, self.c
        st = ExitStack()
        hot = self.sb("deg_hot", [P, 2, BODY, P], BF16, st)
        one = self.sb("one_bf", [P, 1], BF16, st)
        by_step = self.sb("deg_step", [P, STEPS], F32, st)
        turned = self.sb("deg_turned", [KP, KJ, P], F32, st)
        ps = self.psum(st)
        hots, cols, kept = (nc.alloc_semaphore(n) for n in ("deg_hots", "deg_cols", "deg_kept"))
        with nc.Block() as block:
            @block.vector
            def _(e):
                e.memset(one[:], 1.0).then_inc(hots, 1)
                with e.Fori(0, ITERS // 2) as i:
                    for b in range(2):
                        e.wait_ge(cols, i * 2 + b + 1)
                        k = i * (2 * BODY) + b * BODY
                        e.tensor_tensor(hot[:, b, :, :], self.iota[:].unsqueeze(1).to_broadcast([P, BODY, P]),
                                        over_features(self.place[:, bass.ds(k, BODY)], P),
                                        ALU.is_equal).then_inc(hots, 1)

            @block.tensor
            def _(e):
                e.sem_inc(cols, 2)
                with e.Fori(0, ITERS // 2) as i:
                    for b in range(2):
                        e.wait_ge(hots, i * 2 + b + 2)
                        e.wait_ge(kept, i * 2 + b + 1)
                        for s in range(BODY):
                            mm = e.matmul(ps[:, b, s:s + 1], hot[:, b, s, :], one[:], start=True, stop=True)
                        mm.then_inc(cols, 1)

            @block.scalar
            def _(e):
                e.sem_inc(kept, 2)
                with e.Fori(0, ITERS // 2) as i:
                    for b in range(2):
                        e.wait_ge(cols, i * 2 + b + 3)
                        e.copy(by_step[:, bass.ds(i * (2 * BODY) + b * BODY, BODY)],
                               ps[:, b, 0:BODY]).then_inc(kept, 1)

        def turn(e):
            for j in range(KJ):
                last = e.transpose(ps[0:KP, 0, P * j:P * (j + 1)], by_step[:, KP * j:KP * (j + 1)], self.ident[:])
            return last
        c.op("t", turn)
        c.op("v", lambda e: e.tensor_copy(turned[:].rearrange("p j q -> p (j q)"), ps[0:KP, 0, :]))

        def total(e):
            for j in range(KJ):
                last = e.matmul(ps[:, 1, 0:NT], turned[:, j, :], self.win_hot[:, j, :],
                                start=j == 0, stop=j == KJ - 1)
            return last
        c.op("t", total)
        c.op("v", lambda e: e.tensor_scalar(self.dinv[:], ps[:, 1, 0:NT], 1.0, None, ALU.add))
        c.op("v", lambda e: e.reciprocal(self.dinv[:], self.dinv[:]))
        c.op("a", lambda e: e.sqrt(self.dinv[:], self.dinv[:]))
        c.run()
        st.close()

    def edge_sums(self, ps, table, width, acc, heads=(), extra=None, scaled=None, turned=False, sems=None,
                  before=0):
        nc = self.nc
        st = ExitStack()
        n_hot = len(heads) + (not heads or extra is not None)
        rows = self.sb("rows", [P, BODY, width], F32, st)
        index = self.sb("index", [P, BODY], I32, st)
        hot = self.sb("hot", [P, RING, n_hot, P], F32, st)
        msg = self.sb("msg", [P, RING, width], F32, st) if scaled is not None else None
        cols = width + (extra.shape[2] if extra is not None else 0)
        if sems is None:
            sems = self.edge_sems()
        indexed, ready, summed, kept, started, *fetched = sems

        def landed(i):
            return before * (ITERS * 16 * GRP) + i * (16 * GRP) + 16 * GRP

        def each(e, body):
            with e.Fori(0, ITERS) as i:
                body(i, i * BODY)

        with nc.Block() as block:
            @block.scalar
            def _(e):
                def body(i, k):
                    for g in range(NG):
                        e.wait_ge(summed, k + GRP * (g + 1))
                        e.copy(index[:, GRP * g:GRP * (g + 1)],
                               self.src_idx[:, bass.ds(k + GRP * g, GRP)]).then_inc(indexed, 1)
                each(e, body)

            @block.gpsimd
            def _(e):
                def body(i, k):
                    for g in range(NG):
                        e.wait_ge(indexed, i * NG + g + 1)
                        e.sem_inc(started, 1)
                        for s in range(GRP * g, GRP * (g + 1)):
                            e.indirect_dma_start(
                                out=rows[:, s, :], out_offset=None, in_=table,
                                in_offset=bass.IndirectOffsetOnAxis(ap=index[:, s:s + 1], axis=0)
                            ).then_inc(fetched[g], 16)
                each(e, body)

            @block.vector
            def _(e):
                regs = [e.alloc_register(self.name("window_reg")) for _ in range(GRP)]

                def add(r, w, own):
                    e.wait_ge(kept, own)
                    if turned:
                        a = acc[:, :, bass.ds(w * P, P)]
                        b = ps[:, r, 0:width].rearrange("p (f n) -> p f n", n=P)
                    else:
                        a = acc[:].rearrange("p t w -> p (t w)")[:, bass.ds(w * cols, cols)]
                        b = ps[:, r, 0:cols]
                    e.tensor_tensor(a, a, b, ALU.add).then_inc(kept, 1)

                def body(i, k):
                    for s in range(BODY):
                        if s % GRP == 0:
                            e.load(regs, self.window[0:1, bass.ds(k + s, GRP)])
                            w = [e.snap(r, min_val=0, max_val=NT - 1) for r in regs]
                            if scaled is not None:
                                e.wait_ge(fetched[s // GRP], landed(i))
                        r = s % RING
                        e.wait_ge(summed, k + s + BODY - RING + 1)
                        place = self.place[:, bass.ds(k + s, 1)]
                        todo = []
                        for h, weight in enumerate(heads):
                            todo.append(lambda h=h, weight=weight: e.tensor_scalar(
                                hot[:, r, h, :], self.iota[:], place, weight[:, bass.ds(k + s, 1)],
                                ALU.is_equal, ALU.mult))
                        if n_hot > len(heads):
                            todo.append(lambda: e.tensor_scalar(hot[:, r, n_hot - 1, :], self.iota[:], place,
                                                                None, ALU.is_equal))
                        if scaled is not None:
                            per = width // 8
                            todo.append(lambda: e.tensor_tensor(
                                msg[:, r, :].rearrange("p (h c) -> p h c", h=8),
                                rows[:, s, :].rearrange("p (h c) -> p h c", h=8),
                                over_features(scaled[:, bass.ds(k + s, 1), :].rearrange("p a h -> p (a h)"), per),
                                ALU.mult))
                        for n, build in enumerate(todo):
                            inst = build()
                        inst.then_inc(ready, 1)
                        e.wait_ge(summed, k + s + BODY)
                        add((s - 1) % RING, w[s % GRP], k + s + RING)
                each(e, body)
                e.load(regs[:1], self.window[0:1, STEPS:STEPS + 1])
                w = e.snap(regs[0], min_val=0, max_val=NT - 1)
                e.wait_ge(summed, STEPS + BODY)
                add((STEPS - 1) % RING, w, STEPS + RING)
                e.wait_ge(kept, STEPS + RING + 1)
                for r in regs:
                    e.free_register(r)

            @block.tensor
            def _(e):
                e.sem_inc(summed, BODY)
                e.sem_inc(kept, RING)

                def body(i, k):
                    for s in range(BODY):
                        r = s % RING
                        if s % GRP == 0:
                            e.wait_ge(fetched[s // GRP], landed(i))
                        e.wait_ge(ready, k + s + 1)
                        e.wait_ge(kept, k + s + 2)
                        plain = hot[:, r, n_hot - 1, :]
                        if turned:
                            for f in range(width // P):
                                mm = e.matmul(ps[:, r, f * P:(f + 1) * P], rows[:, s, f * P:(f + 1) * P], plain,
                                              start=True, stop=True)
                        elif heads:
                            for h in range(len(heads)):
                                mm = e.matmul(ps[:, r, h * P:(h + 1) * P], hot[:, r, h, :],
                                              rows[:, s, h * P:(h + 1) * P], start=True, stop=True)
                        else:
                            source = rows[:, s, :] if scaled is None else msg[:, r, :]
                            mm = e.matmul(ps[:, r, 0:width], plain, source, start=True, stop=True)
                        if extra is not None:
                            mm = e.matmul(ps[:, r, width:cols], plain,
                                          extra[:, bass.ds(k + s, 1), :].rearrange("p a n -> p (a n)"),
                                          start=True, stop=True)
                        mm.then_inc(summed, 1)
                each(e, body)
        st.close()

    def edge_sems(self):
        self.count += 1
        names = ["indexed", "ready", "summed", "kept", "started"] + [f"fetched{g}" for g in range(NG)]
        return [self.nc.alloc_semaphore(f"{n}_{self.count}") for n in names]

    def to_features(self, ps, h, ht, width=D):
        c = self.c
        flat = ps[:].rearrange("p b n -> p (b n)")

        def turn(e):
            for t in range(NT):
                last = e.transpose(flat[0:width, t * P:(t + 1) * P], h[:, t, :], self.ident[:])
            return last
        c.op("t", turn)
        half = 12 * P
        with c.together():
            c.op("v", lambda e: e.tensor_copy(ht[0:width, 0:half], flat[0:width, 0:half]))
            c.op("a", lambda e: e.copy(ht[0:width, half:NP], flat[0:width, half:NP]))

    def layer_norm(self, x, d, gamma=None, beta=None):
        c = self.c
        st = ExitStack()
        sq = self.sb("sq", [P, NT, D], F32, st)
        mean, var = self.sb("mean", [P, NT], F32, st), self.sb("var", [P, NT], F32, st)
        c.op("v", lambda e: e.tensor_reduce(mean[:], x, AX.X, ALU.add))
        c.op("v", lambda e: e.tensor_scalar(mean[:], mean[:], 1.0 / D, None, ALU.mult))
        c.op("v", lambda e: e.tensor_tensor(d, x, over_features(mean[:], D), ALU.subtract))
        c.op("a", lambda e: e.activation(sq[:], d, ACT.Square))
        c.op("v", lambda e: e.tensor_reduce(var[:], sq[:], AX.X, ALU.add))
        c.op("v", lambda e: e.tensor_scalar(var[:], var[:], 1.0 / D, EPS, ALU.mult, ALU.add))
        c.op("v", lambda e: e.reciprocal(var[:], var[:]))
        c.op("a", lambda e: e.sqrt(var[:], var[:]))
        if gamma is None:
            c.op("v", lambda e: e.scalar_tensor_tensor(d, d, 0.0, over_features(var[:], D), ALU.max, ALU.mult))
        else:
            c.op("v", lambda e: e.tensor_tensor(d, d, over_features(var[:], D), ALU.mult))
            c.op("v", lambda e: e.tensor_tensor(d, d, over_nodes(gamma), ALU.mult))
            c.op("v", lambda e: e.tensor_tensor(d, d, over_nodes(beta), ALU.add))
            c.op("a", lambda e: e.activation(d, d, ACT.Silu))
        c.run()
        st.close()

    def row(self, name, st, parts=P):
        v = self.ins[name]
        if len(v.shape) == 2:
            v = v.rearrange("h c -> (h c)")
        t = self.sb(name, [parts, v.shape[0]], F32, st)
        self.c.dma("s", t[:], v.partition_broadcast(parts))
        return t

    def columns(self, name, st):
        v = self.ins[name]
        t = self.sb(name, [P, v.shape[0] // P], F32, st)
        for j in range(v.shape[0] // P):
            self.c.dma("s", t[:, j:j + 1], v[j * P:(j + 1) * P].rearrange("(p a) -> p a", a=1))
        return t

    def matrix(self, name, st):
        v = self.ins[name]
        k, w = v.shape
        if k <= P:
            t = self.sb(name, [k, w], F32, st)
            self.c.dma("s", t[:], v)
        else:
            t = self.sb(name, [P, k // P, w], F32, st)
            for j in range(k // P):
                self.c.dma("s", t[:, j, :], v[j * P:(j + 1) * P, :])
        return t

    def gcn(self, h, weight, bias, out):
        c = self.c
        st = ExitStack()
        table = self.dram("gcn_table", [NP, D])
        ps = self.psum(st)
        with c.together():
            w = self.matrix(weight, st)
            b = self.row(bias, st)
        inner = ExitStack()
        own = self.sb("own", [P, NT, D], F32, st)
        ht = self.sb("ht", [P, NP], F32, inner)
        self.to_features(ps, h, ht)
        flat = ps[:].rearrange("p b n -> p (b n)")[:, 0:NP].rearrange("p (t w) -> p t w", w=D)

        def product(e):
            for t in range(NT):
                last = e.matmul(flat[:, t, :], ht[:, t * P:(t + 1) * P], w[:], start=True, stop=True)
            return last
        c.op("t", product)
        c.op("v", lambda e: e.tensor_tensor(own[:], flat, over_features(self.dinv[:], D), ALU.mult))
        with c.together():
            c.dma("s", node_rows(table), own[:])
            c.op("v", lambda e: e.memset(ps[:, RING - 1, :], 0.0))
            c.op("a", lambda e: e.copy(out, own[:]))
        c.run()
        inner.close()
        self.edge_sums(ps, table, D, out)
        c.op("v", lambda e: e.tensor_tensor(out, out, over_features(self.dinv[:], D), ALU.mult))
        c.op("v", lambda e: e.tensor_tensor(out, out, over_nodes(b[:]), ALU.add))
        c.run()
        st.close()

    def attend(self, ht, kdim, weight, att_src, att_dst, heads, per, finish):
        c, nc = self.c, self.nc
        st = ExitStack()
        hc = heads * per
        nx = 2 * heads + 1
        table = self.dram("gat_table", [NP, hc])
        h = self.sb("h", [P, NT, hc], F32, st)
        ext = self.sb("ext", [P, STEPS, nx], F32, st)
        es = self.sb("es", [P, NT, heads], F32, st)
        mid = ExitStack()
        ps = self.psum(mid)
        on_src = self.sb("on_src", [P, STEPS, heads], F32, mid)
        on_dst = self.sb("on_dst", [P, STEPS, 2 * heads], F32, mid)
        tabs = ExitStack()
        tab_src = self.sb("tab_src", [P, heads, NT], F32, tabs)
        tab_dst = self.sb("tab_dst", [P, STEPS, 2 * heads], F32, tabs)
        inner = ExitStack()
        with c.together():
            w = self.matrix(weight, inner)
            both = [self.row(a, inner, kdim) for a in (att_src, att_dst)]
        prod = self.sb("prod", [kdim, heads, per], F32, inner)
        wa = self.sb("wa", [kdim, 2, heads], F32, inner)
        node_a = self.sb("node_a", [P, NT, 2, heads], F32, inner)
        for n, a in enumerate(both):
            c.op("v", lambda e, a=a: e.tensor_tensor(prod[:].rearrange("p h c -> p (h c)"), w[:], a[:], ALU.mult))
            c.op("v", lambda e, n=n: e.tensor_reduce(wa[:, n, :], prod[:], AX.X, ALU.add))
        flat = ps[:].rearrange("p b n -> p (b n)")
        step = min(hc, P)
        for n in range(hc // step):
            def product(e, n=n):
                for t in range(NT):
                    last = e.matmul(flat[:, t * step:(t + 1) * step], ht[0:kdim, t * P:(t + 1) * P],
                                    w[:, n * step:(n + 1) * step], start=True, stop=True)
                return last
            c.op("t", product)
            c.op("v", lambda e, n=n: e.tensor_copy(h[:, :, n * step:(n + 1) * step],
                                                   flat[:, 0:NT * step].rearrange("p (t w) -> p t w", w=step)))

        def attention(e):
            for t in range(NT):
                last = e.matmul(ps[:, 7, t * 2 * heads:(t + 1) * 2 * heads], ht[0:kdim, t * P:(t + 1) * P],
                                wa[:].rearrange("p a h -> p (a h)"), start=True, stop=True)
            return last
        with c.together():
            c.op("t", attention)
            c.dma("s", node_rows(table), h[:])
        flat_a = node_a[:].rearrange("p t a h -> p (t a h)")
        c.op("v", lambda e: e.tensor_copy(flat_a, ps[:, 7, 0:NT * 2 * heads]))
        c.op("v", lambda e: e.tensor_tensor(es[:], node_a[:, :, 0, :], node_a[:, :, 1, :], ALU.add))
        c.op("v", lambda e: e.scalar_tensor_tensor(es[:], es[:], NEG, es[:], ALU.mult, ALU.max))
        c.op("v", lambda e: e.tensor_copy(tab_src[:].rearrange("p h t -> p t h"), node_a[:, :, 0, :]))
        hot_t = self.sb("hot_t", [NT, STEPS], F32, inner)
        cols_t = self.sb("cols_t", [NT, 2 * heads, P], F32, inner)

        def turn(e):
            for j in range(KJ):
                e.transpose(ps[0:NT, 6, KP * j:KP * (j + 1)], self.win_hot[:, j, :], self.ident[0:KP, 0:KP])
            for n in range(2 * heads):
                col = node_a[:, :, 1, n] if n < heads else es[:, :, n - heads]
                last = e.transpose(flat[0:NT, n * P:(n + 1) * P], col, self.ident[:])
            return last
        c.op("t", turn)
        with c.together():
            c.op("a", lambda e: e.copy(hot_t[:], ps[0:NT, 6, 0:STEPS]))
            c.op("v", lambda e: e.tensor_copy(cols_t[:].rearrange("p n q -> p (n q)"), flat[0:NT, 0:2 * heads * P]))
        for lo in range(0, 2 * heads, 8):
            hi = min(lo + 8, 2 * heads)

            def spread(e, lo=lo, hi=hi):
                for n in range(lo, hi):
                    last = e.matmul(ps[:, n - lo, 0:STEPS], cols_t[:, n, :], hot_t[:], start=True, stop=True)
                return last
            c.op("t", spread)
            c.op("v", lambda e, lo=lo, hi=hi: e.tensor_copy(tab_dst[:, :, lo:hi].rearrange("p k n -> p n k"),
                                                            ps[:, 0:hi - lo, 0:STEPS]))
        c.run()
        inner.close()
        self.by_edge(ps, tab_src, tab_dst, on_src, on_dst, heads)
        tabs.close()
        self.softmax(ps, on_src, on_dst, ext, heads)
        mid.close()
        tail = ExitStack()
        ps = self.psum(tail)
        acc = self.sb("acc", [P, NT, hc + nx], F32, tail)
        with c.together():
            c.op("v", lambda e: e.memset(acc[:], 0.0))
            c.op("v", lambda e: e.memset(ps[:, RING - 1, :], 0.0))
        c.run()
        if per == P:
            self.edge_sums(ps, table, hc, acc, heads=[ext[:, :, n] for n in range(heads)], extra=ext[:])
        else:
            self.edge_sums(ps, table, hc, acc, scaled=ext[:, :, 0:heads], extra=ext[:])
        own = self.sb("own", [P, NT, heads], F32, tail)
        none = self.sb("none", [P, NT], F32, tail)
        den = self.sb("den", [P, NT, heads], F32, tail)
        c.op("v", lambda e: e.tensor_scalar(none[:], acc[:, :, hc + 2 * heads], -1.0, 1.0, ALU.mult, ALU.add))
        c.op("v", lambda e: e.tensor_tensor(own[:], acc[:, :, hc + heads:hc + 2 * heads],
                                            over_features(none[:], heads), ALU.add))
        c.op("v", lambda e: e.tensor_tensor(den[:], own[:], acc[:, :, hc:hc + heads], ALU.add))
        c.op("v", lambda e: e.reciprocal(den[:], den[:]))
        by_head = lambda t: t.rearrange("p t (h c) -> p t h c", h=heads)
        wide = lambda t: t.unsqueeze(3).to_broadcast([P, NT, heads, per])
        hh = by_head(h[:])
        c.op("v", lambda e: e.tensor_tensor(hh, hh, wide(own[:]), ALU.mult))
        c.op("v", lambda e: e.tensor_tensor(hh, hh, by_head(acc[:, :, 0:hc]), ALU.add))
        c.op("v", lambda e: e.tensor_tensor(hh, hh, wide(den[:]), ALU.mult))
        c.run()
        tail.close()
        finish(hh)
        st.close()

    def by_edge(self, ps, tab_src, tab_dst, on_src, on_dst, heads):
        nc = self.nc
        st = ExitStack()
        per_bank = 10 if heads <= 2 else 2
        sub = 2 * per_bank
        iters = STEPS // (2 * sub)
        w = heads * NT
        rows = self.sb("rows", [P, 2, 2, sub * P], BF16, st)
        hot = self.sb("hot", [P, 2, 2, sub * P], F32, st)
        win = self.sb("win", [P, 2, sub, NT], F32, st)
        kept = self.sb("kept", [P, 2, sub, heads, NT], F32, st)
        names = ("rows0", "rows1", "hots", "products", "taken_v", "taken_a", "own")
        landed0, landed1, hots, products, taken_v, taken_a, own = (nc.alloc_semaphore(self.name(n)) for n in names)
        landed = (landed0, landed1)
        with nc.Block() as block:
            @block.sync
            def _(e):
                with e.Fori(0, iters) as i:
                    for b in range(2):
                        e.wait_ge(hots, i * 2 + b + 1)
                        for n in range(2):
                            cut = self.row_scratch[n, bass.ds((i * 2 + b) * (sub * P), sub * P)]
                            e.dma_start(rows[:, b, n, :], cut.partition_broadcast(P)).then_inc(landed[b], 16)

            @block.vector
            def _(e):
                e.sem_inc(hots, 2)
                e.sem_inc(own, 1)

                def take(i, b, n):
                    k = n * sub
                    e.wait_ge(products, n + 3)
                    for bank in range(2):
                        part = slice(bank * per_bank, (bank + 1) * per_bank)
                        inst = e.tensor_tensor(kept[:, b, part, :, :],
                                        ps[:, 3 * b + bank, 0:per_bank * w].rearrange("p (s h t) -> p s h t", h=heads, t=NT),
                                        win[:, b, part, :].unsqueeze(2).to_broadcast([P, per_bank, heads, NT]), ALU.mult)
                    inst.then_inc(taken_v, 1)
                    e.wait_ge(taken_v, n + 3)
                    e.tensor_reduce(on_src[:, bass.ds(k, sub), :].rearrange("p s h -> p (s h)"),
                                    kept[:, b, :, :, :].rearrange("p s h t -> p (s h) t"), AX.X, ALU.add).then_inc(own, 1)

                def make(i, b, n):
                    k = n * sub
                    e.wait_ge(landed[b], i * 32 + 32)
                    e.wait_ge(products, n + 1)
                    for m in range(2):
                        inst = e.tensor_scalar(hot[:, b, m, :], rows[:, b, m, :], self.pidx[:, 0:1], None, ALU.is_equal)
                    e.wait_ge(taken_v, n + 1)
                    inst = e.tensor_tensor(win[:, b, :, :], self.iota_nt[:].unsqueeze(1).to_broadcast([P, sub, NT]),
                                           over_features(self.src_win[:, bass.ds(k, sub)], NT), ALU.is_equal)
                    inst.then_inc(hots, 1)

                e.sem_inc(taken_v, 2)
                with e.Fori(0, iters) as i:
                    for b in range(2):
                        make(i, b, i * 2 + b)
                    for b in range(2):
                        e.wait_ge(own, i * 2 + b + 1)
                        e.wait_ge(hots, i * 2 + b + 3)
                        take(i, b, i * 2 + b)

            @block.tensor
            def _(e):
                e.sem_inc(products, 2)
                with e.Fori(0, iters) as i:
                    for b in range(2):
                        n = i * 2 + b
                        k = n * sub
                        e.wait_ge(hots, n + 3)
                        e.wait_ge(taken_v, n + 1)
                        e.wait_ge(taken_a, n + 1)
                        for s in range(sub):
                            e.matmul(ps[:, 3 * b + s // per_bank, (s % per_bank) * w:(s % per_bank + 1) * w],
                                     hot[:, b, 0, s * P:(s + 1) * P], tab_src[:].rearrange("p h t -> p (h t)"),
                                     start=True, stop=True)
                            mm = e.matmul(ps[:, 3 * b + 2, s * 2 * heads:(s + 1) * 2 * heads],
                                          hot[:, b, 1, s * P:(s + 1) * P],
                                          tab_dst[:, bass.ds(k + s, 1), :].rearrange("p a n -> p (a n)"),
                                          start=True, stop=True)
                        mm.then_inc(products, 1)

            @block.scalar
            def _(e):
                e.sem_inc(taken_a, 2)
                with e.Fori(0, iters) as i:
                    for b in range(2):
                        n = i * 2 + b
                        e.wait_ge(products, n + 3)
                        e.copy(on_dst[:, bass.ds(n * sub, sub), :].rearrange("p s n -> p (s n)"),
                               ps[:, 3 * b + 2, 0:sub * 2 * heads]).then_inc(taken_a, 1)
        st.close()

    def softmax(self, ps, on_src, on_dst, ext, heads):
        c = self.c
        st = ExitStack()
        jh = KJ * heads
        logit = on_src
        floor = self.sb("floor", [P, STEPS], F32, st)
        rows = self.sb("rows", [KP, jh, P], F32, st)
        fwd = self.sb("fwd", [KP, jh, P], F32, st)
        bwd = self.sb("bwd", [KP, jh, P], F32, st)
        ends = self.sb("ends", [8, 2, STEPS], F32, st)
        carry = self.sb("carry", [8, 2, STEPS + 1], F32, st)
        carried = self.sb("carried", [KP, 2, jh], F32, st)
        most = self.sb("most", [P, STEPS, heads], F32, st)
        by_head = lambda t: t.unsqueeze(2).to_broadcast([P, STEPS, heads])
        c.op("v", lambda e: e.tensor_tensor(logit[:], on_src[:], on_dst[:, :, 0:heads], ALU.add))
        with c.together():
            c.op("v", lambda e: e.tensor_scalar(floor[:], self.valid[:], -1.0, BIG, ALU.add, ALU.mult))
            c.op("p", lambda e: e.memset(carry[:], -BIG))
        c.op("v", lambda e: e.scalar_tensor_tensor(logit[:], logit[:], NEG, logit[:], ALU.mult, ALU.max))
        c.op("v", lambda e: e.tensor_tensor(logit[:], logit[:], by_head(self.valid[:]), ALU.mult))
        c.op("v", lambda e: e.tensor_tensor(logit[:], logit[:], by_head(floor[:]), ALU.add))
        flat = ps[:].rearrange("p b n -> p (b n)")

        def turn(e):
            for j in range(KJ):
                for n in range(heads):
                    m = j * heads + n
                    last = e.transpose(flat[0:KP, m * P:(m + 1) * P], logit[:, KP * j:KP * (j + 1), n], self.ident[:])
            return last
        c.op("t", turn)
        c.op("v", lambda e: e.tensor_copy(rows[:].rearrange("p m q -> p (m q)"), flat[0:KP, 0:jh * P]))

        def scan(initial):
            with c.together():
                for m in range(jh):
                    j = m // heads
                    c.op("v", lambda e, m=m, j=j: e.tensor_tensor_scan(
                        fwd[:, m, :], self.cut_start[:, j, :], rows[:, m, :], initial(0, m), ALU.add, ALU.max))
                    c.op("v", lambda e, m=m, j=j: e.tensor_tensor_scan(
                        bwd[:, m, ::-1], self.cut_last[:, j, ::-1], rows[:, m, ::-1], initial(1, m), ALU.add, ALU.max))
        scan(lambda way, m: -BIG)

        def turn_ends(e):
            for way, (t, at) in enumerate(((fwd, P - 1), (bwd, 0))):
                for j in range(KJ):
                    last = e.transpose(ps[0:heads, way, KP * j:KP * (j + 1)],
                                       t[:, j * heads:(j + 1) * heads, at], self.ident[0:KP, 0:KP])
            return last
        c.op("t", turn_ends)
        c.op("v", lambda e: e.tensor_copy(ends[0:heads, :, :], ps[0:heads, 0:2, 0:STEPS]))
        with c.together():
            c.op("v", lambda e: e.tensor_tensor_scan(carry[0:heads, 0, 1:STEPS + 1], self.rows_start[0:heads, :],
                                                     ends[0:heads, 0, :], -BIG, ALU.add, ALU.max))
            c.op("v", lambda e: e.tensor_tensor_scan(carry[0:heads, 1, 0:STEPS][:, ::-1],
                                                     self.rows_last[0:heads, ::-1], ends[0:heads, 1, ::-1],
                                                     -BIG, ALU.add, ALU.max))

        def turn_back(e):
            for way in range(2):
                for j in range(KJ):
                    m = way * jh + j * heads
                    last = e.transpose(ps[0:KP, 0, m:m + heads],
                                       carry[0:heads, way, KP * j + way:KP * (j + 1) + way],
                                       self.ident[0:heads, 0:heads])
            return last
        c.op("t", turn_back)
        c.op("v", lambda e: e.tensor_copy(carried[:].rearrange("p w m -> p (w m)"), ps[0:KP, 0, 0:2 * jh]))
        scan(lambda way, m: carried[:, way, m:m + 1])
        c.op("v", lambda e: e.tensor_tensor(fwd[:], fwd[:], bwd[:], ALU.max))

        def back(e):
            for m in range(jh):
                last = e.transpose(flat[:, m * P:m * P + KP], fwd[:, m, :], self.ident[0:KP, 0:KP])
            return last
        c.op("t", back)
        own = on_dst[:, :, heads:2 * heads]
        most_v = most[:].rearrange("q (j p) h -> q j h p", j=KJ)
        c.op("v", lambda e: e.tensor_copy(most_v, flat[:, 0:jh * P].rearrange("q (j h p) -> q j h p", j=KJ, h=heads)[:, :, :, 0:KP]))
        c.op("v", lambda e: e.tensor_tensor(most[:], most[:], own, ALU.max))
        with c.together():
            c.op("v", lambda e: e.tensor_tensor(logit[:], logit[:], most[:], ALU.subtract))
            c.op("v", lambda e: e.tensor_tensor(own, own, most[:], ALU.subtract))
        with c.together():
            c.op("a", lambda e: e.activation(ext[:, :, 0:heads], logit[:], ACT.Exp))
            c.op("a", lambda e: e.activation(own, own, ACT.Exp))
            c.op("v", lambda e: e.tensor_copy(ext[:, :, 2 * heads], self.last[:]))
        c.op("v", lambda e: e.tensor_tensor(ext[:, :, heads:2 * heads], own, by_head(self.last[:]), ALU.mult))
        c.run()
        st.close()

    def batch_norm_relu(self, h, gamma, beta):
        c = self.c
        st = ExitStack()
        ps = self.psum(st)
        sq = self.sb("sq", [P, NT, D], F32, st)
        mean, scale = self.sb("bn_mean", [P, D], F32, st), self.sb("bn_scale", [P, D], F32, st)
        with c.together():
            g, b = self.row(gamma, st), self.row(beta, st)

        def total(bank, t0):
            def build(e):
                for t in range(NT):
                    last = e.matmul(ps[:, bank, 0:D], (self.live if t == NT - 1 else self.ones)[:], t0[:, t, :],
                                    start=t == 0, stop=t == NT - 1)
                return last
            c.op("t", build)
        total(0, h)
        c.op("v", lambda e: e.tensor_scalar(mean[:], ps[:, 0, 0:D], 1.0 / N, None, ALU.mult))
        c.op("v", lambda e: e.tensor_tensor(h[:], h[:], over_nodes(mean[:]), ALU.subtract))
        c.op("a", lambda e: e.activation(sq[:], h[:], ACT.Square))
        total(1, sq)
        c.op("v", lambda e: e.tensor_scalar(scale[:], ps[:, 1, 0:D], 1.0 / N, EPS, ALU.mult, ALU.add))
        c.op("v", lambda e: e.reciprocal(scale[:], scale[:]))
        c.op("a", lambda e: e.sqrt(scale[:], scale[:]))
        c.op("v", lambda e: e.tensor_tensor(scale[:], scale[:], g[:], ALU.mult))
        c.op("v", lambda e: e.tensor_tensor(h[:], h[:], over_nodes(scale[:]), ALU.mult))
        c.op("v", lambda e: e.tensor_tensor(h[:], h[:], over_nodes(b[:]), ALU.add))
        c.op("a", lambda e: e.activation(h[:], h[:], ACT.Relu))
        c.run()
        st.close()

    def add_to_x(self, h):
        self.c.op("v", lambda e: e.tensor_tensor(self.x[:], self.x[:], h, ALU.add))

    def gcn_layer(self):
        st = ExitStack()
        h, out = self.sb("h0", [P, NT, D], F32, st), self.sb("out0", [P, NT, D], F32, st)
        self.layer_norm(self.x[:], h[:])
        self.gcn(h, "L0_gnn_W", "L0_gnn_b", out[:])
        self.batch_norm_relu(out, "L0_gnn_gamma", "L0_gnn_beta")
        self.add_to_x(h[:])
        self.add_to_x(out[:])
        self.c.run()
        st.close()

    def gcn_gat_layer(self):
        c = self.c
        st = ExitStack()
        with c.together():
            g, b, bias = (self.row("L1_gnn_" + n, st) for n in ("ln_gamma", "ln_beta", "gat_b"))
        ht = self.sb("ht1", [P, NP], F32, st)
        inner = ExitStack()
        h, out = self.sb("h1", [P, NT, D], F32, inner), self.sb("out1", [P, NT, D], F32, inner)
        self.layer_norm(self.x[:], h[:])
        self.gcn(h, "L1_gnn_gcn_w", "L1_gnn_gcn_b", out[:])
        self.layer_norm(out[:], out[:], g[:], b[:])
        turn = ExitStack()
        self.to_features(self.psum(turn), out, ht)
        c.run()
        turn.close()
        inner.close()

        def finish(heads):
            last = ExitStack()
            y = self.sb("y1", [P, NT, D], F32, last)
            c.op("v", lambda e: e.tensor_tensor(y[:], heads[:, :, 0, :], heads[:, :, 1, :], ALU.add))
            c.op("v", lambda e: e.tensor_scalar(y[:], y[:], 0.5, None, ALU.mult))
            c.op("v", lambda e: e.tensor_tensor(y[:], y[:], over_nodes(bias[:]), ALU.add))
            self.layer_norm(y[:], y[:], g[:], b[:])
            self.add_to_x(y[:])
            c.run()
            last.close()
        self.attend(ht, P, "L1_gnn_gat_w", "L1_gnn_att_src", "L1_gnn_att_dst", 2, D, finish)
        st.close()

    def gated_layer(self):
        nc, c = self.nc, self.c
        st = ExitStack()
        state = self.sb("state", [P, 2, NP], F32, st)
        x1t = self.sb("x1t", [P, NP], F32, st)
        table = self.dram("state_table", [NP, S2])
        first = ExitStack()
        h = self.sb("h2", [P, NT, D], F32, first)
        self.layer_norm(self.x[:], h[:])
        self.to_features(self.psum(first), h, x1t)
        with c.together():
            c.op("v", lambda e: e.memset(state[:, 1, :], 0.0))
            c.op("a", lambda e: e.copy(state[:, 0, :], x1t[:]))
        with c.together():
            c.dma("s", node_rows(table[:, 0:D]), h[:])
            c.dma("s", node_rows(table[:, D:S2]), state[:, 1, :].rearrange("p (t w) -> p t w", w=D))
        c.run()
        first.close()

        loop = ExitStack()
        with c.together():
            wih, whh = self.matrix("L2_gnn_w_ih", loop), self.matrix("L2_gnn_w_hh", loop)
            bih, bhh = self.columns("L2_gnn_b_ih", loop), self.columns("L2_gnn_b_hh", loop)
        brz = self.sb("brz", [P, 6], F32, loop)
        c.op("v", lambda e: e.tensor_tensor(brz[:], bih[:], bhh[:], ALU.add))
        c.run()
        ps = self.psum(loop)
        acc = self.sb("sums", [P, 2, NP], F32, loop)
        wl = self.sb("wl", [P, 2, S2], F32, loop)
        fold = self.sb("fold", [P, 2, 3 * S2], F32, loop)
        stage = self.sb("stage", [P, NT, S2], F32, loop)
        sums_sems = self.edge_sems()
        gate_sems = [nc.alloc_semaphore(n) for n in ("gates_pe", "gates_act", "gates_dve")]
        lc = Chain(nc, "layer")
        with nc.Fori(0, LAYERS) as layer:
            lc.counts = (0, 0, 0)
            w_layer = self.ins["L2_gnn_W"]
            with lc.together():
                for j in range(2):
                    lc.dma("s", wl[:, j, :], w_layer[bass.ds(layer, 1), j * P:(j + 1) * P, :].rearrange("a p w -> p (a w)"))
                lc.op("v", lambda e: e.memset(acc[:], 0.0))
                lc.op("v", lambda e: e.memset(ps[:, RING - 1, :], 0.0))

            def folded(e):
                for m in range(2):
                    for half in range(2):
                        for j in range(2):
                            last = e.matmul(ps[:, 4 + 2 * m + half, 0:384], wl[:, j, m * P:(m + 1) * P],
                                            wih[:, j, half * 384:(half + 1) * 384], start=j == 0, stop=j == 1)
                return last
            lc.op("t", folded)
            lc.op("v", lambda e: e.tensor_copy(fold[:].rearrange("p m (f w) -> p (m f) w", f=2), ps[:, 4:8, 0:384]))
            lc.run()
            self.edge_sums(ps, table, S2, acc, turned=True, sems=sums_sems, before=layer)
            self.gates(ps, acc, state, fold, whh, brz, bih, bhh, gate_sems)
            flat = ps[:].rearrange("p b n -> p (b n)")
            for f in range(2):
                def turn(e, f=f):
                    for t in range(NT):
                        last = e.transpose(flat[:, t * P:(t + 1) * P], state[:, f, t * P:(t + 1) * P], self.ident[:])
                    return last
                lc.op("t", turn)
                tiles = flat[:, 0:NP].rearrange("p (t w) -> p t w", w=P)
                with lc.together():
                    lc.op("v", lambda e, f=f: e.tensor_copy(stage[:, 0:12, f * P:(f + 1) * P], tiles[:, 0:12, :]))
                    lc.op("a", lambda e, f=f: e.copy(stage[:, 12:NT, f * P:(f + 1) * P], tiles[:, 12:NT, :]))
            lc.dma("s", node_rows(table), stage[:])
            lc.run()
            with nc.Block() as block:
                @block.sync
                def _(e):
                    for s in (lc.done, lc.landed, *sums_sems[:5], *gate_sems):
                        e.sem_clear(s)
        loop.close()

        mlp = ExitStack()
        with c.together():
            l0, l1 = self.matrix("L2_gnn_l0_w", mlp), self.matrix("L2_gnn_l1_w", mlp)
            b0, b1 = self.columns("L2_gnn_l0_b", mlp), self.columns("L2_gnn_l1_b", mlp)
        ps = self.psum(mlp)
        y1 = self.sb("y1", [P, 2, NP], F32, mlp)
        y2 = self.sb("y2", [P, NP], F32, mlp)

        def dense(w, m, sources, out, bias):
            def build(e):
                for q in range(NCH):
                    for j, src in enumerate(sources):
                        last = e.matmul(ps[:, q, 0:CH], w[:, j, m * P:(m + 1) * P], src[:, q * CH:(q + 1) * CH],
                                        start=j == 0, stop=j == len(sources) - 1)
                return last
            c.op("t", build)
            c.op("a", lambda e: e.activation(out.rearrange("p (q n) -> p q n", n=CH), ps[:, :, 0:CH], ACT.Relu, bias=bias))
        for m in range(2):
            dense(l0, m, (state[:, 0, :], state[:, 1, :], x1t[:]), y1[:, m, :], b0[:, m:m + 1])
        dense(l1, 0, (y1[:, 0, :], y1[:, 1, :]), y2[:], b1[:, 0:1])
        flat = ps[:].rearrange("p b n -> p (b n)")

        def back(e):
            for t in range(NT):
                last = e.transpose(flat[:, t * P:(t + 1) * P], y2[:, t * P:(t + 1) * P], self.ident[:])
            return last
        c.op("t", back)
        self.add_to_x(flat[:, 0:NP].rearrange("p (t w) -> p t w", w=D))
        c.run()
        mlp.close()
        st.close()

    def gates(self, ps, sums, state, fold, whh, brz, bih, bhh, sems):
        nc = self.nc
        st = ExitStack()
        r, z, t, n, d = (self.sb(w, [P, 2, CH], F32, st) for w in ("r", "z", "t", "n", "d"))
        made, act, dve = sems
        V = 10
        A = 6
        with nc.Block() as block:
            @block.tensor
            def _(e):
                e.sem_inc(dve, V)
                with e.Fori(0, NCH) as i:
                    cut = bass.ds(i * CH, CH)
                    for f in range(2):
                        e.wait_ge(dve, i * V + 2 * (f + 1))
                        for gate in range(3):
                            at = slice(gate * S2 + f * P, gate * S2 + (f + 1) * P)
                            pairs = [(whh, state, 0), (whh, state, 1), (fold, sums, 0), (fold, sums, 1)]
                            for bank, group in (((gate, pairs),) if gate < 2 else ((2, pairs[:2]), (3, pairs[2:]))):
                                for q, (w, src, j) in enumerate(group):
                                    mm = e.matmul(ps[:, 4 * f + bank, 0:CH], w[:, j, at], src[:, j, cut],
                                                  start=q == 0, stop=q == len(group) - 1)
                        mm.then_inc(made, 1)

            @block.scalar
            def _(e):
                with e.Fori(0, NCH) as i:
                    for f in range(2):
                        e.wait_ge(made, i * 2 + f + 1)
                        e.wait_ge(dve, i * V + 6 + 2 * f)
                        e.activation(r[:, f, :], ps[:, 4 * f, 0:CH], ACT.Sigmoid, bias=brz[:, f:f + 1]).then_inc(act, 1)
                        e.activation(z[:, f, :], ps[:, 4 * f + 1, 0:CH], ACT.Sigmoid,
                                     bias=brz[:, 2 + f:3 + f]).then_inc(act, 1)
                    for f in range(2):
                        e.wait_ge(dve, i * V + V + 2 * (f + 1))
                        e.activation(n[:, f, :], t[:, f, :], ACT.Tanh, bias=bih[:, 4 + f:5 + f]).then_inc(act, 1)

            @block.vector
            def _(e):
                with e.Fori(0, NCH) as i:
                    cut = bass.ds(i * CH, CH)
                    done = i * V + V
                    for f in range(2):
                        e.wait_ge(act, i * A + 2 * (f + 1))
                        e.scalar_tensor_tensor(t[:, f, :], ps[:, 4 * f + 2, 0:CH], bhh[:, 4 + f:5 + f], r[:, f, :],
                                               ALU.add, ALU.mult).then_inc(dve, 1)
                        e.wait_ge(dve, done + 2 * f + 1)
                        e.tensor_tensor(t[:, f, :], t[:, f, :], ps[:, 4 * f + 3, 0:CH], ALU.add).then_inc(dve, 1)
                    for f in range(2):
                        e.wait_ge(act, i * A + 5 + f)
                        e.tensor_tensor(d[:, f, :], state[:, f, cut], n[:, f, :], ALU.subtract).then_inc(dve, 1)
                        e.wait_ge(dve, done + 5 + 2 * f)
                        e.tensor_tensor(d[:, f, :], d[:, f, :], z[:, f, :], ALU.mult).then_inc(dve, 1)
                    for f in range(2):
                        e.wait_ge(dve, done + 6 + 2 * f)
                        e.tensor_tensor(state[:, f, cut], n[:, f, :], d[:, f, :], ALU.add).then_inc(dve, 1)
        st.close()

    def gat_gat_layer(self):
        c = self.c
        st = ExitStack()
        with c.together():
            b1, b2 = self.row("L3_gnn_b1", st), self.row("L3_gnn_b2", st)
        g = self.sb("g3", [P, NT, 64], F32, st)
        ht = self.sb("ht3", [P, NP], F32, st)
        inner = ExitStack()
        h = self.sb("h3", [P, NT, D], F32, inner)
        first = self.sb("first3", [P, NP], F32, inner)
        with c.together():
            wm, bm = self.matrix("L3_gnn_W_map", inner), self.columns("L3_gnn_b_map", inner)
        self.layer_norm(self.x[:], h[:])
        ps = self.psum(inner)
        self.to_features(ps, h, first)

        def mapped(e):
            for q in range(NCH):
                last = e.matmul(ps[:, q, 0:CH], wm[:], first[:, q * CH:(q + 1) * CH], start=True, stop=True)
            return last
        c.op("t", mapped)
        c.op("a", lambda e: e.activation(ht[:].rearrange("p (q n) -> p q n", n=CH), ps[:, :, 0:CH],
                                         ACT.Identity, bias=bm[:, 0:1]))
        c.run()
        inner.close()

        def elu(heads):
            last = ExitStack()
            low = self.sb("low", [P, NT, 64], F32, last)
            v = heads.rearrange("p t h c -> p t (h c)")
            c.op("v", lambda e: e.tensor_tensor(g[:], v, over_nodes(b1[:]), ALU.add))
            c.op("v", lambda e: e.tensor_scalar(low[:], g[:], 0.0, None, ALU.min))
            c.op("a", lambda e: e.activation(low[:], low[:], ACT.Exp))
            c.op("v", lambda e: e.tensor_scalar(g[:], g[:], 0.0, -1.0, ALU.max, ALU.add))
            c.op("v", lambda e: e.tensor_tensor(g[:], g[:], low[:], ALU.add))
            c.run()
            last.close()
        self.attend(ht, P, "L3_gnn_W1", "L3_gnn_att_src1", "L3_gnn_att_dst1", 8, 8, elu)
        turn = ExitStack()
        self.to_features(self.psum(turn), g, ht, 64)
        c.run()
        turn.close()

        def finish(heads):
            v = heads.rearrange("p t h c -> p t (h c)")
            c.op("v", lambda e: e.tensor_tensor(v, v, over_nodes(b2[:]), ALU.add))
            self.add_to_x(v)
            c.run()
        self.attend(ht, 64, "L3_gnn_W2", "L3_gnn_att_src2", "L3_gnn_att_dst2", 1, D, finish)
        st.close()

    def store(self):
        c = self.c
        with c.together():
            c.dma("s", node_rows(self.out[0:(NT - 1) * P, :]), self.x[:, 0:NT - 1, :])
            c.dma("a", self.out[(NT - 1) * P:N, :], self.x[0:LAST, NT - 1, :])
        c.run()


def build(nc, ins, out):
    k = Kernel(nc, ins, out)
    with k.stack:
        k.constants()
        k.graph()
        k.degrees()
        k.gcn_layer()
        k.gcn_gat_layer()
        k.gated_layer()
        k.gat_gat_layer()
        k.store()


_TURNED = ("L2_gnn_W", "L2_gnn_w_ih", "L2_gnn_w_hh", "L2_gnn_l0_w", "L2_gnn_l1_w")


def kernel(**inputs):
    import concourse.bacc as _bacc
    from concourse.bass_utils import run_bass_kernel_spmd as _run

    nc = _bacc.Bacc("TRN2", target_bir_lowering=False, num_devices=1)
    arrays, ins = {}, {}
    for name, value in inputs.items():
        a = np.asarray(value)
        a = np.ascontiguousarray(a.swapaxes(-1, -2) if name in _TURNED else a)
        arrays[name] = a
        ins[name] = nc.dram_tensor(name, a.shape, mybir.dt.from_np(a.dtype), kind="ExternalInput").ap()
    out = nc.dram_tensor("out", (N, D), F32, kind="ExternalOutput").ap()
    build(nc, ins, out)
    r = _run(nc, [arrays], core_ids=[0])
    return r.results[0]["out"]
```

```python
from contextlib import ExitStack

import numpy as np

import concourse.bass as bass
from concourse import mybir

F32 = mybir.dt.float32
BF16 = mybir.dt.bfloat16
I32 = mybir.dt.int32
ALU = mybir.AluOpType
ACT = mybir.ActivationFunctionType
AX = mybir.AxisListType

P = 128
N = 3125
E = 53125
D = 128
NT = -(-N // P)
NP = NT * P
LAST = N - (NT - 1) * P
ET = -(-E // P)
EPR = 512
ER = ET * P // EPR
ETR = EPR // P
STEPS = ET + NT - 1
KJ = 4
KP = STEPS // KJ
BODY = 20
GRP = 5
NG = BODY // GRP
ITERS = STEPS // BODY
AHEAD = STEPS + BODY
RING = 4
BIG = 1e30
NEG = 0.2
EPS = 1e-5
S2 = 256
LAYERS = 5
CH = 400
NCH = NP // CH
TQ = 100
assert ER * EPR == ET * P and KP * KJ == STEPS and ITERS * BODY == STEPS and NCH * CH == NP


class Chain:

    def __init__(self, nc, name):
        self.nc, self.name = nc, name
        self.done = nc.alloc_semaphore(name + "_done")
        self.landed = nc.alloc_semaphore(name + "_landed")
        self.fetched = nc.alloc_semaphore(name + "_fetched")
        self.counts = (0, 0, 0)
        self.queues = {k: [] for k in "ptvas"}
        self.floor = None

    def together(self):
        return _Together(self)

    def _queue(self, engine, build, kind):
        self.queues[engine].append((self.floor or self.counts, build, kind))
        self.counts = tuple(n + (0 if k != kind else 16 if k else 1) for k, n in enumerate(self.counts))

    def op(self, engine, build):
        self._queue(engine, build, 0)

    def dma(self, engine, out, in_):
        self._queue(engine, lambda e: e.dma_start(out, in_), 1)

    def gather(self, out, table, index):
        self._queue("p", lambda e: e.indirect_dma_start(
            out=out, out_offset=None, in_=table,
            in_offset=bass.IndirectOffsetOnAxis(ap=index, axis=0)), 2)

    def run(self):
        sems = (self.done, self.landed, self.fetched)
        queues, self.queues = self.queues, {k: [] for k in "ptvas"}

        def wait(e, need, seen):
            for sem, n, was in zip(sems, need, seen):
                if n > was:
                    e.wait_ge(sem, n)
            return tuple(map(max, need, seen))

        def emit(e, queue):
            seen = (0, 0, 0)
            for need, build, kind in queue:
                seen = wait(e, need, seen)
                build(e).then_inc(sems[kind], 16 if kind else 1)

        with self.nc.Block() as block:
            @block.gpsimd
            def _(e):
                emit(e, queues["p"])

            @block.tensor
            def _(e):
                emit(e, queues["t"])

            @block.vector
            def _(e):
                emit(e, queues["v"])

            @block.scalar
            def _(e):
                emit(e, queues["a"])

            @block.sync
            def _(e):
                emit(e, queues["s"])
                wait(e, self.counts, (0, 0, 0))


class _Together:
    def __init__(self, chain):
        self.chain = chain

    def __enter__(self):
        self.chain.floor = self.chain.counts

    def __exit__(self, *_):
        self.chain.floor = None


def node_rows(dram):
    return dram.rearrange("(t p) w -> p t w", p=P)


def over_nodes(ap, nt=NT):
    return ap.unsqueeze(1).to_broadcast([ap.shape[0], nt, ap.shape[1]])


def over_features(ap, w):
    return ap.unsqueeze(2).to_broadcast([ap.shape[0], ap.shape[1], w])


class Kernel:
    def __init__(self, nc, ins, out):
        self.nc, self.ins, self.out = nc, ins, out
        self.stack = ExitStack()
        self.count = 0

    def name(self, what):
        self.count += 1
        return f"{what}_{self.count}"

    def sb(self, what, shape, dt=F32, stack=None):
        return (stack or self.stack).enter_context(self.nc.sbuf_tensor(self.name(what), shape, dt))

    def dram(self, what, shape, dt=F32):
        return self.nc.dram_tensor(self.name(what), shape, dt, kind="Internal").ap()

    def psum(self, stack, shape=(P, 8, 512)):
        return stack.enter_context(self.nc.psum_tensor(self.name("psum"), list(shape), F32))

    def constants(self):
        sb = self.sb
        self.ident = sb("ident", [P, P])
        self.iota = sb("iota", [P, P])
        self.iota_nt = sb("iota_nt", [P, NT])
        self.pidx = sb("pidx", [P, 1])
        self.ones = sb("ones", [P, P])
        self.live = sb("live", [P, P])
        self.src_idx = sb("src_idx", [P, AHEAD], I32)
        self.place = sb("place", [P, AHEAD])
        self.window = sb("window", [1, STEPS + 4], I32)
        self.src_win = sb("src_win", [P, STEPS])
        self.valid = sb("valid", [P, STEPS])
        self.last = sb("last", [P, STEPS])
        self.cut_start = sb("cut_start", [KP, KJ, P])
        self.cut_last = sb("cut_last", [KP, KJ, P])
        self.rows_start = sb("rows_start", [8, STEPS])
        self.rows_last = sb("rows_last", [8, STEPS])
        self.win_hot = sb("win_hot", [KP, KJ, NT])
        self.dinv = sb("dinv", [P, NT])
        self.x = sb("x", [P, NT, D])
        self.row_scratch = self.dram("row_scratch", [2, STEPS * P], BF16)
        self.edge_scratch = self.dram("edge_scratch", [ET, 4 * P])
        c = self.c = Chain(self.nc, "c")
        with c.together():
            c.op("p", lambda e: e.memset(self.ident[:], 0.0))
            c.op("p", lambda e: e.iota(self.iota[:], [[1, P]], base=0, channel_multiplier=0,
                                       allow_small_or_imprecise_dtypes=True))
            c.op("p", lambda e: e.iota(self.iota_nt[:], [[1, NT]], base=0, channel_multiplier=0,
                                       allow_small_or_imprecise_dtypes=True))
            c.op("p", lambda e: e.iota(self.pidx[:], [[1, 1]], base=0, channel_multiplier=1,
                                       allow_small_or_imprecise_dtypes=True))
            c.op("v", lambda e: e.memset(self.ones[:], 1.0))
            c.op("v", lambda e: e.memset(self.live[:], 0.0))
            c.op("v", lambda e: e.memset(self.window[:], 0))
            c.op("v", lambda e: e.memset(self.src_idx[:], 0))
            c.op("v", lambda e: e.memset(self.place[:], 0.0))
            c.op("v", lambda e: e.memset(self.x[:, NT - 1, :], 0.0))
        with c.together():
            c.op("p", lambda e: e.affine_select(out=self.ident[:], in_=self.ident[:], compare_op=ALU.not_equal,
                                                fill=1.0, base=0, pattern=[[-1, P]], channel_multiplier=1))
            c.op("v", lambda e: e.memset(self.live[0:LAST, :], 1.0))
            x = self.ins["x"]
            c.dma("s", self.x[:, 0:NT - 1, :], node_rows(x[0:(NT - 1) * P, :]))
            c.dma("s", self.x[0:LAST, NT - 1, :], x[(NT - 1) * P:N, :])

    def graph(self):
        c = self.c
        st = ExitStack()
        sb = lambda *a: self.sb(*a, stack=st)
        src, dst = self.ins["src"], self.ins["dst"]
        whole, rest = E // EPR, E % EPR
        si, di, pi, ni = (sb(w, [ER, EPR], I32) for w in ("src_i", "dst_i", "prev_i", "next_i"))
        pack = sb("pack", [ER, ETR, 4, P])
        first = sb("first", [ER, ETR], I32)
        first_f = sb("first_f", [ER, ETR])
        tile_no = sb("tile_no", [ER, ETR])
        some = sb("some", [ER, ETR])
        step_row = sb("step_row", [P, STEPS])
        reached = sb("reached", [ER, ETR, STEPS])
        tile_c = sb("tile_c", [KP, KJ])
        tile_i = sb("tile_i", [KP, KJ], I32)
        step_c = sb("step_c", [KP, KJ])
        win_c = sb("win_c", [KP, KJ])
        win128 = sb("win128", [KP, KJ])
        win_r = sb("win_r", [1, STEPS])
        rows = sb("rows", [KP, KJ, 4 * P])
        place_r = sb("place_r", [KP, KJ, P])
        valid_r = sb("valid_r", [KP, KJ, P])
        start_r = sb("start_r", [KP, KJ, P])
        last_r = sb("last_r", [KP, KJ, P])
        src_ri = sb("src_ri", [KP, KJ, P], I32)
        low_i = sb("low_i", [KP, KJ, P], I32)
        high_i = sb("high_i", [KP, KJ, P], I32)
        low_f = sb("low_f", [KP, KJ, P])
        high_f = sb("high_f", [KP, KJ, P])
        bf = sb("bf", [KP, 2, KJ, P], BF16)
        any_f = sb("any_f", [KP, 2, KJ])
        any8 = sb("any8", [KP, 2, KJ, 8])
        ps = self.psum(st)

        with c.together():
            for t, fill in ((si, 0), (di, NP), (pi, -1), (ni, -1)):
                c.op("v", lambda e, t=t, fill=fill: e.memset(t[:], fill))
            c.op("p", lambda e: e.iota(tile_no[:], [[1, ETR]], base=0, channel_multiplier=ETR,
                                       allow_small_or_imprecise_dtypes=True))
            c.op("p", lambda e: e.iota(step_row[:], [[1, STEPS]], base=0, channel_multiplier=0,
                                       allow_small_or_imprecise_dtypes=True))
            c.op("p", lambda e: e.iota(step_c[:], [[KP, KJ]], base=0, channel_multiplier=1,
                                       allow_small_or_imprecise_dtypes=True))
        one = lambda ap: ap.rearrange("(a b) -> a b", a=1)
        many = lambda ap: ap.rearrange("(a b) -> a b", b=EPR)
        with c.together():
            for t, a in ((si, src), (di, dst)):
                c.dma("s", t[0:whole, :], many(a[0:whole * EPR]))
                c.dma("a", t[whole:whole + 1, 0:rest], one(a[whole * EPR:E]))
            c.dma("s", pi[0:1, 1:EPR], one(dst[0:EPR - 1]))
            c.dma("s", pi[1:whole, :], many(dst[EPR - 1:whole * EPR - 1]))
            c.dma("a", pi[whole:whole + 1, 0:rest + 1], one(dst[whole * EPR - 1:E]))
            c.dma("s", ni[0:whole, :], many(dst[1:whole * EPR + 1]))
            c.dma("a", ni[whole:whole + 1, 0:rest - 1], one(dst[whole * EPR + 1:E]))
        row = lambda t: t[:].rearrange("p (g q) -> p g q", g=ETR)
        with c.together():
            c.op("v", lambda e: e.tensor_copy(pack[:, :, 0, :], row(si)))
            c.op("v", lambda e: e.tensor_copy(pack[:, :, 1, :], row(di)))
            c.op("v", lambda e: e.tensor_tensor(pack[:, :, 2, :], row(di), row(pi), ALU.not_equal))
            c.op("v", lambda e: e.tensor_tensor(pack[:, :, 3, :], row(di), row(ni), ALU.not_equal))
            c.op("v", lambda e: e.tensor_scalar(first[:], di[:, 0:EPR:P], 7, None, ALU.arith_shift_right))
            c.op("v", lambda e: e.tensor_scalar(some[:], tile_no[:], 1.0, None, ALU.min))
        c.dma("s", self.edge_scratch.rearrange("(p g) w -> p (g w)", g=ETR),
              pack[:].rearrange("p g c q -> p (g c q)"))
        c.op("v", lambda e: e.tensor_copy(first_f[:], first[:]))
        c.op("v", lambda e: e.tensor_tensor(first_f[:], first_f[:], tile_no[:], ALU.add))
        c.op("v", lambda e: e.tensor_tensor(first_f[:], first_f[:], some[:], ALU.mult))
        with c.together():
            for g in range(ETR):
                c.op("v", lambda e, g=g: e.tensor_scalar(reached[:, g, :], step_row[0:ER, :],
                                                         first_f[:, g:g + 1], None, ALU.is_ge))

        def count(e):
            for g in range(ETR):
                e.matmul(ps[0:1, 0, 0:STEPS], self.ones[0:ER, 0:1], reached[:, g, :],
                         start=g == 0, stop=g == ETR - 1)
            for j in range(KJ):
                for g in range(ETR):
                    last = e.matmul(ps[0:KP, 1, j:j + 1], reached[:, g, KP * j:KP * (j + 1)],
                                    self.ones[0:ER, 0:1], start=g == 0, stop=g == ETR - 1)
            return last
        c.op("t", count)
        with c.together():
            c.op("v", lambda e: e.tensor_scalar(tile_c[:], ps[0:KP, 1, 0:KJ], -1.0, None, ALU.add))
            c.op("v", lambda e: e.scalar_tensor_tensor(win_r[:], ps[0:1, 0, 0:STEPS], -1.0, step_row[0:1, :],
                                                       ALU.mult, ALU.add))
        with c.together():
            c.op("v", lambda e: e.tensor_copy(tile_i[:], tile_c[:]))
            c.op("v", lambda e: e.tensor_tensor(win_c[:], step_c[:], tile_c[:], ALU.subtract))
            c.op("v", lambda e: e.tensor_scalar(self.window[:, 1:STEPS + 1], win_r[:], 1.0, None, ALU.add))
        c.op("v", lambda e: e.tensor_scalar(win128[:], win_c[:], float(P), None, ALU.mult))
        with c.together():
            for j in range(KJ):
                c.gather(rows[:, j, :], self.edge_scratch, tile_i[:, j:j + 1])
                c.op("v", lambda e, j=j: e.tensor_scalar(self.win_hot[:, j, :], self.iota_nt[0:KP, :],
                                                         win_c[:, j:j + 1], None, ALU.is_equal))
        part = lambda n: rows[:, :, n * P:(n + 1) * P]
        with c.together():
            for j in range(KJ):
                c.op("v", lambda e, j=j: e.tensor_scalar(place_r[:, j, :], rows[:, j, P:2 * P],
                                                         win128[:, j:j + 1], None, ALU.subtract))
            c.op("a", lambda e: e.copy(src_ri[:], part(0)))
        with c.together():
            c.op("v", lambda e: e.tensor_scalar(valid_r[:], place_r[:], 0.0, None, ALU.is_ge))
            c.op("v", lambda e: e.tensor_scalar(low_i[:], src_ri[:], P - 1, None, ALU.bitwise_and))
            c.op("v", lambda e: e.tensor_scalar(high_i[:], src_ri[:], 7, None, ALU.arith_shift_right))
            c.op("a", lambda e: e.copy(bf[:, 1, :, :], place_r[:]))
        with c.together():
            c.op("v", lambda e: e.scalar_tensor_tensor(valid_r[:], place_r[:], P - 1.0, valid_r[:],
                                                       ALU.is_le, ALU.mult))
            c.op("a", lambda e: e.copy(low_f[:], low_i[:]))
            c.op("a", lambda e: e.copy(bf[:, 0, :, :], low_i[:]))
            c.op("a", lambda e: e.copy(high_f[:], high_i[:]))
        with c.together():
            c.op("v", lambda e: e.tensor_tensor(start_r[:], part(2), valid_r[:], ALU.mult))
            c.op("v", lambda e: e.tensor_tensor(last_r[:], part(3), valid_r[:], ALU.mult))
            for n in range(2):
                c.dma("s", self.row_scratch[n, :].rearrange("(j p q) -> p j q", j=KJ, p=KP), bf[:, n, :, :])
        with c.together():
            c.op("v", lambda e: e.tensor_scalar(self.cut_start[:], start_r[:], -BIG, None, ALU.mult))
            c.op("v", lambda e: e.tensor_scalar(self.cut_last[:], last_r[:], -BIG, None, ALU.mult))
        with c.together():
            c.op("v", lambda e: e.tensor_reduce(any_f[:, 0, :], self.cut_start[:], AX.X, ALU.min))
            c.op("v", lambda e: e.tensor_reduce(any_f[:, 1, :], self.cut_last[:], AX.X, ALU.min))
        c.op("v", lambda e: e.tensor_copy(any8[:], any_f[:].unsqueeze(3).to_broadcast([KP, 2, KJ, 8])))

        turned = (part(0), place_r, high_f, valid_r, last_r)

        def turn(e):
            for n, t in enumerate(turned):
                for j in range(KJ):
                    e.transpose(ps[:, n, KP * j:KP * (j + 1)], t[:, j, :], self.ident[0:KP, 0:KP])
            for n in range(2):
                for j in range(KJ):
                    last = e.transpose(ps[0:8, 5 + n, KP * j:KP * (j + 1)], any8[:, n, j, :],
                                       self.ident[0:KP, 0:KP])
            return last
        c.op("t", turn)
        with c.together():
            for n, t in enumerate((self.src_idx, self.place, self.src_win, self.valid, self.last)):
                c.op("va"[n % 2], lambda e, n=n, t=t: (e.copy if n % 2 else e.tensor_copy)(t[:, 0:STEPS], ps[:, n, 0:STEPS]))
            c.op("v", lambda e: e.tensor_copy(self.rows_start[:], ps[0:8, 5, 0:STEPS]))
            c.op("v", lambda e: e.tensor_copy(self.rows_last[:], ps[0:8, 6, 0:STEPS]))
        c.run()
        st.close()

    def degrees(self):
        nc, c = self.nc, self.c
        st = ExitStack()
        hot = self.sb("deg_hot", [P, 2, BODY, P], BF16, st)
        one = self.sb("one_bf", [P, 1], BF16, st)
        by_step = self.sb("deg_step", [P, STEPS], F32, st)
        turned = self.sb("deg_turned", [KP, KJ, P], F32, st)
        ps = self.psum(st)
        hots, cols, kept = (nc.alloc_semaphore(n) for n in ("deg_hots", "deg_cols", "deg_kept"))
        with nc.Block() as block:
            @block.vector
            def _(e):
                e.memset(one[:], 1.0).then_inc(hots, 1)
                with e.Fori(0, ITERS // 2) as i:
                    for b in range(2):
                        e.wait_ge(cols, i * 2 + b + 1)
                        k = i * (2 * BODY) + b * BODY
                        e.tensor_tensor(hot[:, b, :, :], self.iota[:].unsqueeze(1).to_broadcast([P, BODY, P]),
                                        over_features(self.place[:, bass.ds(k, BODY)], P),
                                        ALU.is_equal).then_inc(hots, 1)

            @block.tensor
            def _(e):
                e.sem_inc(cols, 2)
                with e.Fori(0, ITERS // 2) as i:
                    for b in range(2):
                        e.wait_ge(hots, i * 2 + b + 2)
                        e.wait_ge(kept, i * 2 + b + 1)
                        for s in range(BODY):
                            mm = e.matmul(ps[:, b, s:s + 1], hot[:, b, s, :], one[:], start=True, stop=True)
                        mm.then_inc(cols, 1)

            @block.scalar
            def _(e):
                e.sem_inc(kept, 2)
                with e.Fori(0, ITERS // 2) as i:
                    for b in range(2):
                        e.wait_ge(cols, i * 2 + b + 3)
                        e.copy(by_step[:, bass.ds(i * (2 * BODY) + b * BODY, BODY)],
                               ps[:, b, 0:BODY]).then_inc(kept, 1)

        def turn(e):
            for j in range(KJ):
                last = e.transpose(ps[0:KP, 0, P * j:P * (j + 1)], by_step[:, KP * j:KP * (j + 1)], self.ident[:])
            return last
        c.op("t", turn)
        c.op("v", lambda e: e.tensor_copy(turned[:].rearrange("p j q -> p (j q)"), ps[0:KP, 0, :]))

        def total(e):
            for j in range(KJ):
                last = e.matmul(ps[:, 1, 0:NT], turned[:, j, :], self.win_hot[:, j, :],
                                start=j == 0, stop=j == KJ - 1)
            return last
        c.op("t", total)
        c.op("v", lambda e: e.tensor_scalar(self.dinv[:], ps[:, 1, 0:NT], 1.0, None, ALU.add))
        c.op("v", lambda e: e.reciprocal(self.dinv[:], self.dinv[:]))
        c.op("a", lambda e: e.sqrt(self.dinv[:], self.dinv[:]))
        c.run()
        st.close()

    def edge_sums(self, ps, table, width, acc, heads=0, extra=None, turned=False, sems=None, before=0):
        nc = self.nc
        st = ExitStack()
        nx = extra.shape[2] if extra is not None else 0
        cols = width + nx
        per = width // max(heads, 1)
        rows = self.sb("rows", [P, BODY, cols], F32, st)
        index = self.sb("index", [P, BODY], I32, st)
        place = self.sb("place_now", [P, BODY], F32, st)
        hot = self.sb("hot", [P, BODY, P], F32, st)
        by_act = heads and per == P
        if sems is None:
            sems = self.edge_sems()
        indexed, ready, summed, kept, scaled, started, *fetched = sems

        def landed(i):
            return before * (ITERS * 16 * GRP) + i * (16 * GRP) + 16 * GRP

        with nc.Block() as block:
            @block.gpsimd
            def _(e):
                with e.Fori(0, ITERS) as i:
                    for g in range(NG):
                        e.wait_ge(indexed, i * NG + g + 1)
                        e.sem_inc(started, 1)
                        for s in range(GRP * g, GRP * (g + 1)):
                            e.indirect_dma_start(
                                out=rows[:, s, 0:width], out_offset=None, in_=table,
                                in_offset=bass.IndirectOffsetOnAxis(ap=index[:, s:s + 1], axis=0)
                            ).then_inc(fetched[g], 16)

            @block.vector
            def _(e):
                regs = [e.alloc_register(self.name("window_reg")) for _ in range(GRP)]

                def bring(k, g):
                    part = slice(GRP * g, GRP * (g + 1))
                    e.tensor_copy(index[:, part], self.src_idx[:, k])
                    inst = e.tensor_copy(place[:, part], self.place[:, k])
                    if nx:
                        inst = e.tensor_copy(rows[:, part, width:cols], extra[:, k, :])
                    inst.then_inc(indexed, 1)

                def add(r, w, own):
                    e.wait_ge(kept, own)
                    if turned:
                        a = acc[:, :, bass.ds(w * P, P)]
                        b = ps[:, r, 0:width].rearrange("p (f n) -> p f n", n=P)
                    else:
                        a = acc[:].rearrange("p t w -> p (t w)")[:, bass.ds(w * cols, cols)]
                        b = ps[:, r, 0:cols]
                    e.tensor_tensor(a, a, b, ALU.add).then_inc(kept, 1)

                def compare(g):
                    part = slice(GRP * g, GRP * (g + 1))
                    e.tensor_tensor(hot[:, part, :], self.iota[:].unsqueeze(1).to_broadcast([P, GRP, P]),
                                    over_features(place[:, part], P), ALU.is_equal).then_inc(ready, 1)

                for g in range(NG):
                    bring(slice(GRP * g, GRP * (g + 1)), g)
                e.wait_ge(indexed, 1)
                compare(0)
                with e.Fori(0, ITERS) as i:
                    k = i * BODY
                    for g in range(NG):
                        s0 = GRP * g
                        e.load(regs, self.window[0:1, bass.ds(k + s0, GRP)])
                        w = [e.snap(r, min_val=0, max_val=NT - 1) for r in regs]
                        e.wait_ge(indexed, i * NG + g + 2)
                        e.wait_ge(summed, k + s0 + 2 * GRP)
                        compare((g + 1) % NG)
                        if heads and not by_act:
                            e.wait_ge(fetched[g], landed(i))
                            scale = rows[:, s0:s0 + GRP, 0:width].rearrange("p s (h c) -> p s h c", h=heads)
                            by = rows[:, s0:s0 + GRP, width:width + heads].unsqueeze(3)
                            e.tensor_tensor(scale, scale, by.to_broadcast([P, GRP, heads, per]),
                                            ALU.mult).then_inc(scaled, GRP)
                        for s in range(s0, s0 + GRP):
                            e.wait_ge(summed, k + s + BODY)
                            if s == s0 and g > 0:
                                e.wait_ge(ready, i * NG + g)
                                bring(bass.ds(k + BODY + s - GRP, GRP), g - 1)
                            add((s - 1) % RING, w[s - s0], k + s + RING)
                    e.wait_ge(summed, k + BODY + BODY)
                    e.wait_ge(ready, i * NG + NG)
                    bring(bass.ds(k + BODY + BODY - GRP, GRP), NG - 1)
                e.load(regs[:1], self.window[0:1, STEPS:STEPS + 1])
                w = e.snap(regs[0], min_val=0, max_val=NT - 1)
                add((STEPS - 1) % RING, w, STEPS + RING)
                e.wait_ge(kept, STEPS + RING + 1)
                e.wait_ge(indexed, (ITERS + 1) * NG)
                e.wait_ge(ready, ITERS * NG + 1)
                for r in regs:
                    e.free_register(r)

            @block.scalar
            def _(e):
                if by_act:
                    with e.Fori(0, ITERS) as i:
                        for g in range(NG):
                            e.wait_ge(indexed, i * NG + g + 1)
                            e.wait_ge(fetched[g], landed(i))
                            for s in range(GRP * g, GRP * (g + 1)):
                                for h in range(heads):
                                    own = rows[:, s, h * per:(h + 1) * per]
                                    inst = e.activation(own, own, ACT.Copy, scale=rows[:, s, width + h:width + h + 1])
                                inst.then_inc(scaled, 1)

            @block.tensor
            def _(e):
                e.sem_inc(summed, BODY)
                e.sem_inc(kept, RING)
                with e.Fori(0, ITERS) as i:
                    k = i * BODY
                    for s in range(BODY):
                        r = s % RING
                        if s % GRP == 0:
                            e.wait_ge(fetched[s // GRP], landed(i))
                            if nx:
                                e.wait_ge(indexed, i * NG + s // GRP + 1)
                            e.wait_ge(ready, i * NG + s // GRP + 1)
                        if heads:
                            e.wait_ge(scaled, k + s + 1)
                        e.wait_ge(kept, k + s + 2)
                        if turned:
                            for f in range(width // P):
                                mm = e.matmul(ps[:, r, f * P:(f + 1) * P], rows[:, s, f * P:(f + 1) * P], hot[:, s, :],
                                              start=True, stop=True)
                        else:
                            mm = e.matmul(ps[:, r, 0:cols], hot[:, s, :], rows[:, s, :], start=True, stop=True)
                        mm.then_inc(summed, 1)
        st.close()

    def edge_sems(self):
        self.count += 1
        names = ["indexed", "ready", "summed", "kept", "scaled", "started"] + [f"fetched{g}" for g in range(NG)]
        return [self.nc.alloc_semaphore(f"{n}_{self.count}") for n in names]

    def to_features(self, ps, h, ht, width=D):
        c = self.c
        flat = ps[:].rearrange("p b n -> p (b n)")

        def turn(e):
            for t in range(NT):
                last = e.transpose(flat[0:width, t * P:(t + 1) * P], h[:, t, :], self.ident[:])
            return last
        c.op("t", turn)
        half = 12 * P
        with c.together():
            c.op("v", lambda e: e.tensor_copy(ht[0:width, 0:half], flat[0:width, 0:half]))
            c.op("a", lambda e: e.copy(ht[0:width, half:NP], flat[0:width, half:NP]))

    def layer_norm(self, x, d, gamma=None, beta=None):
        c = self.c
        st = ExitStack()
        sq = self.sb("sq", [P, NT, D], F32, st)
        mean, var = self.sb("mean", [P, NT], F32, st), self.sb("var", [P, NT], F32, st)
        c.op("v", lambda e: e.tensor_reduce(mean[:], x, AX.X, ALU.add))
        c.op("v", lambda e: e.tensor_scalar(mean[:], mean[:], 1.0 / D, None, ALU.mult))
        c.op("v", lambda e: e.tensor_tensor(d, x, over_features(mean[:], D), ALU.subtract))
        c.op("a", lambda e: e.activation(sq[:], d, ACT.Square))
        c.op("v", lambda e: e.tensor_reduce(var[:], sq[:], AX.X, ALU.add))
        c.op("v", lambda e: e.tensor_scalar(var[:], var[:], 1.0 / D, EPS, ALU.mult, ALU.add))
        c.op("v", lambda e: e.reciprocal(var[:], var[:]))
        c.op("a", lambda e: e.sqrt(var[:], var[:]))
        if gamma is None:
            c.op("v", lambda e: e.scalar_tensor_tensor(d, d, 0.0, over_features(var[:], D), ALU.max, ALU.mult))
        else:
            c.op("v", lambda e: e.tensor_tensor(d, d, over_features(var[:], D), ALU.mult))
            c.op("v", lambda e: e.tensor_tensor(d, d, over_nodes(gamma), ALU.mult))
            c.op("v", lambda e: e.tensor_tensor(d, d, over_nodes(beta), ALU.add))
            c.op("a", lambda e: e.activation(d, d, ACT.Silu))
        c.run()
        st.close()

    def row(self, name, st, parts=P):
        v = self.ins[name]
        if len(v.shape) == 2:
            v = v.rearrange("h c -> (h c)")
        t = self.sb(name, [parts, v.shape[0]], F32, st)
        self.c.dma("s", t[:], v.partition_broadcast(parts))
        return t

    def columns(self, name, st):
        v = self.ins[name]
        t = self.sb(name, [P, v.shape[0] // P], F32, st)
        for j in range(v.shape[0] // P):
            self.c.dma("s", t[:, j:j + 1], v[j * P:(j + 1) * P].rearrange("(p a) -> p a", a=1))
        return t

    def matrix(self, name, st):
        v = self.ins[name]
        k, w = v.shape
        if k <= P:
            t = self.sb(name, [k, w], F32, st)
            self.c.dma("s", t[:], v)
        else:
            t = self.sb(name, [P, k // P, w], F32, st)
            for j in range(k // P):
                self.c.dma("s", t[:, j, :], v[j * P:(j + 1) * P, :])
        return t

    def gcn(self, h, weight, bias, out):
        c = self.c
        st = ExitStack()
        table = self.dram("gcn_table", [NP, D])
        ps = self.psum(st)
        with c.together():
            w = self.matrix(weight, st)
            b = self.row(bias, st)
        inner = ExitStack()
        own = self.sb("own", [P, NT, D], F32, st)
        ht = self.sb("ht", [P, NP], F32, inner)
        self.to_features(ps, h, ht)
        flat = ps[:].rearrange("p b n -> p (b n)")[:, 0:NP].rearrange("p (t w) -> p t w", w=D)

        def product(e):
            for t in range(NT):
                last = e.matmul(flat[:, t, :], ht[:, t * P:(t + 1) * P], w[:], start=True, stop=True)
            return last
        c.op("t", product)
        c.op("v", lambda e: e.tensor_tensor(own[:], flat, over_features(self.dinv[:], D), ALU.mult))
        with c.together():
            c.dma("s", node_rows(table), own[:])
            c.op("v", lambda e: e.memset(ps[:, RING - 1, :], 0.0))
            c.op("a", lambda e: e.copy(out, own[:]))
        c.run()
        inner.close()
        self.edge_sums(ps, table, D, out)
        c.op("v", lambda e: e.tensor_tensor(out, out, over_features(self.dinv[:], D), ALU.mult))
        c.op("v", lambda e: e.tensor_tensor(out, out, over_nodes(b[:]), ALU.add))
        c.run()
        st.close()

    def attend(self, ht, kdim, weight, att_src, att_dst, heads, per, finish):
        c, nc = self.c, self.nc
        st = ExitStack()
        hc = heads * per
        nx = 2 * heads + 1
        table = self.dram("gat_table", [NP, hc])
        h = self.sb("h", [P, NT, hc], F32, st)
        ext = self.sb("ext", [P, AHEAD, nx], F32, st)
        es = self.sb("es", [P, NT, heads], F32, st)
        mid = ExitStack()
        ps = self.psum(mid)
        on_src = self.sb("on_src", [P, STEPS, heads], F32, mid)
        on_dst = self.sb("on_dst", [P, STEPS, 2 * heads], F32, mid)
        tabs = ExitStack()
        tab_src = self.sb("tab_src", [P, 3, heads, NT], BF16, tabs)
        tab_dst = self.sb("tab_dst", [P, STEPS, 6 * heads], BF16, tabs)
        inner = ExitStack()
        with c.together():
            w = self.matrix(weight, inner)
            both = [self.row(a, inner, kdim) for a in (att_src, att_dst)]
        prod = self.sb("prod", [kdim, heads, per], F32, inner)
        wa = self.sb("wa", [kdim, 2, heads], F32, inner)
        node_a = self.sb("node_a", [P, NT, 2, heads], F32, inner)
        for n, a in enumerate(both):
            c.op("v", lambda e, a=a: e.tensor_tensor(prod[:].rearrange("p h c -> p (h c)"), w[:], a[:], ALU.mult))
            c.op("v", lambda e, n=n: e.tensor_reduce(wa[:, n, :], prod[:], AX.X, ALU.add))
        flat = ps[:].rearrange("p b n -> p (b n)")
        step = min(hc, P)
        for n in range(hc // step):
            def product(e, n=n):
                for t in range(NT):
                    last = e.matmul(flat[:, t * step:(t + 1) * step], ht[0:kdim, t * P:(t + 1) * P],
                                    w[:, n * step:(n + 1) * step], start=True, stop=True)
                return last
            c.op("t", product)
            c.op("v", lambda e, n=n: e.tensor_copy(h[:, :, n * step:(n + 1) * step],
                                                   flat[:, 0:NT * step].rearrange("p (t w) -> p t w", w=step)))

        def attention(e):
            for t in range(NT):
                last = e.matmul(ps[:, 7, t * 2 * heads:(t + 1) * 2 * heads], ht[0:kdim, t * P:(t + 1) * P],
                                wa[:].rearrange("p a h -> p (a h)"), start=True, stop=True)
            return last
        with c.together():
            c.op("t", attention)
            c.dma("s", node_rows(table), h[:])
        flat_a = node_a[:].rearrange("p t a h -> p (t a h)")
        c.op("v", lambda e: e.tensor_copy(flat_a, ps[:, 7, 0:NT * 2 * heads]))
        c.op("v", lambda e: e.tensor_tensor(es[:], node_a[:, :, 0, :], node_a[:, :, 1, :], ALU.add))
        c.op("v", lambda e: e.scalar_tensor_tensor(es[:], es[:], NEG, es[:], ALU.mult, ALU.max))
        self.split([tab_src[:, n, :, :].rearrange("p h t -> p t h") for n in range(3)], node_a[:, :, 0, :])
        hot_t = self.sb("hot_t", [NT, STEPS], BF16, inner)
        parts_t = self.sb("parts_t", [NT, 3, 2 * heads, P], BF16, inner)
        cols_t = self.sb("cols_t", [NT, 2 * heads, P], F32, inner)

        def turn(e):
            for j in range(KJ):
                e.transpose(ps[0:NT, 6, KP * j:KP * (j + 1)], self.win_hot[:, j, :], self.ident[0:KP, 0:KP])
            for n in range(2 * heads):
                col = node_a[:, :, 1, n] if n < heads else es[:, :, n - heads]
                last = e.transpose(flat[0:NT, n * P:(n + 1) * P], col, self.ident[:])
            return last
        c.op("t", turn)
        with c.together():
            c.op("a", lambda e: e.copy(hot_t[:], ps[0:NT, 6, 0:STEPS]))
            c.op("v", lambda e: e.tensor_copy(cols_t[:].rearrange("p n q -> p (n q)"), flat[0:NT, 0:2 * heads * P]))
        self.split([parts_t[:, n, :, :] for n in range(3)], cols_t[:])
        for lo in range(0, 6 * heads, 8):
            hi = min(lo + 8, 6 * heads)

            def spread(e, lo=lo, hi=hi):
                for n in range(lo, hi):
                    last = e.matmul(ps[:, n - lo, 0:STEPS], parts_t[:, n // (2 * heads), n % (2 * heads), :], hot_t[:],
                                    start=True, stop=True)
                return last
            c.op("t", spread)
            cut = (hi - lo) // 2
            with c.together():
                c.op("v", lambda e, lo=lo, cut=cut: e.tensor_copy(
                    tab_dst[:, :, lo:lo + cut].rearrange("p k n -> p n k"), ps[:, 0:cut, 0:STEPS]))
                c.op("a", lambda e, lo=lo, hi=hi, cut=cut: e.copy(
                    tab_dst[:, :, lo + cut:hi].rearrange("p k n -> p n k"), ps[:, cut:hi - lo, 0:STEPS]))
        c.run()
        inner.close()
        self.by_edge(ps, tab_src, tab_dst, on_src, on_dst, heads)
        tabs.close()
        self.softmax(ps, on_src, on_dst, ext, heads)
        mid.close()
        tail = ExitStack()
        ps = self.psum(tail)
        acc = self.sb("acc", [P, NT, hc + nx], F32, tail)
        with c.together():
            c.op("v", lambda e: e.memset(acc[:], 0.0))
            c.op("v", lambda e: e.memset(ps[:, RING - 1, :], 0.0))
            c.op("p", lambda e: e.memset(ext[:, STEPS:AHEAD, :], 0.0))
        c.run()
        self.edge_sums(ps, table, hc, acc, heads=heads, extra=ext[:])
        own = self.sb("own", [P, NT, heads], F32, tail)
        none = self.sb("none", [P, NT], F32, tail)
        den = self.sb("den", [P, NT, heads], F32, tail)
        c.op("v", lambda e: e.tensor_scalar(none[:], acc[:, :, hc + 2 * heads], -1.0, 1.0, ALU.mult, ALU.add))
        c.op("v", lambda e: e.tensor_tensor(own[:], acc[:, :, hc + heads:hc + 2 * heads],
                                            over_features(none[:], heads), ALU.add))
        c.op("v", lambda e: e.tensor_tensor(den[:], own[:], acc[:, :, hc:hc + heads], ALU.add))
        c.op("v", lambda e: e.reciprocal(den[:], den[:]))
        by_head = lambda t: t.rearrange("p t (h c) -> p t h c", h=heads)
        wide = lambda t: t.unsqueeze(3).to_broadcast([P, NT, heads, per])
        hh = by_head(h[:])
        c.op("v", lambda e: e.tensor_tensor(hh, hh, wide(own[:]), ALU.mult))
        c.op("v", lambda e: e.tensor_tensor(hh, hh, by_head(acc[:, :, 0:hc]), ALU.add))
        c.op("v", lambda e: e.tensor_tensor(hh, hh, wide(den[:]), ALU.mult))
        c.run()
        tail.close()
        finish(hh)
        st.close()

    def split(self, parts, t):
        c = self.c
        for n, part in enumerate(parts):
            c.op("v", lambda e, part=part: e.tensor_copy(part, t))
            if n < 2:
                c.op("v", lambda e, part=part: e.tensor_tensor(t, t, part, ALU.subtract))

    def by_edge(self, ps, tab_src, tab_dst, on_src, on_dst, heads):
        nc = self.nc
        st = ExitStack()
        per_bank = 10 if heads <= 2 else 2
        sub = 2 * per_bank
        iters = STEPS // (2 * sub)
        w = heads * NT
        rows = self.sb("rows", [P, 2, 2, sub * P], BF16, st)
        hot = self.sb("hot", [P, 2, 2, sub * P], BF16, st)
        win = self.sb("win", [P, 2, sub, NT], F32, st)
        kept = self.sb("kept", [P, sub, heads, NT], F32, st)
        step_tab = self.sb("step_tab", [P, 2, sub, 6 * heads], BF16, st)
        names = ("rows0", "rows1", "hots", "products", "taken_v", "taken_a", "own", "cut")
        landed0, landed1, hots, products, taken_v, taken_a, own, cut_out = (nc.alloc_semaphore(self.name(n)) for n in names)
        landed = (landed0, landed1)
        with nc.Block() as block:
            @block.sync
            def _(e):
                with e.Fori(0, iters) as i:
                    for b in range(2):
                        e.wait_ge(hots, i * 2 + b + 1)
                        for n in range(2):
                            cut = self.row_scratch[n, bass.ds((i * 2 + b) * (sub * P), sub * P)]
                            e.dma_start(rows[:, b, n, :], cut.partition_broadcast(P)).then_inc(landed[b], 16)

            @block.vector
            def _(e):
                def make(i, b):
                    n = i * 2 + b
                    e.wait_ge(landed[b], i * 32 + 32)
                    e.wait_ge(products, n + 1)
                    e.tensor_scalar(hot[:, b, :, :], rows[:, b, :, :], self.pidx[:, 0:1], None, ALU.is_equal)
                    e.wait_ge(taken_v, n + 1)
                    e.tensor_tensor(win[:, b, :, :], self.iota_nt[:].unsqueeze(1).to_broadcast([P, sub, NT]),
                                    over_features(self.src_win[:, bass.ds(n * sub, sub)], NT),
                                    ALU.is_equal).then_inc(hots, 1)

                def take(i, b):
                    n = i * 2 + b
                    e.wait_ge(own, n + 1)
                    e.wait_ge(hots, n + 3)
                    e.wait_ge(products, n + 3)
                    for bank in range(2):
                        part = slice(bank * per_bank, (bank + 1) * per_bank)
                        inst = e.tensor_tensor(kept[:, part, :, :],
                                               ps[:, 3 * b + bank, 0:per_bank * w].rearrange("p (s h t) -> p s h t", h=heads, t=NT),
                                               win[:, b, part, :].unsqueeze(2).to_broadcast([P, per_bank, heads, NT]), ALU.mult)
                    inst.then_inc(taken_v, 1)
                    e.wait_ge(taken_v, n + 3)
                    e.tensor_reduce(on_src[:, bass.ds(n * sub, sub), :].rearrange("p s h -> p (s h)"),
                                    kept[:].rearrange("p s h t -> p (s h) t"), AX.X, ALU.add).then_inc(own, 1)

                e.sem_inc(hots, 2)
                e.sem_inc(own, 1)
                e.sem_inc(taken_v, 2)
                make(0, 0)
                with e.Fori(0, iters - 1) as i:
                    make(i, 1)
                    take(i, 0)
                    make(i + 1, 0)
                    take(i, 1)
                make(iters - 1, 1)
                take(iters - 1, 0)
                take(iters - 1, 1)

            @block.tensor
            def _(e):
                e.sem_inc(products, 2)
                with e.Fori(0, iters) as i:
                    for b in range(2):
                        n = i * 2 + b
                        e.wait_ge(hots, n + 3)
                        e.wait_ge(taken_v, n + 1)
                        e.wait_ge(taken_a, n + 1)
                        e.wait_ge(cut_out, n + 1)
                        for s in range(sub):
                            for m in range(3):
                                e.matmul(ps[:, 3 * b + s // per_bank, (s % per_bank) * w:(s % per_bank + 1) * w],
                                         hot[:, b, 0, s * P:(s + 1) * P], tab_src[:, m, :, :].rearrange("p h t -> p (h t)"),
                                         start=m == 0, stop=m == 2)
                            for m in range(3):
                                mm = e.matmul(ps[:, 3 * b + 2, s * 2 * heads:(s + 1) * 2 * heads],
                                              hot[:, b, 1, s * P:(s + 1) * P],
                                              step_tab[:, b, s, m * 2 * heads:(m + 1) * 2 * heads],
                                              start=m == 0, stop=m == 2)
                        mm.then_inc(products, 1)

            @block.scalar
            def _(e):
                def cut(n, b):
                    e.copy(step_tab[:, b, :, :], tab_dst[:, bass.ds(n * sub, sub), :]).then_inc(cut_out, 1)

                def take(n, b):
                    e.wait_ge(products, n + 3)
                    e.copy(on_dst[:, bass.ds(n * sub, sub), :].rearrange("p s n -> p (s n)"),
                           ps[:, 3 * b + 2, 0:sub * 2 * heads]).then_inc(taken_a, 1)

                e.sem_inc(taken_a, 2)
                cut(0, 0)
                cut(1, 1)
                with e.Fori(0, iters - 1) as i:
                    for b in range(2):
                        take(i * 2 + b, b)
                        cut(i * 2 + b + 2, b)
                for b in range(2):
                    take(iters * 2 - 2 + b, b)
        st.close()

    def softmax(self, ps, on_src, on_dst, ext, heads):
        c = self.c
        st = ExitStack()
        jh = KJ * heads
        logit = on_src
        floor = self.sb("floor", [P, STEPS], F32, st)
        rows = self.sb("rows", [KP, jh, P], F32, st)
        fwd = self.sb("fwd", [KP, jh, P], F32, st)
        bwd = self.sb("bwd", [KP, jh, P], F32, st)
        ends = self.sb("ends", [8, 2, STEPS], F32, st)
        carry = self.sb("carry", [8, 2, STEPS + 1], F32, st)
        carried = self.sb("carried", [KP, 2, jh], F32, st)
        most = self.sb("most", [P, STEPS, heads], F32, st)
        by_head = lambda t: t.unsqueeze(2).to_broadcast([P, STEPS, heads])
        c.op("v", lambda e: e.tensor_tensor(logit[:], on_src[:], on_dst[:, :, 0:heads], ALU.add))
        with c.together():
            c.op("v", lambda e: e.tensor_scalar(floor[:], self.valid[:], -1.0, BIG, ALU.add, ALU.mult))
            c.op("p", lambda e: e.memset(carry[:], -BIG))
        c.op("v", lambda e: e.scalar_tensor_tensor(logit[:], logit[:], NEG, logit[:], ALU.mult, ALU.max))
        c.op("v", lambda e: e.tensor_tensor(logit[:], logit[:], by_head(self.valid[:]), ALU.mult))
        c.op("v", lambda e: e.tensor_tensor(logit[:], logit[:], by_head(floor[:]), ALU.add))
        flat = ps[:].rearrange("p b n -> p (b n)")

        def turn(e):
            for j in range(KJ):
                for n in range(heads):
                    m = j * heads + n
                    last = e.transpose(flat[0:KP, m * P:(m + 1) * P], logit[:, KP * j:KP * (j + 1), n], self.ident[:])
            return last
        c.op("t", turn)
        c.op("v", lambda e: e.tensor_copy(rows[:].rearrange("p m q -> p (m q)"), flat[0:KP, 0:jh * P]))

        def scan(initial):
            with c.together():
                for m in range(jh):
                    j = m // heads
                    c.op("v", lambda e, m=m, j=j: e.tensor_tensor_scan(
                        fwd[:, m, :], self.cut_start[:, j, :], rows[:, m, :], initial(0, m), ALU.add, ALU.max))
                    c.op("v", lambda e, m=m, j=j: e.tensor_tensor_scan(
                        bwd[:, m, ::-1], self.cut_last[:, j, ::-1], rows[:, m, ::-1], initial(1, m), ALU.add, ALU.max))
        scan(lambda way, m: -BIG)

        def turn_ends(e):
            for way, (t, at) in enumerate(((fwd, P - 1), (bwd, 0))):
                for j in range(KJ):
                    last = e.transpose(ps[0:heads, way, KP * j:KP * (j + 1)],
                                       t[:, j * heads:(j + 1) * heads, at], self.ident[0:KP, 0:KP])
            return last
        c.op("t", turn_ends)
        c.op("v", lambda e: e.tensor_copy(ends[0:heads, :, :], ps[0:heads, 0:2, 0:STEPS]))
        with c.together():
            c.op("v", lambda e: e.tensor_tensor_scan(carry[0:heads, 0, 1:STEPS + 1], self.rows_start[0:heads, :],
                                                     ends[0:heads, 0, :], -BIG, ALU.add, ALU.max))
            c.op("v", lambda e: e.tensor_tensor_scan(carry[0:heads, 1, 0:STEPS][:, ::-1],
                                                     self.rows_last[0:heads, ::-1], ends[0:heads, 1, ::-1],
                                                     -BIG, ALU.add, ALU.max))

        def turn_back(e):
            for way in range(2):
                for j in range(KJ):
                    m = way * jh + j * heads
                    last = e.transpose(ps[0:KP, 0, m:m + heads],
                                       carry[0:heads, way, KP * j + way:KP * (j + 1) + way],
                                       self.ident[0:heads, 0:heads])
            return last
        c.op("t", turn_back)
        c.op("v", lambda e: e.tensor_copy(carried[:].rearrange("p w m -> p (w m)"), ps[0:KP, 0, 0:2 * jh]))
        scan(lambda way, m: carried[:, way, m:m + 1])
        c.op("v", lambda e: e.tensor_tensor(fwd[:], fwd[:], bwd[:], ALU.max))

        def back(e):
            for m in range(jh):
                last = e.transpose(flat[:, m * P:m * P + KP], fwd[:, m, :], self.ident[0:KP, 0:KP])
            return last
        c.op("t", back)
        own = on_dst[:, :, heads:2 * heads]
        most_v = most[:].rearrange("q (j p) h -> q j h p", j=KJ)
        c.op("v", lambda e: e.tensor_copy(most_v, flat[:, 0:jh * P].rearrange("q (j h p) -> q j h p", j=KJ, h=heads)[:, :, :, 0:KP]))
        c.op("v", lambda e: e.tensor_tensor(most[:], most[:], own, ALU.max))
        with c.together():
            c.op("v", lambda e: e.tensor_tensor(logit[:], logit[:], most[:], ALU.subtract))
            c.op("v", lambda e: e.tensor_tensor(own, own, most[:], ALU.subtract))
        with c.together():
            c.op("a", lambda e: e.activation(ext[:, 0:STEPS, 0:heads], logit[:], ACT.Exp))
            c.op("a", lambda e: e.activation(own, own, ACT.Exp))
            c.op("v", lambda e: e.tensor_copy(ext[:, 0:STEPS, 2 * heads], self.last[:]))
        c.op("v", lambda e: e.tensor_tensor(ext[:, 0:STEPS, heads:2 * heads], own, by_head(self.last[:]), ALU.mult))
        c.run()
        st.close()

    def batch_norm_relu(self, h, gamma, beta):
        c = self.c
        st = ExitStack()
        ps = self.psum(st)
        sq = self.sb("sq", [P, NT, D], F32, st)
        mean, scale = self.sb("bn_mean", [P, D], F32, st), self.sb("bn_scale", [P, D], F32, st)
        with c.together():
            g, b = self.row(gamma, st), self.row(beta, st)

        def total(bank, t0):
            def build(e):
                for t in range(NT):
                    last = e.matmul(ps[:, bank, 0:D], (self.live if t == NT - 1 else self.ones)[:], t0[:, t, :],
                                    start=t == 0, stop=t == NT - 1)
                return last
            c.op("t", build)
        total(0, h)
        c.op("v", lambda e: e.tensor_scalar(mean[:], ps[:, 0, 0:D], 1.0 / N, None, ALU.mult))
        c.op("v", lambda e: e.tensor_tensor(h[:], h[:], over_nodes(mean[:]), ALU.subtract))
        c.op("a", lambda e: e.activation(sq[:], h[:], ACT.Square))
        total(1, sq)
        c.op("v", lambda e: e.tensor_scalar(scale[:], ps[:, 1, 0:D], 1.0 / N, EPS, ALU.mult, ALU.add))
        c.op("v", lambda e: e.reciprocal(scale[:], scale[:]))
        c.op("a", lambda e: e.sqrt(scale[:], scale[:]))
        c.op("v", lambda e: e.tensor_tensor(scale[:], scale[:], g[:], ALU.mult))
        c.op("v", lambda e: e.tensor_tensor(h[:], h[:], over_nodes(scale[:]), ALU.mult))
        c.op("v", lambda e: e.tensor_tensor(h[:], h[:], over_nodes(b[:]), ALU.add))
        c.op("a", lambda e: e.activation(h[:], h[:], ACT.Relu))
        c.run()
        st.close()

    def add_to_x(self, h):
        self.c.op("v", lambda e: e.tensor_tensor(self.x[:], self.x[:], h, ALU.add))

    def gcn_layer(self):
        st = ExitStack()
        h, out = self.sb("h0", [P, NT, D], F32, st), self.sb("out0", [P, NT, D], F32, st)
        self.layer_norm(self.x[:], h[:])
        self.gcn(h, "L0_gnn_W", "L0_gnn_b", out[:])
        self.batch_norm_relu(out, "L0_gnn_gamma", "L0_gnn_beta")
        self.add_to_x(h[:])
        self.add_to_x(out[:])
        self.c.run()
        st.close()

    def gcn_gat_layer(self):
        c = self.c
        st = ExitStack()
        with c.together():
            g, b, bias = (self.row("L1_gnn_" + n, st) for n in ("ln_gamma", "ln_beta", "gat_b"))
        ht = self.sb("ht1", [P, NP], F32, st)
        inner = ExitStack()
        h, out = self.sb("h1", [P, NT, D], F32, inner), self.sb("out1", [P, NT, D], F32, inner)
        self.layer_norm(self.x[:], h[:])
        self.gcn(h, "L1_gnn_gcn_w", "L1_gnn_gcn_b", out[:])
        self.layer_norm(out[:], out[:], g[:], b[:])
        turn = ExitStack()
        self.to_features(self.psum(turn), out, ht)
        c.run()
        turn.close()
        inner.close()

        def finish(heads):
            last = ExitStack()
            y = self.sb("y1", [P, NT, D], F32, last)
            c.op("v", lambda e: e.tensor_tensor(y[:], heads[:, :, 0, :], heads[:, :, 1, :], ALU.add))
            c.op("v", lambda e: e.tensor_scalar(y[:], y[:], 0.5, None, ALU.mult))
            c.op("v", lambda e: e.tensor_tensor(y[:], y[:], over_nodes(bias[:]), ALU.add))
            self.layer_norm(y[:], y[:], g[:], b[:])
            self.add_to_x(y[:])
            c.run()
            last.close()
        self.attend(ht, P, "L1_gnn_gat_w", "L1_gnn_att_src", "L1_gnn_att_dst", 2, D, finish)
        st.close()

    def gated_layer(self):
        nc, c = self.nc, self.c
        st = ExitStack()
        state = self.sb("state", [P, 2, NP], F32, st)
        x1t = self.sb("x1t", [P, NP], F32, st)
        table = self.dram("state_table", [NP, S2])
        first = ExitStack()
        h = self.sb("h2", [P, NT, D], F32, first)
        self.layer_norm(self.x[:], h[:])
        self.to_features(self.psum(first), h, x1t)
        with c.together():
            c.op("v", lambda e: e.memset(state[:, 1, :], 0.0))
            c.op("a", lambda e: e.copy(state[:, 0, :], x1t[:]))
        with c.together():
            c.dma("s", node_rows(table[:, 0:D]), h[:])
            c.dma("s", node_rows(table[:, D:S2]), state[:, 1, :].rearrange("p (t w) -> p t w", w=D))
        c.run()
        first.close()

        loop = ExitStack()
        with c.together():
            wih, whh = self.matrix("L2_gnn_w_ih", loop), self.matrix("L2_gnn_w_hh", loop)
            bih, bhh = self.columns("L2_gnn_b_ih", loop), self.columns("L2_gnn_b_hh", loop)
        brz = self.sb("brz", [P, 6], F32, loop)
        c.op("v", lambda e: e.tensor_tensor(brz[:], bih[:], bhh[:], ALU.add))
        c.run()
        ps = self.psum(loop)
        acc = self.sb("sums", [P, 2, NP], F32, loop)
        wl = self.sb("wl", [P, 2, S2], F32, loop)
        fold = self.sb("fold", [P, 2, 3 * S2], F32, loop)
        stage = self.sb("stage", [P, NT, S2], F32, loop)
        sums_sems = self.edge_sems()
        gate_sems = [nc.alloc_semaphore(n) for n in ("gates_pe", "gates_act", "gates_dve")]
        lc = Chain(nc, "layer")
        with nc.Fori(0, LAYERS) as layer:
            lc.counts = (0, 0, 0)
            w_layer = self.ins["L2_gnn_W"]
            with lc.together():
                for j in range(2):
                    lc.dma("s", wl[:, j, :], w_layer[bass.ds(layer, 1), j * P:(j + 1) * P, :].rearrange("a p w -> p (a w)"))
                lc.op("v", lambda e: e.memset(acc[:], 0.0))
                lc.op("v", lambda e: e.memset(ps[:, RING - 1, :], 0.0))

            def folded(e):
                for m in range(2):
                    for half in range(2):
                        for j in range(2):
                            last = e.matmul(ps[:, 4 + 2 * m + half, 0:384], wl[:, j, m * P:(m + 1) * P],
                                            wih[:, j, half * 384:(half + 1) * 384], start=j == 0, stop=j == 1)
                return last
            lc.op("t", folded)
            lc.op("v", lambda e: e.tensor_copy(fold[:].rearrange("p m (f w) -> p (m f) w", f=2), ps[:, 4:8, 0:384]))
            lc.run()
            self.edge_sums(ps, table, S2, acc, turned=True, sems=sums_sems, before=layer)
            self.gates(ps, acc, state, fold, whh, brz, bih, bhh, gate_sems)
            flat = ps[:].rearrange("p b n -> p (b n)")
            for f in range(2):
                def turn(e, f=f):
                    for t in range(NT):
                        last = e.transpose(flat[:, t * P:(t + 1) * P], state[:, f, t * P:(t + 1) * P], self.ident[:])
                    return last
                lc.op("t", turn)
                tiles = flat[:, 0:NP].rearrange("p (t w) -> p t w", w=P)
                with lc.together():
                    lc.op("v", lambda e, f=f: e.tensor_copy(stage[:, 0:12, f * P:(f + 1) * P], tiles[:, 0:12, :]))
                    lc.op("a", lambda e, f=f: e.copy(stage[:, 12:NT, f * P:(f + 1) * P], tiles[:, 12:NT, :]))
            lc.dma("s", node_rows(table), stage[:])
            lc.run()
            with nc.Block() as block:
                @block.sync
                def _(e):
                    for s in (lc.done, lc.landed, *sums_sems[:6], *gate_sems):
                        e.sem_clear(s)
        loop.close()

        mlp = ExitStack()
        with c.together():
            l0, l1 = self.matrix("L2_gnn_l0_w", mlp), self.matrix("L2_gnn_l1_w", mlp)
            b0, b1 = self.columns("L2_gnn_l0_b", mlp), self.columns("L2_gnn_l1_b", mlp)
        ps = self.psum(mlp)
        y1 = self.sb("y1", [P, 2, NP], F32, mlp)
        y2 = self.sb("y2", [P, NP], F32, mlp)

        def dense(w, m, sources, out, bias):
            def build(e):
                for q in range(NCH):
                    for j, src in enumerate(sources):
                        last = e.matmul(ps[:, q, 0:CH], w[:, j, m * P:(m + 1) * P], src[:, q * CH:(q + 1) * CH],
                                        start=j == 0, stop=j == len(sources) - 1)
                return last
            c.op("t", build)
            c.op("a", lambda e: e.activation(out.rearrange("p (q n) -> p q n", n=CH), ps[:, :, 0:CH], ACT.Relu, bias=bias))
        for m in range(2):
            dense(l0, m, (state[:, 0, :], state[:, 1, :], x1t[:]), y1[:, m, :], b0[:, m:m + 1])
        dense(l1, 0, (y1[:, 0, :], y1[:, 1, :]), y2[:], b1[:, 0:1])
        flat = ps[:].rearrange("p b n -> p (b n)")

        def back(e):
            for t in range(NT):
                last = e.transpose(flat[:, t * P:(t + 1) * P], y2[:, t * P:(t + 1) * P], self.ident[:])
            return last
        c.op("t", back)
        self.add_to_x(flat[:, 0:NP].rearrange("p (t w) -> p t w", w=D))
        c.run()
        mlp.close()
        st.close()

    def gates(self, ps, sums, state, fold, whh, brz, bih, bhh, sems):
        nc = self.nc
        st = ExitStack()
        r, z, t, n, d = (self.sb(w, [P, 2, CH], F32, st) for w in ("r", "z", "t", "n", "d"))
        made, act, dve = sems
        V = 10
        A = 6
        with nc.Block() as block:
            @block.tensor
            def _(e):
                e.sem_inc(dve, V)
                with e.Fori(0, NCH) as i:
                    cut = bass.ds(i * CH, CH)
                    for f in range(2):
                        e.wait_ge(dve, i * V + 2 * (f + 1))
                        for gate in range(3):
                            at = slice(gate * S2 + f * P, gate * S2 + (f + 1) * P)
                            pairs = [(whh, state, 0), (whh, state, 1), (fold, sums, 0), (fold, sums, 1)]
                            for bank, group in (((gate, pairs),) if gate < 2 else ((2, pairs[:2]), (3, pairs[2:]))):
                                for q, (w, src, j) in enumerate(group):
                                    mm = e.matmul(ps[:, 4 * f + bank, 0:CH], w[:, j, at], src[:, j, cut],
                                                  start=q == 0, stop=q == len(group) - 1)
                        mm.then_inc(made, 1)

            @block.scalar
            def _(e):
                with e.Fori(0, NCH) as i:
                    for f in range(2):
                        e.wait_ge(made, i * 2 + f + 1)
                        e.wait_ge(dve, i * V + 6 + 2 * f)
                        e.activation(r[:, f, :], ps[:, 4 * f, 0:CH], ACT.Sigmoid, bias=brz[:, f:f + 1]).then_inc(act, 1)
                        e.activation(z[:, f, :], ps[:, 4 * f + 1, 0:CH], ACT.Sigmoid,
                                     bias=brz[:, 2 + f:3 + f]).then_inc(act, 1)
                    for f in range(2):
                        e.wait_ge(dve, i * V + V + 2 * (f + 1))
                        e.activation(n[:, f, :], t[:, f, :], ACT.Tanh, bias=bih[:, 4 + f:5 + f]).then_inc(act, 1)

            @block.vector
            def _(e):
                with e.Fori(0, NCH) as i:
                    cut = bass.ds(i * CH, CH)
                    done = i * V + V
                    for f in range(2):
                        e.wait_ge(act, i * A + 2 * (f + 1))
                        e.scalar_tensor_tensor(t[:, f, :], ps[:, 4 * f + 2, 0:CH], bhh[:, 4 + f:5 + f], r[:, f, :],
                                               ALU.add, ALU.mult).then_inc(dve, 1)
                        e.wait_ge(dve, done + 2 * f + 1)
                        e.tensor_tensor(t[:, f, :], t[:, f, :], ps[:, 4 * f + 3, 0:CH], ALU.add).then_inc(dve, 1)
                    for f in range(2):
                        e.wait_ge(act, i * A + 5 + f)
                        e.tensor_tensor(d[:, f, :], state[:, f, cut], n[:, f, :], ALU.subtract).then_inc(dve, 1)
                        e.wait_ge(dve, done + 5 + 2 * f)
                        e.tensor_tensor(d[:, f, :], d[:, f, :], z[:, f, :], ALU.mult).then_inc(dve, 1)
                    for f in range(2):
                        e.wait_ge(dve, done + 6 + 2 * f)
                        e.tensor_tensor(state[:, f, cut], n[:, f, :], d[:, f, :], ALU.add).then_inc(dve, 1)
        st.close()

    def gat_gat_layer(self):
        c = self.c
        st = ExitStack()
        with c.together():
            b1, b2 = self.row("L3_gnn_b1", st), self.row("L3_gnn_b2", st)
        g = self.sb("g3", [P, NT, 64], F32, st)
        ht = self.sb("ht3", [P, NP], F32, st)
        inner = ExitStack()
        h = self.sb("h3", [P, NT, D], F32, inner)
        first = self.sb("first3", [P, NP], F32, inner)
        with c.together():
            wm, bm = self.matrix("L3_gnn_W_map", inner), self.columns("L3_gnn_b_map", inner)
        self.layer_norm(self.x[:], h[:])
        ps = self.psum(inner)
        self.to_features(ps, h, first)

        def mapped(e):
            for q in range(NCH):
                last = e.matmul(ps[:, q, 0:CH], wm[:], first[:, q * CH:(q + 1) * CH], start=True, stop=True)
            return last
        c.op("t", mapped)
        c.op("a", lambda e: e.activation(ht[:].rearrange("p (q n) -> p q n", n=CH), ps[:, :, 0:CH],
                                         ACT.Identity, bias=bm[:, 0:1]))
        c.run()
        inner.close()

        def elu(heads):
            last = ExitStack()
            low = self.sb("low", [P, NT, 64], F32, last)
            v = heads.rearrange("p t h c -> p t (h c)")
            c.op("v", lambda e: e.tensor_tensor(g[:], v, over_nodes(b1[:]), ALU.add))
            c.op("v", lambda e: e.tensor_scalar(low[:], g[:], 0.0, None, ALU.min))
            c.op("a", lambda e: e.activation(low[:], low[:], ACT.Exp))
            c.op("v", lambda e: e.tensor_scalar(g[:], g[:], 0.0, -1.0, ALU.max, ALU.add))
            c.op("v", lambda e: e.tensor_tensor(g[:], g[:], low[:], ALU.add))
            c.run()
            last.close()
        self.attend(ht, P, "L3_gnn_W1", "L3_gnn_att_src1", "L3_gnn_att_dst1", 8, 8, elu)
        turn = ExitStack()
        self.to_features(self.psum(turn), g, ht, 64)
        c.run()
        turn.close()

        def finish(heads):
            v = heads.rearrange("p t h c -> p t (h c)")
            c.op("v", lambda e: e.tensor_tensor(v, v, over_nodes(b2[:]), ALU.add))
            self.add_to_x(v)
            c.run()
        self.attend(ht, 64, "L3_gnn_W2", "L3_gnn_att_src2", "L3_gnn_att_dst2", 1, D, finish)
        st.close()

    def store(self):
        c = self.c
        with c.together():
            c.dma("s", node_rows(self.out[0:(NT - 1) * P, :]), self.x[:, 0:NT - 1, :])
            c.dma("a", self.out[(NT - 1) * P:N, :], self.x[0:LAST, NT - 1, :])
        c.run()


def build(nc, ins, out):
    k = Kernel(nc, ins, out)
    with k.stack:
        k.constants()
        k.graph()
        k.degrees()
        k.gcn_layer()
        k.gcn_gat_layer()
        k.gated_layer()
        k.gat_gat_layer()
        k.store()


_TURNED = ("L2_gnn_W", "L2_gnn_w_ih", "L2_gnn_w_hh", "L2_gnn_l0_w", "L2_gnn_l1_w")


def kernel(**inputs):
    import concourse.bacc as _bacc
    from concourse.bass_utils import run_bass_kernel_spmd as _run

    nc = _bacc.Bacc("TRN2", target_bir_lowering=False, num_devices=1)
    arrays, ins = {}, {}
    for name, value in inputs.items():
        a = np.asarray(value)
        a = np.ascontiguousarray(a.swapaxes(-1, -2) if name in _TURNED else a)
        arrays[name] = a
        ins[name] = nc.dram_tensor(name, a.shape, mybir.dt.from_np(a.dtype), kind="ExternalInput").ap()
    out = nc.dram_tensor("out", (N, D), F32, kind="ExternalOutput").ap()
    build(nc, ins, out)
    r = _run(nc, [arrays], core_ids=[0])
    return r.results[0]["out"]
```

```python
from contextlib import ExitStack

import numpy as np

import concourse.bass as bass
from concourse import mybir

F32 = mybir.dt.float32
BF16 = mybir.dt.bfloat16
I32 = mybir.dt.int32
ALU = mybir.AluOpType
ACT = mybir.ActivationFunctionType
AX = mybir.AxisListType

P = 128
N = 3125
E = 53125
D = 128
NT = -(-N // P)
NP = NT * P
LAST = N - (NT - 1) * P
SPLIT = NT // 2
ET = -(-E // P)
EPR = 512
ER = ET * P // EPR
ETR = EPR // P
STEPS = ET + NT - 1
KJ = 4
KP = STEPS // KJ
BODY = 20
GRP = 5
NG = BODY // GRP
ITERS = STEPS // BODY
AHEAD = STEPS + BODY
RING = 4
BIG = 1e30
NEG = 0.2
EPS = 1e-5
S2 = 256
LAYERS = 5
CH = 400
GC = 400
NGC = NP // GC
HW = 155
HSTEP = (NP - HW) // (ITERS - 1)
NCH = NP // CH
TQ = 100
assert ER * EPR == ET * P and KP * KJ == STEPS and ITERS * BODY == STEPS and NCH * CH == NP
assert HSTEP <= HW and HSTEP * (ITERS - 1) + HW == NP


class Chain:

    def __init__(self, nc, name):
        self.nc, self.name = nc, name
        self.done = nc.alloc_semaphore(name + "_done")
        self.landed = nc.alloc_semaphore(name + "_landed")
        self.fetched = nc.alloc_semaphore(name + "_fetched")
        self.counts = (0, 0, 0)
        self.queues = {k: [] for k in "ptvas"}
        self.queued = 0
        self.floor = None

    def together(self):
        return _Together(self)

    def _queue(self, engine, build, kind):
        self.queues[engine].append((self.queued, self.floor or self.counts, build, kind))
        self.queued += 1
        self.counts = tuple(n + (0 if k != kind else 16 if k else 1) for k, n in enumerate(self.counts))

    def op(self, engine, build):
        self._queue(engine, build, 0)

    def dma(self, engine, out, in_):
        self._queue(engine, lambda e: e.dma_start(out, in_), 1)

    def gather(self, out, table, index):
        self._queue("p", lambda e: e.indirect_dma_start(
            out=out, out_offset=None, in_=table,
            in_offset=bass.IndirectOffsetOnAxis(ap=index, axis=0)), 2)

    def run(self, *lanes):
        chains = (self,) + lanes
        queues = {k: sorted(((at, n, need, build, kind) for n, c in enumerate(chains)
                             for at, need, build, kind in c.queues[k]), key=lambda q: q[:2]) for k in "ptvas"}
        for c in chains:
            c.queues, c.queued = {k: [] for k in "ptvas"}, 0

        def wait(e, c, need, seen):
            for sem, n, was in zip((c.done, c.landed, c.fetched), need, seen):
                if n > was:
                    e.wait_ge(sem, n)
            return tuple(map(max, need, seen))

        def emit(e, queue):
            seen = [(0, 0, 0)] * len(chains)
            for _, n, need, build, kind in queue:
                c = chains[n]
                seen[n] = wait(e, c, need, seen[n])
                build(e).then_inc((c.done, c.landed, c.fetched)[kind], 16 if kind else 1)

        with self.nc.Block() as block:
            @block.gpsimd
            def _(e):
                emit(e, queues["p"])

            @block.tensor
            def _(e):
                emit(e, queues["t"])

            @block.vector
            def _(e):
                emit(e, queues["v"])

            @block.scalar
            def _(e):
                emit(e, queues["a"])

            @block.sync
            def _(e):
                emit(e, queues["s"])
                for c in chains:
                    wait(e, c, c.counts, (0, 0, 0))


class _Together:
    def __init__(self, chain):
        self.chain = chain

    def __enter__(self):
        self.chain.floor = self.chain.counts

    def __exit__(self, *_):
        self.chain.floor = None


def node_rows(dram):
    return dram.rearrange("(t p) w -> p t w", p=P)


def half_way(lo, hi):
    return lo + 4 * ((hi - lo + 4) // 8)


def over_nodes(ap, nt=NT):
    return ap.unsqueeze(1).to_broadcast([ap.shape[0], nt, ap.shape[1]])


def over_features(ap, w):
    return ap.unsqueeze(2).to_broadcast([ap.shape[0], ap.shape[1], w])


class Hidden:

    def __init__(self, k, ps, state, wih, whh, stack, room):
        self.k, self.ps, self.state, self.wih, self.whh = k, ps, state, wih, whh
        self.wl = k.sb("wl", [P, 2, S2], F32, stack)
        self.zero = k.sb("zero", [P, GC], F32, stack)
        self.folded = k.sb("folded", [P, 2, 3 * S2], F32, stack)
        self.rz = k.sb("hidden_rz", [P, 2, 2, NP], F32, stack)
        self.n = (k.x[:].rearrange("p t w -> p (t w)"), room[:])
        self.sems = [k.nc.alloc_semaphore("hidden_" + n) for n in ("weights", "made", "kept")]

    def load(self, e):
        for sem in self.idle:
            e.sem_clear(sem)
        for j in range(2):
            w = self.k.ins["L2_gnn_W"][bass.ds(self.layer, 1), j * P:(j + 1) * P, :]
            e.dma_start(self.wl[:, j, :], w.rearrange("a p w -> p (a w)")).then_inc(self.sems[0], 16)

    def fold(self, e):
        weights, made, kept = self.sems
        e.wait_ge(weights, 32)
        for m in range(2):
            for half in range(2):
                for j in range(2):
                    mm = e.matmul(self.ps[:, RING + 2 * m + half, 0:384], self.wl[:, j, m * P:(m + 1) * P],
                                  self.wih[:, j, half * 384:(half + 1) * 384], start=j == 0, stop=j == 1)
        mm.then_inc(made, 1)

    def product(self, e, i, f):
        weights, made, kept = self.sems
        e.wait_ge(kept, i * 2 + f + 1)
        for gate in range(3):
            at = slice(gate * S2 + f * P, gate * S2 + (f + 1) * P)
            for j in range(self.halves):
                mm = e.matmul(self.ps[:, RING + f, gate * HW:(gate + 1) * HW], self.whh[:, j, at],
                              self.state[:, j, bass.ds(i * HSTEP, HW)], start=j == 0, stop=j == self.halves - 1)
        mm.then_inc(made, 1)

    def keep(self, e):
        weights, made, kept = self.sems
        e.wait_ge(made, 1)
        e.copy(self.folded[:].rearrange("p m (f w) -> p (m f) w", f=2), self.ps[:, RING:RING + 4, 0:384]).then_inc(kept, 1)
        with e.Fori(0, ITERS) as i:
            for f in range(2):
                cut = bass.ds(i * HSTEP, HW)
                e.wait_ge(made, i * 2 + f + 2)
                e.copy(self.rz[:, f, :, cut], self.ps[:, RING + f, 0:2 * HW].rearrange("p (g n) -> p g n", g=2))
                e.copy(self.n[f][:, cut], self.ps[:, RING + f, 2 * HW:3 * HW]).then_inc(kept, 1)


class Kernel:
    def __init__(self, nc, ins, out):
        self.nc, self.ins, self.out = nc, ins, out
        self.stack = ExitStack()
        self.count = 0

    def name(self, what):
        self.count += 1
        return f"{what}_{self.count}"

    def sb(self, what, shape, dt=F32, stack=None):
        return (stack or self.stack).enter_context(self.nc.sbuf_tensor(self.name(what), shape, dt))

    def dram(self, what, shape, dt=F32):
        return self.nc.dram_tensor(self.name(what), shape, dt, kind="Internal").ap()

    def psum(self, stack, shape=(P, 8, 512)):
        return stack.enter_context(self.nc.psum_tensor(self.name("psum"), list(shape), F32))

    def constants(self):
        sb = self.sb
        self.ident = sb("ident", [P, P])
        self.iota = sb("iota", [P, P])
        self.iota_nt = sb("iota_nt", [P, NT])
        self.pidx = sb("pidx", [P, 1])
        self.ones = sb("ones", [P, P])
        self.live = sb("live", [P, P])
        self.src_idx = sb("src_idx", [P, AHEAD], I32)
        self.place = sb("place", [P, AHEAD])
        self.window = sb("window", [1, STEPS + 4], I32)
        self.src_win = sb("src_win", [P, STEPS])
        self.valid = sb("valid", [P, STEPS])
        self.last = sb("last", [P, STEPS])
        self.cut_start = sb("cut_start", [KP, KJ, P])
        self.cut_last = sb("cut_last", [KP, KJ, P])
        self.rows_start = sb("rows_start", [8, STEPS])
        self.rows_last = sb("rows_last", [8, STEPS])
        self.win_hot = sb("win_hot", [KP, KJ, NT])
        self.dinv = sb("dinv", [P, NT])
        self.x = sb("x", [P, NT, D])
        self.row_scratch = self.dram("row_scratch", [2, STEPS * P], BF16)
        self.edge_scratch = self.dram("edge_scratch", [ET, 4 * P])
        c = self.c = Chain(self.nc, "c")
        self.lanes = ((Chain(self.nc, "low"), 0, SPLIT), (Chain(self.nc, "high"), SPLIT, NT))
        with c.together():
            c.op("p", lambda e: e.memset(self.ident[:], 0.0))
            c.op("p", lambda e: e.iota(self.iota[:], [[1, P]], base=0, channel_multiplier=0,
                                       allow_small_or_imprecise_dtypes=True))
            c.op("p", lambda e: e.iota(self.iota_nt[:], [[1, NT]], base=0, channel_multiplier=0,
                                       allow_small_or_imprecise_dtypes=True))
            c.op("p", lambda e: e.iota(self.pidx[:], [[1, 1]], base=0, channel_multiplier=1,
                                       allow_small_or_imprecise_dtypes=True))
            c.op("v", lambda e: e.memset(self.ones[:], 1.0))
            c.op("v", lambda e: e.memset(self.live[:], 0.0))
            c.op("v", lambda e: e.memset(self.window[:], 0))
            c.op("v", lambda e: e.memset(self.src_idx[:], 0))
            c.op("v", lambda e: e.memset(self.place[:], 0.0))
            c.op("v", lambda e: e.memset(self.x[:, NT - 1, :], 0.0))
        with c.together():
            c.op("p", lambda e: e.affine_select(out=self.ident[:], in_=self.ident[:], compare_op=ALU.not_equal,
                                                fill=1.0, base=0, pattern=[[-1, P]], channel_multiplier=1))
            c.op("v", lambda e: e.memset(self.live[0:LAST, :], 1.0))
            x = self.ins["x"]
            c.dma("s", self.x[:, 0:NT - 1, :], node_rows(x[0:(NT - 1) * P, :]))
            c.dma("s", self.x[0:LAST, NT - 1, :], x[(NT - 1) * P:N, :])

    def graph(self):
        c = self.c
        st = ExitStack()
        sb = lambda *a: self.sb(*a, stack=st)
        src, dst = self.ins["src"], self.ins["dst"]
        whole, rest = E // EPR, E % EPR
        si, di, pi, ni = (sb(w, [ER, EPR], I32) for w in ("src_i", "dst_i", "prev_i", "next_i"))
        pack = sb("pack", [ER, ETR, 4, P])
        first = sb("first", [ER, ETR], I32)
        first_f = sb("first_f", [ER, ETR])
        tile_no = sb("tile_no", [ER, ETR])
        some = sb("some", [ER, ETR])
        step_row = sb("step_row", [P, STEPS])
        reached = sb("reached", [ER, ETR, STEPS])
        tile_c = sb("tile_c", [KP, KJ])
        tile_i = sb("tile_i", [KP, KJ], I32)
        step_c = sb("step_c", [KP, KJ])
        win_c = sb("win_c", [KP, KJ])
        win128 = sb("win128", [KP, KJ])
        win_r = sb("win_r", [1, STEPS])
        rows = sb("rows", [KP, KJ, 4 * P])
        place_r = sb("place_r", [KP, KJ, P])
        valid_r = sb("valid_r", [KP, KJ, P])
        start_r = sb("start_r", [KP, KJ, P])
        last_r = sb("last_r", [KP, KJ, P])
        src_ri = sb("src_ri", [KP, KJ, P], I32)
        low_i = sb("low_i", [KP, KJ, P], I32)
        high_i = sb("high_i", [KP, KJ, P], I32)
        low_f = sb("low_f", [KP, KJ, P])
        high_f = sb("high_f", [KP, KJ, P])
        bf = sb("bf", [KP, 2, KJ, P], BF16)
        any_f = sb("any_f", [KP, 2, KJ])
        any8 = sb("any8", [KP, 2, KJ, 8])
        ps = self.psum(st)

        with c.together():
            for t, fill in ((si, 0), (di, NP), (pi, -1), (ni, -1)):
                c.op("v", lambda e, t=t, fill=fill: e.memset(t[:], fill))
            c.op("p", lambda e: e.iota(tile_no[:], [[1, ETR]], base=0, channel_multiplier=ETR,
                                       allow_small_or_imprecise_dtypes=True))
            c.op("p", lambda e: e.iota(step_row[:], [[1, STEPS]], base=0, channel_multiplier=0,
                                       allow_small_or_imprecise_dtypes=True))
            c.op("p", lambda e: e.iota(step_c[:], [[KP, KJ]], base=0, channel_multiplier=1,
                                       allow_small_or_imprecise_dtypes=True))
        one = lambda ap: ap.rearrange("(a b) -> a b", a=1)
        many = lambda ap: ap.rearrange("(a b) -> a b", b=EPR)
        with c.together():
            for t, a in ((si, src), (di, dst)):
                c.dma("s", t[0:whole, :], many(a[0:whole * EPR]))
                c.dma("a", t[whole:whole + 1, 0:rest], one(a[whole * EPR:E]))
            c.dma("s", pi[0:1, 1:EPR], one(dst[0:EPR - 1]))
            c.dma("s", pi[1:whole, :], many(dst[EPR - 1:whole * EPR - 1]))
            c.dma("a", pi[whole:whole + 1, 0:rest + 1], one(dst[whole * EPR - 1:E]))
            c.dma("s", ni[0:whole, :], many(dst[1:whole * EPR + 1]))
            c.dma("a", ni[whole:whole + 1, 0:rest - 1], one(dst[whole * EPR + 1:E]))
        row = lambda t: t[:].rearrange("p (g q) -> p g q", g=ETR)
        with c.together():
            c.op("v", lambda e: e.tensor_copy(pack[:, :, 0, :], row(si)))
            c.op("v", lambda e: e.tensor_copy(pack[:, :, 1, :], row(di)))
            c.op("v", lambda e: e.tensor_tensor(pack[:, :, 2, :], row(di), row(pi), ALU.not_equal))
            c.op("v", lambda e: e.tensor_tensor(pack[:, :, 3, :], row(di), row(ni), ALU.not_equal))
            c.op("v", lambda e: e.tensor_scalar(first[:], di[:, 0:EPR:P], 7, None, ALU.arith_shift_right))
            c.op("v", lambda e: e.tensor_scalar(some[:], tile_no[:], 1.0, None, ALU.min))
        c.dma("s", self.edge_scratch.rearrange("(p g) w -> p (g w)", g=ETR),
              pack[:].rearrange("p g c q -> p (g c q)"))
        c.op("v", lambda e: e.tensor_copy(first_f[:], first[:]))
        c.op("v", lambda e: e.tensor_tensor(first_f[:], first_f[:], tile_no[:], ALU.add))
        c.op("v", lambda e: e.tensor_tensor(first_f[:], first_f[:], some[:], ALU.mult))
        with c.together():
            for g in range(ETR):
                c.op("v", lambda e, g=g: e.tensor_scalar(reached[:, g, :], step_row[0:ER, :],
                                                         first_f[:, g:g + 1], None, ALU.is_ge))

        def count(e):
            for g in range(ETR):
                e.matmul(ps[0:1, 0, 0:STEPS], self.ones[0:ER, 0:1], reached[:, g, :],
                         start=g == 0, stop=g == ETR - 1)
            for j in range(KJ):
                for g in range(ETR):
                    last = e.matmul(ps[0:KP, 1, j:j + 1], reached[:, g, KP * j:KP * (j + 1)],
                                    self.ones[0:ER, 0:1], start=g == 0, stop=g == ETR - 1)
            return last
        c.op("t", count)
        with c.together():
            c.op("v", lambda e: e.tensor_scalar(tile_c[:], ps[0:KP, 1, 0:KJ], -1.0, None, ALU.add))
            c.op("v", lambda e: e.scalar_tensor_tensor(win_r[:], ps[0:1, 0, 0:STEPS], -1.0, step_row[0:1, :],
                                                       ALU.mult, ALU.add))
        with c.together():
            c.op("v", lambda e: e.tensor_copy(tile_i[:], tile_c[:]))
            c.op("v", lambda e: e.tensor_tensor(win_c[:], step_c[:], tile_c[:], ALU.subtract))
            c.op("v", lambda e: e.tensor_scalar(self.window[:, 1:STEPS + 1], win_r[:], 1.0, None, ALU.add))
        c.op("v", lambda e: e.tensor_scalar(win128[:], win_c[:], float(P), None, ALU.mult))
        with c.together():
            for j in range(KJ):
                c.gather(rows[:, j, :], self.edge_scratch, tile_i[:, j:j + 1])
                c.op("v", lambda e, j=j: e.tensor_scalar(self.win_hot[:, j, :], self.iota_nt[0:KP, :],
                                                         win_c[:, j:j + 1], None, ALU.is_equal))
        part = lambda n: rows[:, :, n * P:(n + 1) * P]
        with c.together():
            for j in range(KJ):
                c.op("v", lambda e, j=j: e.tensor_scalar(place_r[:, j, :], rows[:, j, P:2 * P],
                                                         win128[:, j:j + 1], None, ALU.subtract))
            c.op("a", lambda e: e.copy(src_ri[:], part(0)))
        with c.together():
            c.op("v", lambda e: e.tensor_scalar(valid_r[:], place_r[:], 0.0, None, ALU.is_ge))
            c.op("v", lambda e: e.tensor_scalar(low_i[:], src_ri[:], P - 1, None, ALU.bitwise_and))
            c.op("v", lambda e: e.tensor_scalar(high_i[:], src_ri[:], 7, None, ALU.arith_shift_right))
            c.op("a", lambda e: e.copy(bf[:, 1, :, :], place_r[:]))
        with c.together():
            c.op("v", lambda e: e.scalar_tensor_tensor(valid_r[:], place_r[:], P - 1.0, valid_r[:],
                                                       ALU.is_le, ALU.mult))
            c.op("a", lambda e: e.copy(low_f[:], low_i[:]))
            c.op("a", lambda e: e.copy(bf[:, 0, :, :], low_i[:]))
            c.op("a", lambda e: e.copy(high_f[:], high_i[:]))
        with c.together():
            c.op("v", lambda e: e.tensor_tensor(start_r[:], part(2), valid_r[:], ALU.mult))
            c.op("v", lambda e: e.tensor_tensor(last_r[:], part(3), valid_r[:], ALU.mult))
            for n in range(2):
                c.dma("s", self.row_scratch[n, :].rearrange("(j p q) -> p j q", j=KJ, p=KP), bf[:, n, :, :])
        with c.together():
            c.op("v", lambda e: e.tensor_scalar(self.cut_start[:], start_r[:], -BIG, None, ALU.mult))
            c.op("v", lambda e: e.tensor_scalar(self.cut_last[:], last_r[:], -BIG, None, ALU.mult))
        with c.together():
            c.op("v", lambda e: e.tensor_reduce(any_f[:, 0, :], self.cut_start[:], AX.X, ALU.min))
            c.op("v", lambda e: e.tensor_reduce(any_f[:, 1, :], self.cut_last[:], AX.X, ALU.min))
        c.op("v", lambda e: e.tensor_copy(any8[:], any_f[:].unsqueeze(3).to_broadcast([KP, 2, KJ, 8])))

        turned = (part(0), place_r, high_f, valid_r, last_r)

        def turn(e):
            for n, t in enumerate(turned):
                for j in range(KJ):
                    e.transpose(ps[:, n, KP * j:KP * (j + 1)], t[:, j, :], self.ident[0:KP, 0:KP])
            for n in range(2):
                for j in range(KJ):
                    last = e.transpose(ps[0:8, 5 + n, KP * j:KP * (j + 1)], any8[:, n, j, :],
                                       self.ident[0:KP, 0:KP])
            return last
        c.op("t", turn)
        with c.together():
            for n, t in enumerate((self.src_idx, self.place, self.src_win, self.valid, self.last)):
                c.op("va"[n % 2], lambda e, n=n, t=t: (e.copy if n % 2 else e.tensor_copy)(t[:, 0:STEPS], ps[:, n, 0:STEPS]))
            c.op("v", lambda e: e.tensor_copy(self.rows_start[:], ps[0:8, 5, 0:STEPS]))
            c.op("v", lambda e: e.tensor_copy(self.rows_last[:], ps[0:8, 6, 0:STEPS]))
        self.run_lanes(c)
        st.close()

    def degrees(self):
        nc, c = self.nc, self.c
        st = ExitStack()
        hot = self.sb("deg_hot", [P, 2, BODY, P], BF16, st)
        one = self.sb("one_bf", [P, 1], BF16, st)
        by_step = self.sb("deg_step", [P, STEPS], F32, st)
        iota_bf, place_bf = self.sb("iota_bf", [P, P], BF16, st), self.sb("place_bf", [P, STEPS], BF16, st)
        with c.together():
            c.op("v", lambda e: e.tensor_copy(iota_bf[:], self.iota[:]))
            c.op("v", lambda e: e.tensor_copy(place_bf[:], self.place[:, 0:STEPS]))
        c.run()
        turned = self.sb("deg_turned", [KP, KJ, P], F32, st)
        ps = self.psum(st)
        hots, cols, kept = (nc.alloc_semaphore(n) for n in ("deg_hots", "deg_cols", "deg_kept"))
        with nc.Block() as block:
            @block.vector
            def _(e):
                e.memset(one[:], 1.0).then_inc(hots, 1)
                with e.Fori(0, ITERS // 2) as i:
                    for b in range(2):
                        e.wait_ge(cols, i * 2 + b + 1)
                        k = i * (2 * BODY) + b * BODY
                        e.tensor_tensor(hot[:, b, :, :], iota_bf[:].unsqueeze(1).to_broadcast([P, BODY, P]),
                                        over_features(place_bf[:, bass.ds(k, BODY)], P),
                                        ALU.is_equal).then_inc(hots, 1)

            @block.tensor
            def _(e):
                e.sem_inc(cols, 2)
                with e.Fori(0, ITERS // 2) as i:
                    for b in range(2):
                        e.wait_ge(hots, i * 2 + b + 2)
                        e.wait_ge(kept, i * 2 + b + 1)
                        for s in range(BODY):
                            mm = e.matmul(ps[:, b, s:s + 1], hot[:, b, s, :], one[:], start=True, stop=True)
                        mm.then_inc(cols, 1)

            @block.scalar
            def _(e):
                e.sem_inc(kept, 2)
                with e.Fori(0, ITERS // 2) as i:
                    for b in range(2):
                        e.wait_ge(cols, i * 2 + b + 3)
                        e.copy(by_step[:, bass.ds(i * (2 * BODY) + b * BODY, BODY)],
                               ps[:, b, 0:BODY]).then_inc(kept, 1)

        def turn(e):
            for j in range(KJ):
                last = e.transpose(ps[0:KP, 0, P * j:P * (j + 1)], by_step[:, KP * j:KP * (j + 1)], self.ident[:])
            return last
        c.op("t", turn)
        c.op("v", lambda e: e.tensor_copy(turned[:].rearrange("p j q -> p (j q)"), ps[0:KP, 0, :]))

        def total(e):
            for j in range(KJ):
                last = e.matmul(ps[:, 1, 0:NT], turned[:, j, :], self.win_hot[:, j, :],
                                start=j == 0, stop=j == KJ - 1)
            return last
        c.op("t", total)
        c.op("v", lambda e: e.tensor_scalar(self.dinv[:], ps[:, 1, 0:NT], 1.0, None, ALU.add))
        c.op("v", lambda e: e.reciprocal(self.dinv[:], self.dinv[:]))
        c.op("a", lambda e: e.sqrt(self.dinv[:], self.dinv[:]))
        c.run()
        st.close()

    def edge_sums(self, ps, table, width, acc, heads=0, extra=None, turned=False, sems=None, before=0, beside=None):
        nc = self.nc
        st = ExitStack()
        nx = extra.shape[2] if extra is not None else 0
        cols = width + nx
        per = width // max(heads, 1)
        rows = self.sb("rows", [P, BODY, cols], F32, st)
        index = self.sb("index", [P, BODY], I32, st)
        place = self.sb("place_now", [P, BODY], F32, st)
        hot = self.sb("hot", [P, BODY, P], F32, st)
        by_act = heads and per == P
        if sems is None:
            sems = self.edge_sems()
        indexed, ready, summed, kept, scaled, started, *fetched = sems

        def landed(i):
            return before * (ITERS * 16 * GRP) + i * (16 * GRP) + 16 * GRP

        with nc.Block() as block:
            @block.gpsimd
            def _(e):
                with e.Fori(0, ITERS) as i:
                    for g in range(NG):
                        e.wait_ge(indexed, i * NG + g + 1)
                        e.sem_inc(started, 1)
                        for s in range(GRP * g, GRP * (g + 1)):
                            e.indirect_dma_start(
                                out=rows[:, s, 0:width], out_offset=None, in_=table,
                                in_offset=bass.IndirectOffsetOnAxis(ap=index[:, s:s + 1], axis=0)
                            ).then_inc(fetched[g], 16)

            @block.vector
            def _(e):
                regs = [e.alloc_register(self.name("window_reg")) for _ in range(GRP)]

                def bring(k, g):
                    part = slice(GRP * g, GRP * (g + 1))
                    e.tensor_copy(index[:, part], self.src_idx[:, k])
                    inst = e.tensor_copy(place[:, part], self.place[:, k])
                    if nx:
                        inst = e.tensor_copy(rows[:, part, width:cols], extra[:, k, :])
                    inst.then_inc(indexed, 1)

                def add(r, w, own):
                    e.wait_ge(kept, own)
                    if turned:
                        a = acc[:, :, bass.ds(w * P, P)]
                        b = ps[:, r, 0:width].rearrange("p (f n) -> p f n", n=P)
                    else:
                        a = acc[:].rearrange("p t w -> p (t w)")[:, bass.ds(w * cols, cols)]
                        b = ps[:, r, 0:cols]
                    e.tensor_tensor(a, a, b, ALU.add).then_inc(kept, 1)

                def compare(g):
                    part = slice(GRP * g, GRP * (g + 1))
                    e.tensor_tensor(hot[:, part, :], self.iota[:].unsqueeze(1).to_broadcast([P, GRP, P]),
                                    over_features(place[:, part], P), ALU.is_equal).then_inc(ready, 1)

                e.memset(ps[:, RING - 1, 0:cols], 0.0).then_inc(kept, 1)
                for g in range(NG):
                    bring(slice(GRP * g, GRP * (g + 1)), g)
                e.wait_ge(indexed, 1)
                compare(0)
                with e.Fori(0, ITERS) as i:
                    k = i * BODY
                    for g in range(NG):
                        s0 = GRP * g
                        e.load(regs, self.window[0:1, bass.ds(k + s0, GRP)])
                        w = [e.snap(r, min_val=0, max_val=NT - 1) for r in regs]
                        e.wait_ge(indexed, i * NG + g + 2)
                        e.wait_ge(summed, k + s0 + 2 * GRP)
                        compare((g + 1) % NG)
                        if heads and not by_act:
                            e.wait_ge(fetched[g], landed(i))
                            scale = rows[:, s0:s0 + GRP, 0:width].rearrange("p s (h c) -> p s h c", h=heads)
                            by = rows[:, s0:s0 + GRP, width:width + heads].unsqueeze(3)
                            e.tensor_tensor(scale, scale, by.to_broadcast([P, GRP, heads, per]),
                                            ALU.mult).then_inc(scaled, GRP)
                        for s in range(s0, s0 + GRP):
                            e.wait_ge(summed, k + s + BODY)
                            if s == s0 and g > 0:
                                e.wait_ge(ready, i * NG + g)
                                bring(bass.ds(k + BODY + s - GRP, GRP), g - 1)
                            add((s - 1) % RING, w[s - s0], k + s + RING)
                    e.wait_ge(summed, k + BODY + BODY)
                    e.wait_ge(ready, i * NG + NG)
                    bring(bass.ds(k + BODY + BODY - GRP, GRP), NG - 1)
                e.load(regs[:1], self.window[0:1, STEPS:STEPS + 1])
                w = e.snap(regs[0], min_val=0, max_val=NT - 1)
                add((STEPS - 1) % RING, w, STEPS + RING)
                e.wait_ge(kept, STEPS + RING + 1)
                e.wait_ge(indexed, (ITERS + 1) * NG)
                e.wait_ge(ready, ITERS * NG + 1)
                for r in regs:
                    e.free_register(r)

            @block.sync
            def _(e):
                if beside:
                    beside.load(e)

            @block.scalar
            def _(e):
                if beside:
                    beside.keep(e)
                if by_act:
                    with e.Fori(0, ITERS) as i:
                        for g in range(NG):
                            e.wait_ge(indexed, i * NG + g + 1)
                            e.wait_ge(fetched[g], landed(i))
                            for s in range(GRP * g, GRP * (g + 1)):
                                for h in range(heads):
                                    own = rows[:, s, h * per:(h + 1) * per]
                                    inst = e.activation(own, own, ACT.Copy, scale=rows[:, s, width + h:width + h + 1])
                                inst.then_inc(scaled, 1)

            @block.tensor
            def _(e):
                e.sem_inc(summed, BODY)
                e.sem_inc(kept, RING - 1)
                if beside:
                    beside.fold(e)
                with e.Fori(0, ITERS) as i:
                    k = i * BODY
                    for s in range(BODY):
                        r = s % RING
                        if s % GRP == 0:
                            e.wait_ge(fetched[s // GRP], landed(i))
                            if nx:
                                e.wait_ge(indexed, i * NG + s // GRP + 1)
                            e.wait_ge(ready, i * NG + s // GRP + 1)
                        if heads:
                            e.wait_ge(scaled, k + s + 1)
                        e.wait_ge(kept, k + s + 2)
                        if turned:
                            for f in range(width // P):
                                mm = e.matmul(ps[:, r, f * P:(f + 1) * P], rows[:, s, f * P:(f + 1) * P], hot[:, s, :],
                                              start=True, stop=True)
                        else:
                            mm = e.matmul(ps[:, r, 0:cols], hot[:, s, :], rows[:, s, :], start=True, stop=True)
                        mm.then_inc(summed, 1)
                        if beside and s % (BODY // 2) == BODY // 4:
                            beside.product(e, i, s // (BODY // 2))
        st.close()

    def edge_sems(self):
        self.count += 1
        names = ["indexed", "ready", "summed", "kept", "scaled", "started"] + [f"fetched{g}" for g in range(NG)]
        return [self.nc.alloc_semaphore(f"{n}_{self.count}") for n in names]

    def run_lanes(self, *others):
        (low, _, _), (high, _, _) = self.lanes
        low.run(high, *others)

    def to_features(self, ps, h, ht, width=D):
        flat = ps[:].rearrange("p b n -> p (b n)")
        for c, lo, hi in self.lanes:
            def turn(e, lo=lo, hi=hi):
                for t in range(lo, hi):
                    last = e.transpose(flat[0:width, t * P:(t + 1) * P], h[:, t, :], self.ident[:])
                return last
            c.op("t", turn)
            mid = half_way(lo, hi)
            with c.together():
                for engine, t0, t1 in (("v", lo, mid), ("a", mid, hi)):
                    at = slice(t0 * P, t1 * P)
                    c.op(engine, lambda e, engine=engine, at=at:
                         (e.copy if engine == "a" else e.tensor_copy)(ht[0:width, at], flat[0:width, at]))

    def layer_norm(self, st, x, d, gamma=None, beta=None):
        stats = self.sb("stats", [P, NT, 6], F32, st)
        both = self.sb("mean_var", [P, NT, 2], F32, st)
        scale, shift = self.sb("scale", [P, NT], F32, st), self.sb("shift", [P, NT], F32, st)
        for c, lo, hi in self.lanes:
            at = slice(lo, hi)
            by_dve = slice(lo, lo + (hi - lo) * 4 // 7)
            with c.together():
                for t in range(lo, hi):
                    c.op("v", lambda e, t=t: e.bn_stats(out=stats[:, t, :], in_=x[:, t, :]))
            with c.together():
                for t in range(lo, hi):
                    c.op("v", lambda e, t=t: e.bn_aggr(out=both[:, t, :], in_=stats[:, t, :]))
            c.op("v", lambda e, at=at: e.tensor_scalar(scale[:, at], both[:, at, 1], EPS, None, ALU.add))
            c.op("v", lambda e, at=at: e.reciprocal(scale[:, at], scale[:, at]))
            c.op("a", lambda e, at=at: e.sqrt(scale[:, at], scale[:, at]))
            c.op("v", lambda e, at=at: e.scalar_tensor_tensor(shift[:, at], both[:, at, 0], -1.0, scale[:, at],
                                                              ALU.mult, ALU.mult))
            with c.together():
                for t in range(lo, hi):
                    if t < by_dve.stop:
                        c.op("v", lambda e, t=t: e.tensor_scalar(d[:, t, :], x[:, t, :], scale[:, t:t + 1],
                                                                 shift[:, t:t + 1], ALU.mult, ALU.add))
                    else:
                        c.op("a", lambda e, t=t: e.activation(
                            d[:, t, :], x[:, t, :], ACT.Relu if gamma is None else ACT.Identity,
                            scale=scale[:, t:t + 1], bias=shift[:, t:t + 1]))
            if gamma is None:
                c.op("v", lambda e, at=by_dve: e.tensor_scalar(d[:, at, :], d[:, at, :], 0.0, None, ALU.max))
            else:
                c.op("v", lambda e, at=at: e.tensor_tensor(d[:, at, :], d[:, at, :], over_nodes(gamma, at.stop - at.start), ALU.mult))
                c.op("v", lambda e, at=at: e.tensor_tensor(d[:, at, :], d[:, at, :], over_nodes(beta, at.stop - at.start), ALU.add))
                c.op("a", lambda e, at=at: e.activation(d[:, at, :], d[:, at, :], ACT.Silu))

    def row(self, name, st, parts=P):
        v = self.ins[name]
        if len(v.shape) == 2:
            v = v.rearrange("h c -> (h c)")
        t = self.sb(name, [parts, v.shape[0]], F32, st)
        self.c.dma("s", t[:], v.partition_broadcast(parts))
        return t

    def columns(self, name, st):
        v = self.ins[name]
        t = self.sb(name, [P, v.shape[0] // P], F32, st)
        for j in range(v.shape[0] // P):
            self.c.dma("s", t[:, j:j + 1], v[j * P:(j + 1) * P].rearrange("(p a) -> p a", a=1))
        return t

    def matrix(self, name, st):
        v = self.ins[name]
        k, w = v.shape
        if k <= P:
            t = self.sb(name, [k, w], F32, st)
            self.c.dma("s", t[:], v)
        else:
            t = self.sb(name, [P, k // P, w], F32, st)
            for j in range(k // P):
                self.c.dma("s", t[:, j, :], v[j * P:(j + 1) * P, :])
        return t

    def gcn(self, h, weight, bias, out):
        c = self.c
        st = ExitStack()
        table = self.dram("gcn_table", [NP, D])
        ps = self.psum(st)
        with c.together():
            w = self.matrix(weight, st)
            b = self.row(bias, st)
        inner = ExitStack()
        own = self.sb("own", [P, NT, D], F32, st)
        ht = self.sb("ht", [P, NP], F32, inner)
        c.run()
        self.to_features(ps, h, ht)
        flat = ps[:].rearrange("p b n -> p (b n)")[:, 0:NP].rearrange("p (t w) -> p t w", w=D)
        for lane, lo, hi in self.lanes:
            at = slice(lo, hi)

            def product(e, lo=lo, hi=hi):
                for t in range(lo, hi):
                    last = e.matmul(flat[:, t, :], ht[:, t * P:(t + 1) * P], w[:], start=True, stop=True)
                return last
            lane.op("t", product)
            lane.op("v", lambda e, at=at: e.tensor_tensor(own[:, at, :], flat[:, at, :], over_features(self.dinv[:, at], D), ALU.mult))
            with lane.together():
                lane.dma("s", node_rows(table[at.start * P:at.stop * P, :]), own[:, at, :])
                lane.op("a", lambda e, at=at: e.copy(out[:, at, :], own[:, at, :]))
        self.run_lanes()
        inner.close()
        self.edge_sums(ps, table, D, out)
        with c.together():
            for t in range(NT):
                c.op("v", lambda e, t=t: e.scalar_tensor_tensor(out[:, t, :], out[:, t, :], self.dinv[:, t:t + 1], b[:],
                                                                ALU.mult, ALU.add))
        c.run()
        st.close()

    def attention_weights(self, st, weight, att_src, att_dst, heads, per):
        c = self.c
        kdim = self.ins[weight].shape[0]
        w = self.sb("w", [kdim, heads * per], F32, st)
        both = self.sb("att", [kdim, 2, heads * per], F32, st)
        prod = self.sb("prod", [kdim, 2, heads, per], F32, st)
        wa = self.sb("wa", [kdim, 2, heads], F32, st)

        def queue():
            with c.together():
                c.dma("s", w[:], self.ins[weight])
                for n, a in enumerate((att_src, att_dst)):
                    c.dma("s", both[:, n, :], self.ins[a].rearrange("h c -> (h c)").partition_broadcast(kdim))
            with c.together():
                for n in range(2):
                    c.op("v", lambda e, n=n: e.tensor_tensor(prod[:, n, :, :].rearrange("p h c -> p (h c)"), w[:],
                                                             both[:, n, :], ALU.mult))
            c.op("v", lambda e: e.tensor_reduce(wa[:], prod[:], AX.X, ALU.add))
        return w, wa, queue

    def attend(self, ht, weights, heads, per, finish):
        c = self.c
        st = ExitStack()
        w, wa, _ = weights
        kdim = w.shape[0]
        hc = heads * per
        nx = 2 * heads + 1
        table = self.dram("gat_table", [NP, hc])
        node_table = self.dram("gat_node_table", [NP, 2 * heads])
        h = self.sb("h", [P, NT, hc], F32, st)
        ext = self.sb("ext", [P, AHEAD, nx], F32, st)
        es = self.sb("es", [P, NT, heads], F32, st)
        mid = ExitStack()
        ps = self.psum(mid)
        on_src = self.sb("on_src", [P, STEPS, heads], F32, mid)
        on_dst = self.sb("on_dst", [P, STEPS, 2 * heads], F32, mid)
        tabs = ExitStack()
        tab_src = self.sb("tab_src", [P, 3, heads, NT], BF16, tabs)
        tab_dst = self.sb("tab_dst", [P, STEPS, 6 * heads], BF16, tabs)
        inner = ExitStack()
        node_a = self.sb("node_a", [P, NT, 2, heads], F32, inner)
        flat = ps[:].rearrange("p b n -> p (b n)")
        step = min(hc, P)
        for lane, lo, hi in self.lanes:
            at = slice(lo, hi)
            for n in range(hc // step):
                def product(e, n=n, lo=lo, hi=hi):
                    for t in range(lo, hi):
                        last = e.matmul(flat[:, t * P:t * P + step], ht[0:kdim, t * P:(t + 1) * P],
                                        w[:, n * step:(n + 1) * step], start=True, stop=True)
                    return last
                lane.op("t", product)
                half, part = half_way(lo, hi), slice(n * step, (n + 1) * step)
                with lane.together():
                    for engine, t0, t1 in (("v", lo, half), ("a", half, hi)):
                        lane.op(engine, lambda e, engine=engine, t0=t0, t1=t1, part=part:
                                (e.copy if engine == "a" else e.tensor_copy)(
                                    h[:, t0:t1, part], flat[:, t0 * P:t1 * P].rearrange("p (t w) -> p t w", w=P)[:, :, 0:step]))

            bank = 7 if hi == NT else 0

            def attention(e, lo=lo, hi=hi, bank=bank):
                for t in range(lo, hi):
                    last = e.matmul(ps[:, bank, t * 2 * heads:(t + 1) * 2 * heads], ht[0:kdim, t * P:(t + 1) * P],
                                    wa[:].rearrange("p a h -> p (a h)"), start=True, stop=True)
                return last
            with lane.together():
                lane.op("t", attention)
                lane.dma("s", node_rows(table[lo * P:hi * P, :]), h[:, at, :])
            lane.op("v", lambda e, at=at, bank=bank: e.tensor_copy(
                node_a[:, at, :, :].rearrange("p t a h -> p (t a h)"), ps[:, bank, at.start * 2 * heads:at.stop * 2 * heads]))
            lane.dma("s", node_rows(node_table[lo * P:hi * P, :]), node_a[:, at, :, :].rearrange("p t a h -> p t (a h)"))
        self.run_lanes()
        c.op("v", lambda e: e.tensor_tensor(es[:], node_a[:, :, 0, :], node_a[:, :, 1, :], ALU.add))
        c.op("v", lambda e: e.scalar_tensor_tensor(es[:], es[:], NEG, es[:], ALU.mult, ALU.max))
        self.split([tab_src[:, n, :, :].rearrange("p h t -> p t h") for n in range(3)], node_a[:, :, 0, :])
        hot_t = self.sb("hot_t", [NT, STEPS], BF16, inner)
        parts_t = self.sb("parts_t", [NT, 3, 2 * heads, P], BF16, inner)
        cols_t = self.sb("cols_t", [NT, 2 * heads, P], F32, inner)

        def turn(e):
            for j in range(KJ):
                e.transpose(ps[0:NT, 6, KP * j:KP * (j + 1)], self.win_hot[:, j, :], self.ident[0:KP, 0:KP])
            for n in range(2 * heads):
                col = node_a[:, :, 1, n] if n < heads else es[:, :, n - heads]
                last = e.transpose(flat[0:NT, n * P:(n + 1) * P], col, self.ident[:])
            return last
        c.op("t", turn)
        with c.together():
            c.op("a", lambda e: e.copy(hot_t[:], ps[0:NT, 6, 0:STEPS]))
            c.op("v", lambda e: e.tensor_copy(cols_t[:].rearrange("p n q -> p (n q)"), flat[0:NT, 0:2 * heads * P]))
        self.split([parts_t[:, n, :, :] for n in range(3)], cols_t[:])
        c.run()
        for turn_no, lo in enumerate(range(0, 6 * heads, 4)):
            lane, bank = self.lanes[turn_no % 2][0], 4 * (turn_no % 2)
            hi = min(lo + 4, 6 * heads)

            def spread(e, lo=lo, hi=hi, bank=bank):
                for n in range(lo, hi):
                    last = e.matmul(ps[:, bank + n - lo, 0:STEPS], parts_t[:, n // (2 * heads), n % (2 * heads), :],
                                    hot_t[:], start=True, stop=True)
                return last
            lane.op("t", spread)
            cut = (hi - lo) // 2
            with lane.together():
                lane.op("v", lambda e, lo=lo, cut=cut, bank=bank: e.tensor_copy(
                    tab_dst[:, :, lo:lo + cut].rearrange("p k n -> p n k"), ps[:, bank:bank + cut, 0:STEPS]))
                lane.op("a", lambda e, lo=lo, hi=hi, cut=cut, bank=bank: e.copy(
                    tab_dst[:, :, lo + cut:hi].rearrange("p k n -> p n k"), ps[:, bank + cut:bank + hi - lo, 0:STEPS]))
        self.run_lanes()
        inner.close()
        self.by_edge(ps, tab_src, tab_dst, on_src, on_dst, heads, node_table)
        tabs.close()
        self.softmax(ps, on_src, on_dst, ext, heads)
        mid.close()
        tail = ExitStack()
        ps = self.psum(tail)
        acc = self.sb("acc", [P, NT, hc + nx], F32, tail)
        with c.together():
            c.op("v", lambda e: e.memset(acc[:], 0.0))
            c.op("p", lambda e: e.memset(ext[:, STEPS:AHEAD, :], 0.0))
        c.run()
        self.edge_sums(ps, table, hc, acc, heads=heads, extra=ext[:])
        own = self.sb("own", [P, NT, heads], F32, tail)
        none = self.sb("none", [P, NT], F32, tail)
        den = self.sb("den", [P, NT, heads], F32, tail)
        by_head = lambda t: t.rearrange("p t (h c) -> p t h c", h=heads)
        hh, sums = by_head(h[:]), by_head(acc[:, :, 0:hc])
        for lane, lo, hi in self.lanes:
            at = slice(lo, hi)
            wide = lambda t, at=at: t[:, at, :].unsqueeze(3).to_broadcast([P, at.stop - at.start, heads, per])
            lane.op("v", lambda e, at=at: e.tensor_scalar(none[:, at], acc[:, at, hc + 2 * heads], -1.0, 1.0, ALU.mult, ALU.add))
            lane.op("v", lambda e, at=at: e.tensor_tensor(own[:, at, :], acc[:, at, hc + heads:hc + 2 * heads],
                                                          over_features(none[:, at], heads), ALU.add))
            lane.op("v", lambda e, at=at: e.tensor_tensor(den[:, at, :], own[:, at, :], acc[:, at, hc:hc + heads], ALU.add))
            lane.op("v", lambda e, at=at: e.reciprocal(den[:, at, :], den[:, at, :]))
            lane.op("v", lambda e, at=at, wide=wide: e.tensor_tensor(hh[:, at], hh[:, at], wide(own), ALU.mult))
            lane.op("v", lambda e, at=at: e.tensor_tensor(hh[:, at], hh[:, at], sums[:, at], ALU.add))
            lane.op("v", lambda e, at=at, wide=wide: e.tensor_tensor(hh[:, at], hh[:, at], wide(den), ALU.mult))
        finish(hh)
        tail.close()
        st.close()

    def split(self, parts, t):
        c = self.c
        for n, part in enumerate(parts):
            c.op("v", lambda e, part=part: e.tensor_copy(part, t))
            if n < 2:
                c.op("v", lambda e, part=part: e.tensor_tensor(t, t, part, ALU.subtract))

    def by_edge(self, ps, tab_src, tab_dst, on_src, on_dst, heads, node_table):
        nc = self.nc
        st = ExitStack()
        per_bank, sub, own_steps = {1: (9, 20, 18), 2: (8, 20, 16), 8: (2, 10, 6)}[heads]
        banks = own_steps // per_bank
        slot = banks + 1
        fetch = sub - own_steps
        iters = STEPS // (2 * sub)
        w = heads * NT
        rows = self.sb("rows", [P, 2, 2, sub * P], BF16, st)
        hot = self.sb("hot", [P, 2, 2, sub * P], BF16, st)
        win = self.sb("win", [P, 2, own_steps, NT], F32, st)
        kept = self.sb("kept", [P, own_steps, heads, NT], F32, st)
        index = self.sb("index", [P, 2, fetch], I32, st)
        fetched_rows = self.sb("fetched_rows", [P, 2, fetch, 2 * heads], F32, st)
        step_tab = self.sb("step_tab", [P, 2, sub, 6 * heads], BF16, st)
        names = ("rows0", "rows1", "hots", "products", "taken_v", "taken_a", "own", "cut", "started", "fetched0", "fetched1")
        (landed0, landed1, hots, products, taken_v, taken_a, own, cut_out, started,
         *fetched) = (nc.alloc_semaphore(self.name(n)) for n in names)
        landed = (landed0, landed1)
        with nc.Block() as block:
            @block.sync
            def _(e):
                with e.Fori(0, iters) as i:
                    for b in range(2):
                        e.wait_ge(hots, i * 2 + b + 1)
                        for n, steps in enumerate((own_steps, sub)):
                            cut = self.row_scratch[n, bass.ds((i * 2 + b) * (sub * P), steps * P)]
                            e.dma_start(rows[:, b, n, 0:steps * P], cut.partition_broadcast(P)).then_inc(landed[b], 16)

            @block.vector
            def _(e):
                def make(i, b):
                    n = i * 2 + b
                    e.wait_ge(landed[b], i * 32 + 32)
                    e.wait_ge(products, n + 1)
                    for m, steps in enumerate((own_steps, sub)):
                        e.tensor_scalar(hot[:, b, m, 0:steps * P], rows[:, b, m, 0:steps * P], self.pidx[:, 0:1],
                                        None, ALU.is_equal)
                    e.wait_ge(taken_v, n + 1)
                    e.tensor_tensor(win[:, b, :, :], self.iota_nt[:].unsqueeze(1).to_broadcast([P, own_steps, NT]),
                                    over_features(self.src_win[:, bass.ds(n * sub, own_steps)], NT),
                                    ALU.is_equal).then_inc(hots, 1)

                def take(i, b):
                    n = i * 2 + b
                    e.wait_ge(own, n + 1)
                    e.wait_ge(hots, n + 3)
                    e.wait_ge(products, n + 3)
                    for bank in range(banks):
                        lo, hi = bank * per_bank, (bank + 1) * per_bank
                        inst = e.tensor_tensor(kept[:, lo:hi, :, :],
                                               ps[:, slot * b + bank, 0:per_bank * w].rearrange("p (s h t) -> p s h t", h=heads, t=NT),
                                               win[:, b, lo:hi, :].unsqueeze(2).to_broadcast([P, per_bank, heads, NT]), ALU.mult)
                    inst.then_inc(taken_v, 1)
                    e.wait_ge(taken_v, n + 3)
                    e.tensor_reduce(on_src[:, bass.ds(n * sub, own_steps), :].rearrange("p s h -> p (s h)"),
                                    kept[:].rearrange("p s h t -> p (s h) t"), AX.X, ALU.add).then_inc(own, 1)

                e.sem_inc(hots, 2)
                e.sem_inc(own, 1)
                e.sem_inc(taken_v, 2)
                make(0, 0)
                with e.Fori(0, iters - 1) as i:
                    make(i, 1)
                    take(i, 0)
                    make(i + 1, 0)
                    take(i, 1)
                make(iters - 1, 1)
                take(iters - 1, 0)
                take(iters - 1, 1)

            @block.tensor
            def _(e):
                e.sem_inc(products, 2)
                with e.Fori(0, iters) as i:
                    for b in range(2):
                        n = i * 2 + b
                        e.wait_ge(hots, n + 3)
                        e.wait_ge(taken_v, n + 1)
                        e.wait_ge(taken_a, n + 1)
                        e.wait_ge(cut_out, n + 1)
                        for s in range(sub):
                            for m in range(3 if s < own_steps else 0):
                                e.matmul(ps[:, slot * b + s // per_bank, (s % per_bank) * w:(s % per_bank + 1) * w],
                                         hot[:, b, 0, s * P:(s + 1) * P], tab_src[:, m, :, :].rearrange("p h t -> p (h t)"),
                                         start=m == 0, stop=m == 2)
                            for m in range(3):
                                mm = e.matmul(ps[:, slot * b + banks, s * 2 * heads:(s + 1) * 2 * heads],
                                              hot[:, b, 1, s * P:(s + 1) * P],
                                              step_tab[:, b, s, m * 2 * heads:(m + 1) * 2 * heads],
                                              start=m == 0, stop=m == 2)
                        mm.then_inc(products, 1)

            @block.scalar
            def _(e):
                def cut(n, b):
                    e.copy(index[:, b, :], self.src_idx[:, bass.ds(n * sub + own_steps, fetch)])
                    e.copy(step_tab[:, b, :, :], tab_dst[:, bass.ds(n * sub, sub), :]).then_inc(cut_out, 1)

                def take(i, b):
                    n = i * 2 + b
                    e.wait_ge(fetched[b], i * (16 * fetch) + 16 * fetch)
                    e.copy(on_src[:, bass.ds(n * sub + own_steps, fetch), :], fetched_rows[:, b, :, 0:heads])
                    e.wait_ge(products, n + 3)
                    e.copy(on_dst[:, bass.ds(n * sub, sub), :].rearrange("p s n -> p (s n)"),
                           ps[:, slot * b + banks, 0:sub * 2 * heads]).then_inc(taken_a, 1)

                e.sem_inc(taken_a, 2)
                cut(0, 0)
                cut(1, 1)
                with e.Fori(0, iters - 1) as i:
                    for b in range(2):
                        take(i, b)
                        cut(i * 2 + b + 2, b)
                for b in range(2):
                    take(iters - 1, b)

            @block.gpsimd
            def _(e):
                with e.Fori(0, iters) as i:
                    for b in range(2):
                        e.wait_ge(cut_out, i * 2 + b + 1)
                        e.wait_ge(taken_a, i * 2 + b + 1)
                        e.sem_inc(started, 1)
                        for s in range(fetch):
                            e.indirect_dma_start(
                                out=fetched_rows[:, b, s, :], out_offset=None, in_=node_table,
                                in_offset=bass.IndirectOffsetOnAxis(ap=index[:, b, s:s + 1], axis=0)
                            ).then_inc(fetched[b], 16)
        st.close()

    def softmax(self, ps, on_src, on_dst, ext, heads):
        c = self.c
        st = ExitStack()
        jh = KJ * heads
        logit = on_src
        floor = self.sb("floor", [P, STEPS], F32, st)
        rows = self.sb("rows", [KP, jh, P], F32, st)
        fwd = self.sb("fwd", [KP, jh, P], F32, st)
        bwd = self.sb("bwd", [KP, jh, P], F32, st)
        ends = self.sb("ends", [8, 2, STEPS], F32, st)
        carry = self.sb("carry", [8, 2, STEPS + 1], F32, st)
        carried = self.sb("carried", [KP, 2, jh], F32, st)
        most = self.sb("most", [P, STEPS, heads], F32, st)
        by_head = lambda t: t.unsqueeze(2).to_broadcast([P, STEPS, heads])
        c.op("v", lambda e: e.tensor_tensor(logit[:], on_src[:], on_dst[:, :, 0:heads], ALU.add))
        with c.together():
            c.op("v", lambda e: e.tensor_scalar(floor[:], self.valid[:], -1.0, BIG, ALU.add, ALU.mult))
            c.op("p", lambda e: e.memset(carry[:], -BIG))
        c.op("v", lambda e: e.scalar_tensor_tensor(logit[:], logit[:], NEG, logit[:], ALU.mult, ALU.max))
        c.op("v", lambda e: e.tensor_tensor(logit[:], logit[:], by_head(floor[:]), ALU.add))
        flat = ps[:].rearrange("p b n -> p (b n)")

        def turn(e):
            for j in range(KJ):
                for n in range(heads):
                    m = j * heads + n
                    last = e.transpose(flat[0:KP, m * P:(m + 1) * P], logit[:, KP * j:KP * (j + 1), n], self.ident[:])
            return last
        c.op("t", turn)
        half = max(jh // 8, 1) * 4
        with c.together():
            c.op("v", lambda e: e.tensor_copy(rows[:, 0:half, :].rearrange("p m q -> p (m q)"), flat[0:KP, 0:half * P]))
            if half < jh:
                c.op("a", lambda e: e.copy(rows[:, half:jh, :].rearrange("p m q -> p (m q)"), flat[0:KP, half * P:jh * P]))

        def scan(initial):
            with c.together():
                for m in range(jh):
                    j = m // heads
                    c.op("v", lambda e, m=m, j=j: e.tensor_tensor_scan(
                        fwd[:, m, :], self.cut_start[:, j, :], rows[:, m, :], initial(0, m), ALU.add, ALU.max))
                    c.op("v", lambda e, m=m, j=j: e.tensor_tensor_scan(
                        bwd[:, m, ::-1], self.cut_last[:, j, ::-1], rows[:, m, ::-1], initial(1, m), ALU.add, ALU.max))
        scan(lambda way, m: -BIG)

        def turn_ends(e):
            for way, (t, at) in enumerate(((fwd, P - 1), (bwd, 0))):
                for j in range(KJ):
                    last = e.transpose(ps[0:heads, way, KP * j:KP * (j + 1)],
                                       t[:, j * heads:(j + 1) * heads, at], self.ident[0:KP, 0:KP])
            return last
        c.op("t", turn_ends)
        c.op("v", lambda e: e.tensor_copy(ends[0:heads, :, :], ps[0:heads, 0:2, 0:STEPS]))
        with c.together():
            c.op("v", lambda e: e.tensor_tensor_scan(carry[0:heads, 0, 1:STEPS + 1], self.rows_start[0:heads, :],
                                                     ends[0:heads, 0, :], -BIG, ALU.add, ALU.max))
            c.op("v", lambda e: e.tensor_tensor_scan(carry[0:heads, 1, 0:STEPS][:, ::-1],
                                                     self.rows_last[0:heads, ::-1], ends[0:heads, 1, ::-1],
                                                     -BIG, ALU.add, ALU.max))

        def turn_back(e):
            for way in range(2):
                for j in range(KJ):
                    m = way * jh + j * heads
                    last = e.transpose(ps[0:KP, 0, m:m + heads],
                                       carry[0:heads, way, KP * j + way:KP * (j + 1) + way],
                                       self.ident[0:heads, 0:heads])
            return last
        c.op("t", turn_back)
        c.op("v", lambda e: e.tensor_copy(carried[:].rearrange("p w m -> p (w m)"), ps[0:KP, 0, 0:2 * jh]))
        scan(lambda way, m: carried[:, way, m:m + 1])
        c.op("v", lambda e: e.tensor_tensor(fwd[:], fwd[:], bwd[:], ALU.max))

        def back(e):
            for m in range(jh):
                last = e.transpose(flat[:, m * P:m * P + KP], fwd[:, m, :], self.ident[0:KP, 0:KP])
            return last
        c.op("t", back)
        own = on_dst[:, :, heads:2 * heads]
        with c.together():
            for j in range(KJ):
                part = slice(KP * j, KP * (j + 1))
                c.op("v", lambda e, j=j, part=part: e.tensor_tensor(
                    most[:, part, :].rearrange("q p h -> q h p"),
                    flat[:, j * heads * P:(j + 1) * heads * P].rearrange("q (h p) -> q h p", h=heads)[:, :, 0:KP],
                    own[:, part, :].rearrange("q p h -> q h p"), ALU.max))
        with c.together():
            c.op("v", lambda e: e.tensor_tensor(logit[:], logit[:], most[:], ALU.subtract))
            c.op("v", lambda e: e.tensor_tensor(own, own, most[:], ALU.subtract))
        with c.together():
            c.op("a", lambda e: e.activation(ext[:, 0:STEPS, 0:heads], logit[:], ACT.Exp))
            c.op("a", lambda e: e.activation(own, own, ACT.Exp))
            c.op("v", lambda e: e.tensor_copy(ext[:, 0:STEPS, 2 * heads], self.last[:]))
        c.op("v", lambda e: e.tensor_tensor(ext[:, 0:STEPS, heads:2 * heads], own, by_head(self.last[:]), ALU.mult))
        c.run()
        st.close()

    def add_batch_norm_relu(self, x1, h, gamma, beta):
        c = self.c
        st = ExitStack()
        ps = self.psum(st)
        sq = self.sb("sq", [P, NT, D], F32, st)
        mean, scale = self.sb("bn_mean", [P, D], F32, st), self.sb("bn_scale", [P, D], F32, st)
        with c.together():
            g, b = self.row(gamma, st), self.row(beta, st)

        def total(bank, t0):
            def build(e):
                for t in range(NT):
                    last = e.matmul(ps[:, bank, 0:D], (self.live if t == NT - 1 else self.ones)[:], t0[:, t, :],
                                    start=t == 0, stop=t == NT - 1)
                return last
            c.op("t", build)
        with c.together():
            total(0, h)
            self.add_to_x(x1[:])
        c.op("v", lambda e: e.tensor_scalar(mean[:], ps[:, 0, 0:D], 1.0 / N, None, ALU.mult))
        c.op("v", lambda e: e.tensor_tensor(h[:], h[:], over_nodes(mean[:]), ALU.subtract))
        c.op("a", lambda e: e.activation(sq[:], h[:], ACT.Square))
        total(1, sq)
        c.op("v", lambda e: e.tensor_scalar(scale[:], ps[:, 1, 0:D], 1.0 / N, EPS, ALU.mult, ALU.add))
        c.op("v", lambda e: e.reciprocal(scale[:], scale[:]))
        c.op("a", lambda e: e.sqrt(scale[:], scale[:]))
        c.op("v", lambda e: e.tensor_tensor(scale[:], scale[:], g[:], ALU.mult))
        c.op("v", lambda e: e.tensor_tensor(h[:], h[:], over_nodes(scale[:]), ALU.mult))
        c.op("v", lambda e: e.tensor_tensor(h[:], h[:], over_nodes(b[:]), ALU.add))
        c.op("v", lambda e: e.scalar_tensor_tensor(self.x[:], h[:], 0.0, self.x[:], ALU.max, ALU.add))
        c.run()
        st.close()

    def add_to_x(self, h):
        self.c.op("v", lambda e: e.tensor_tensor(self.x[:], self.x[:], h, ALU.add))

    def gcn_layer(self, h, out):
        self.gcn(h, "L0_gnn_W", "L0_gnn_b", out[:])
        self.add_batch_norm_relu(h, out, "L0_gnn_gamma", "L0_gnn_beta")

    def gcn_gat_layer(self):
        c = self.c
        st = ExitStack()
        with c.together():
            g, b, bias = (self.row("L1_gnn_" + n, st) for n in ("ln_gamma", "ln_beta", "gat_b"))
        ht = self.sb("ht1", [P, NP], F32, st)
        weights = self.attention_weights(st, "L1_gnn_gat_w", "L1_gnn_att_src", "L1_gnn_att_dst", 2, D)
        inner = ExitStack()
        h, out = self.sb("h1", [P, NT, D], F32, inner), self.sb("out1", [P, NT, D], F32, inner)
        self.layer_norm(inner, self.x[:], h[:])
        self.gcn(h, "L1_gnn_gcn_w", "L1_gnn_gcn_b", out[:])
        turn = ExitStack()
        self.layer_norm(turn, out[:], out[:], g[:], b[:])
        self.to_features(self.psum(turn), out, ht)
        weights[2]()
        self.run_lanes(c)
        turn.close()
        inner.close()

        def finish(heads):
            last = ExitStack()
            y = self.sb("y1", [P, NT, D], F32, last)
            for lane, lo, hi in self.lanes:
                at, wide = slice(lo, hi), over_nodes(bias[:], hi - lo)
                lane.op("v", lambda e, at=at: e.tensor_tensor(y[:, at, :], heads[:, at, 0, :], heads[:, at, 1, :], ALU.add))
                lane.op("v", lambda e, at=at, wide=wide: e.scalar_tensor_tensor(y[:, at, :], y[:, at, :], 0.5, wide,
                                                                                ALU.mult, ALU.add))
            self.layer_norm(last, y[:], y[:], g[:], b[:])
            for lane, lo, hi in self.lanes:
                at = slice(lo, hi)
                lane.op("v", lambda e, at=at: e.tensor_tensor(self.x[:, at, :], self.x[:, at, :], y[:, at, :], ALU.add))
            self.run_lanes()
            last.close()
        self.attend(ht, weights, 2, D, finish)
        st.close()

    def gated_layer(self):
        nc, c = self.nc, self.c
        st = ExitStack()
        with c.together():
            l0, l1 = self.matrix("L2_gnn_l0_w", st), self.matrix("L2_gnn_l1_w", st)
            b0, b1 = self.columns("L2_gnn_l0_b", st), self.columns("L2_gnn_l1_b", st)
        state = self.sb("state", [P, 2, NP], F32, st)
        x1t = self.sb("x1t", [P, NP], F32, st)
        table, table_0 = self.dram("state_table", [NP, S2]), self.dram("state_table_0", [NP, D])
        loop = ExitStack()
        with c.together():
            wih, whh = self.matrix("L2_gnn_w_ih", loop), self.matrix("L2_gnn_w_hh", loop)
            bih, bhh = self.columns("L2_gnn_b_ih", loop), self.columns("L2_gnn_b_hh", loop)
        brz = self.sb("brz", [P, 6], F32, loop)
        ps = self.psum(loop)
        acc = self.sb("sums", [P, 2, NP], F32, loop)
        hidden = Hidden(self, ps, state, wih, whh, loop, x1t)
        gate_sems = [nc.alloc_semaphore("gates_" + n) for n in ("made", "act", "dve", "turned", "parked", "staged", "stored")]
        flat_x = self.x[:].rearrange("p t w -> p (t w)")
        away = self.dram("away", [2, P, NP])
        with c.together():
            c.op("v", lambda e: e.tensor_tensor(brz[:], bih[:], bhh[:], ALU.add))
            c.dma("s", away[0, :, :], flat_x)
            c.op("p", lambda e: e.memset(acc[:], 0.0))
            c.op("p", lambda e: e.memset(hidden.zero[:], 0.0))
        first = ExitStack()
        h = self.sb("h2", [P, NT, D], F32, first)
        self.layer_norm(first, self.x[:], h[:])
        self.to_features(ps, h, x1t)
        for lane, lo, hi in self.lanes:
            at, cols = slice(lo, hi), slice(lo * P, hi * P)
            with lane.together():
                lane.op("p", lambda e, cols=cols: e.memset(state[:, 1, cols], 0.0))
                lane.op("a", lambda e, cols=cols: e.copy(state[:, 0, cols], x1t[:, cols]))
                lane.dma("s", node_rows(table_0[cols, :]), h[:, at, :])
                lane.dma("s", away[1, :, cols], x1t[:, cols])
        self.run_lanes(c)
        first.close()
        sums_sems = self.edge_sems()

        def one_layer(layer, halves, rows):
            hidden.layer, hidden.halves, hidden.idle = layer, halves, gate_sems
            self.edge_sums(ps, rows, halves * P, acc[:, 0:halves, :], turned=True, sems=sums_sems, before=layer,
                           beside=hidden)
            self.gates(ps, acc, state, hidden, table, brz, bih, bhh, gate_sems, (*hidden.sems, *sums_sems[:6]))

        one_layer(0, 1, table_0)
        with nc.Fori(1, LAYERS) as layer:
            one_layer(layer, 2, table)
        with c.together():
            c.dma("s", flat_x, away[0, :, :])
            c.dma("a", x1t[:], away[1, :, :])
        c.run()
        loop.close()

        mlp = ExitStack()
        ps = self.psum(mlp)
        y1 = self.sb("y1", [P, 2, NP], F32, mlp)
        y2 = self.sb("y2", [P, NP], F32, mlp)

        made, taken = nc.alloc_semaphore("mlp_made"), nc.alloc_semaphore("mlp_taken")
        stages = [(l0, m, (state[:, 0, :], state[:, 1, :], x1t[:]), y1[:, m, :], b0[:, m:m + 1]) for m in range(2)]
        stages.append((l1, 0, (y1[:, 0, :], y1[:, 1, :]), y2[:], b1[:, 0:1]))
        with nc.Block() as block:
            @block.tensor
            def _(e):
                for n, (w, m, sources, out, bias) in enumerate(stages):
                    for q in range(NCH):
                        done = n * NCH + q
                        if n:
                            e.wait_ge(taken, done - NCH + 1)
                        for j, src in enumerate(sources):
                            mm = e.matmul(ps[:, q, 0:CH], w[:, j, m * P:(m + 1) * P], src[:, q * CH:(q + 1) * CH],
                                          start=j == 0, stop=j == len(sources) - 1)
                        mm.then_inc(made, 1)

            @block.scalar
            def _(e):
                for n, (w, m, sources, out, bias) in enumerate(stages):
                    for q in range(NCH):
                        e.wait_ge(made, n * NCH + q + 1)
                        e.activation(out[:, q * CH:(q + 1) * CH], ps[:, q, 0:CH], ACT.Relu, bias=bias).then_inc(taken, 1)
        flat = ps[:].rearrange("p b n -> p (b n)")

        def back(e):
            for t in range(NT):
                last = e.transpose(flat[:, t * P:(t + 1) * P], y2[:, t * P:(t + 1) * P], self.ident[:])
            return last
        c.op("t", back)
        self.add_to_x(flat[:, 0:NP].rearrange("p (t w) -> p t w", w=D))
        c.run()
        mlp.close()
        st.close()

    def gates(self, ps, sums, state, hidden, table, brz, bih, bhh, sems, idle):
        nc = self.nc
        st = ExitStack()
        rz = self.sb("rz", [P, 2, 2, GC], F32, st)
        n, d = (self.sb(w, [P, 2, GC], F32, st) for w in ("n", "d"))
        stage = self.sb("stage", [TQ, GC // TQ, S2], F32, st)
        zero = hidden.zero
        made, act, dve, turned, parked, staged, stored = sems
        V = 12
        A0, D1, E1, F1, B0, C0, A1, D0, E0, F0, B1, C1 = range(1, V + 1)
        with nc.Block() as block:
            @block.tensor
            def _(e):
                def products(i):
                    for f, taken in enumerate((C0, C1)):
                        e.wait_ge(dve, i * V + taken)
                        for gate in range(3):
                            at = slice(gate * S2 + f * P, gate * S2 + (f + 1) * P)
                            for j in range(hidden.halves):
                                mm = e.matmul(ps[:, 3 * f + gate, 0:GC], hidden.folded[:, j, at],
                                              sums[:, j, bass.ds(i * GC, GC)], start=j == 0,
                                              stop=j == hidden.halves - 1)
                        mm.then_inc(made, 1)

                def turn(i):
                    e.wait_ge(dve, i * V + 2 * V + F1)
                    e.wait_ge(staged, i + 1)
                    for f in range(2):
                        for q in range(GC // TQ):
                            mm = e.transpose(ps[0:TQ, 6 + f, q * P:(q + 1) * P], d[:, f, q * TQ:(q + 1) * TQ], self.ident[:])
                    mm.then_inc(turned, 1)

                e.sem_inc(dve, V)
                e.sem_inc(turned, 1)
                products(0)
                with e.Fori(1, NGC) as i:
                    products(i)
                    turn(i - 1)
                turn(NGC - 1)

            @block.scalar
            def _(e):
                def gate_pair(i, f, added):
                    e.wait_ge(dve, i * V + V + added)
                    e.activation(rz[:, f, 0, :], rz[:, f, 0, :], ACT.Sigmoid, bias=brz[:, f:f + 1])
                    e.activation(rz[:, f, 1, :], rz[:, f, 1, :], ACT.Sigmoid, bias=brz[:, 2 + f:3 + f]).then_inc(act, 1)

                def tanh(i, f, added):
                    e.wait_ge(dve, i * V + V + added)
                    e.activation(n[:, f, :], n[:, f, :], ACT.Tanh, bias=bih[:, 4 + f:5 + f]).then_inc(act, 1)

                def put(i):
                    e.wait_ge(turned, i + 2)
                    e.wait_ge(stored, i * 16 + 16)
                    e.copy(stage[:].rearrange("p q (f w) -> p f q w", f=2),
                           ps[0:TQ, 6:8, 0:GC // TQ * P].rearrange("p f (q w) -> p f q w", w=P)).then_inc(staged, 1)

                def chunk(i):
                    gate_pair(i, 0, A0)
                    tanh(i, 0, C0)
                    gate_pair(i, 1, A1)
                    tanh(i, 1, C1)

                e.sem_inc(staged, 1)
                chunk(0)
                with e.Fori(1, NGC) as i:
                    chunk(i)
                    put(i - 1)
                put(NGC - 1)

            @block.vector
            def _(e):
                def add(i, f):
                    e.wait_ge(made, i * 2 + f + 1)
                    e.wait_ge(dve, i * V + V)
                    e.tensor_tensor(rz[:, f, :, :], ps[:, 3 * f:3 * f + 2, 0:GC],
                                    hidden.rz[:, f, :, bass.ds(i * GC, GC)], ALU.add).then_inc(dve, 1)

                def reset(i, f, done, before):
                    e.wait_ge(act, i * 4 + 2 * f + 1)
                    e.scalar_tensor_tensor(n[:, f, :], hidden.n[f][:, bass.ds(i * GC, GC)], bhh[:, 4 + f:5 + f],
                                           rz[:, f, 0, :], ALU.add, ALU.mult).then_inc(dve, 1)
                    e.wait_ge(dve, done + before)
                    e.tensor_tensor(n[:, f, :], n[:, f, :], ps[:, 3 * f + 2, 0:GC], ALU.add).then_inc(dve, 1)

                def renew(i, f, done, before):
                    e.wait_ge(act, i * 4 + 2 * f + 2)
                    e.wait_ge(turned, i + 1)
                    e.wait_ge(parked, i * 2 + f + 1)
                    e.tensor_tensor(d[:, f, :], state[:, f, bass.ds(i * GC, GC)], n[:, f, :], ALU.subtract).then_inc(dve, 1)
                    e.wait_ge(dve, done + before)
                    e.tensor_tensor(d[:, f, :], d[:, f, :], rz[:, f, 1, :], ALU.mult).then_inc(dve, 1)
                    e.wait_ge(dve, done + before + 1)
                    e.tensor_tensor(d[:, f, :], d[:, f, :], n[:, f, :], ALU.add).then_inc(dve, 1)

                def turn(i, last):
                    done = i * V + V
                    add(i, 0)
                    last(done)
                    reset(i, 0, done, B0)
                    add(i, 1)
                    renew(i, 0, done, D0)
                    reset(i, 1, done, B1)

                def none(done):
                    e.wait_ge(dve, done + A0)
                    e.sem_inc(dve, 3)

                turn(0, none)
                with e.Fori(1, NGC) as i:
                    turn(i, lambda done: renew(i - 1, 1, done, D1))
                e.wait_ge(dve, NGC * V + V)
                e.sem_inc(dve, 1)
                renew(NGC - 1, 1, NGC * V + V, D1)

            @block.gpsimd
            def _(e):
                e.sem_inc(parked, 2)
                with e.Fori(0, NGC) as i:
                    cut = bass.ds(i * GC, GC)
                    e.wait_ge(made, i * 2 + 2)
                    e.tensor_copy(sums[:, :, cut], zero[:].unsqueeze(1).to_broadcast([P, 2, GC]))
                    for f, new in enumerate((F0, V + F1)):
                        e.wait_ge(dve, i * V + V + new)
                        e.tensor_copy(state[:, f, cut], d[:, f, :]).then_inc(parked, 1)

            @block.sync
            def _(e):
                for sem in idle:
                    e.sem_clear(sem)
                e.sem_inc(stored, 16)
                with e.Fori(0, NGC) as i:
                    e.wait_ge(staged, i + 2)
                    e.dma_start(table[bass.ds(i * GC, GC), :].rearrange("(q p) w -> p q w", p=TQ),
                                stage[:]).then_inc(stored, 16)
                e.wait_ge(stored, 16 * (NGC + 1))
        st.close()

    def gat_gat_layer(self):
        c = self.c
        st = ExitStack()
        with c.together():
            b1, b2 = self.row("L3_gnn_b1", st), self.row("L3_gnn_b2", st)
        g = self.sb("g3", [P, NT, 64], F32, st)
        ht = self.sb("ht3", [P, NP], F32, st)
        weights_1 = self.attention_weights(st, "L3_gnn_W1", "L3_gnn_att_src1", "L3_gnn_att_dst1", 8, 8)
        weights_2 = self.attention_weights(st, "L3_gnn_W2", "L3_gnn_att_src2", "L3_gnn_att_dst2", 1, D)
        inner = ExitStack()
        h = self.sb("h3", [P, NT, D], F32, inner)
        first = self.sb("first3", [P, NP], F32, inner)
        with c.together():
            wm, bm = self.matrix("L3_gnn_W_map", inner), self.columns("L3_gnn_b_map", inner)
        c.run()
        self.layer_norm(inner, self.x[:], h[:])
        ps = self.psum(inner)
        self.to_features(ps, h, first)

        flat = ps[:].rearrange("p b n -> p (b n)")
        for lane, lo, hi in self.lanes:
            def mapped(e, lo=lo, hi=hi):
                for a in range(lo * P, hi * P, 512):
                    b = min(a + 512, hi * P)
                    last = e.matmul(flat[:, a:b], wm[:], first[:, a:b], start=True, stop=True)
                return last
            lane.op("t", mapped)
            lane.op("a", lambda e, cols=slice(lo * P, hi * P): e.activation(ht[:, cols], flat[:, cols], ACT.Identity, bias=bm[:, 0:1]))
        weights_1[2]()
        weights_2[2]()
        self.run_lanes(c)
        inner.close()

        def elu(heads):
            last = ExitStack()
            low = self.sb("low", [P, NT, 64], F32, last)
            v = heads.rearrange("p t h c -> p t (h c)")
            for lane, lo, hi in self.lanes:
                at = slice(lo, hi)
                lane.op("v", lambda e, at=at: e.tensor_tensor(g[:, at, :], v[:, at, :], over_nodes(b1[:], at.stop - at.start), ALU.add))
                lane.op("v", lambda e, at=at: e.tensor_scalar(low[:, at, :], g[:, at, :], 0.0, None, ALU.min))
                with lane.together():
                    lane.op("a", lambda e, at=at: e.activation(low[:, at, :], low[:, at, :], ACT.Exp))
                    lane.op("v", lambda e, at=at: e.tensor_scalar(g[:, at, :], g[:, at, :], 0.0, -1.0, ALU.max, ALU.add))
                lane.op("v", lambda e, at=at: e.tensor_tensor(g[:, at, :], g[:, at, :], low[:, at, :], ALU.add))
            self.run_lanes()
            last.close()
        self.attend(ht, weights_1, 8, 8, elu)
        turn = ExitStack()
        self.to_features(self.psum(turn), g, ht, 64)
        self.run_lanes()
        turn.close()

        def finish(heads):
            v = heads.rearrange("p t h c -> p t (h c)")
            for lane, lo, hi in self.lanes:
                at = slice(lo, hi)
                lane.op("v", lambda e, at=at: e.tensor_tensor(v[:, at, :], v[:, at, :], over_nodes(b2[:], at.stop - at.start), ALU.add))
                lane.op("v", lambda e, at=at: e.tensor_tensor(self.x[:, at, :], self.x[:, at, :], v[:, at, :], ALU.add))
                rows = slice(lo * P, min(hi, NT - 1) * P)
                lane.dma("s", node_rows(self.out[rows, :]), self.x[:, lo:min(hi, NT - 1), :])
                if hi == NT:
                    lane.dma("s", self.out[(NT - 1) * P:N, :], self.x[0:LAST, NT - 1, :])
            self.run_lanes()
        self.attend(ht, weights_2, 1, D, finish)
        st.close()


def build(nc, ins, out):
    k = Kernel(nc, ins, out)
    with k.stack:
        k.constants()
        k.c.run()
        with ExitStack() as st:
            h, out = k.sb("h0", [P, NT, D], F32, st), k.sb("out0", [P, NT, D], F32, st)
            k.layer_norm(st, k.x[:], h[:])
            k.graph()
            k.degrees()
            k.gcn_layer(h, out)
        k.gcn_gat_layer()
        k.gated_layer()
        k.gat_gat_layer()


_TURNED = ("L2_gnn_W", "L2_gnn_w_ih", "L2_gnn_w_hh", "L2_gnn_l0_w", "L2_gnn_l1_w")


def kernel(**inputs):
    import concourse.bacc as _bacc
    from concourse.bass_utils import run_bass_kernel_spmd as _run

    nc = _bacc.Bacc("TRN2", target_bir_lowering=False, num_devices=1)
    arrays, ins = {}, {}
    for name, value in inputs.items():
        a = np.asarray(value)
        a = np.ascontiguousarray(a.swapaxes(-1, -2) if name in _TURNED else a)
        arrays[name] = a
        ins[name] = nc.dram_tensor(name, a.shape, mybir.dt.from_np(a.dtype), kind="ExternalInput").ap()
    out = nc.dram_tensor("out", (N, D), F32, kind="ExternalOutput").ap()
    build(nc, ins, out)
    r = _run(nc, [arrays], core_ids=[0])
    return r.results[0]["out"]
```
